# Optimizing a Trainium2 kernel written in Bass

```python
import numpy as np
import jax
import jax.numpy as jnp

def _softmax(x, axis=-1):
    return jax.nn.softmax(x, axis=axis)

def _gelu(x):
    return jax.nn.gelu(x, approximate=True)

def _silu(x):
    return jax.nn.silu(x)

def _sigmoid(x):
    return jax.nn.sigmoid(x)

def _layernorm(x, axis=-1, eps=1e-05):
    m = jnp.mean(x, axis=axis, keepdims=True)
    v = jnp.var(x, axis=axis, keepdims=True)
    return (x - m) / jnp.sqrt(v + eps)

def _scatter_add(tgt, idx, src, axis=0):
    return tgt.at[idx].add(src)

def _segment_sum(src, seg, n):
    return jax.ops.segment_sum(src, seg, n)
kernel_name = 'mk_gnn_resnorm_d4_gnn_r64_4f72e0'

def setup_inputs(seed: int=0):
    np.random.seed(seed)
    _w = jnp.asarray

    def _rec_inputs():
        import jax
        import jax.numpy as jnp
        _gk = jax.random.key(seed)
        x = -0.000202 + 1 * jax.random.normal(jax.random.fold_in(_gk, 1), (50000, 128), jnp.float32)
        src = jax.random.randint(jax.random.fold_in(_gk, 2), (25000,), 0, 50000, jnp.int32)
        dst = jax.random.randint(jax.random.fold_in(_gk, 3), (25000,), 0, 50000, jnp.int32)
        _o = jnp.argsort(dst, stable=True)
        src = src[_o]
        dst = dst[_o]
        edge_attr_128 = 4.59472e-05 + 1.00006 * jax.random.normal(jax.random.fold_in(_gk, 12), (25000, 128), jnp.float32)
        edge_attr_26 = 4.66435e-05 + 0.999962 * jax.random.normal(jax.random.fold_in(_gk, 13), (25000, 26), jnp.float32)
        return (x, src, dst, edge_attr_128, edge_attr_26)
    x, src, dst, edge_attr_128, edge_attr_26 = _rec_inputs()

    def _L0_gnn_setup():
        import jax, jax.numpy as jnp
        import numpy as np
        N_NODES = 50000
        N_EDGES = 10000
        D_IN = 128
        D_HID = 128

        def _sage_conv(x, src, dst, Wl, bl, Wr, n_nodes):
            agg = jax.ops.segment_sum(x[src], dst, num_segments=n_nodes)
            cnt = jax.ops.segment_sum(jnp.ones((src.shape[0],), x.dtype), dst, num_segments=n_nodes)
            mean = agg / jnp.maximum(cnt, 1.0)[:, None]
            return mean @ Wl.T + bl + x @ Wr.T
        key = jax.random.key(seed)
        ks = jax.random.split(key, 8)
        x = jax.random.normal(ks[0], (N_NODES, D_IN), dtype=jnp.float32)
        edge_index = jax.random.randint(ks[1], (2, N_EDGES), 0, N_NODES, dtype=jnp.int64)
        s = 1.0 / np.sqrt(D_IN)
        W1l = jax.random.uniform(ks[2], (D_HID, D_IN), jnp.float32, -s, s)
        b1l = jnp.zeros((D_HID,), jnp.float32)
        W1r = jax.random.uniform(ks[3], (D_HID, D_IN), jnp.float32, -s, s)
        s2 = 1.0 / np.sqrt(D_HID)
        W2l = jax.random.uniform(ks[4], (D_HID, D_HID), jnp.float32, -s2, s2)
        b2l = jnp.zeros((D_HID,), jnp.float32)
        W2r = jax.random.uniform(ks[5], (D_HID, D_HID), jnp.float32, -s2, s2)
        return {'x': x, 'edge_index': edge_index, 'W1l': W1l, 'b1l': b1l, 'W1r': W1r, 'W2l': W2l, 'b2l': b2l, 'W2r': W2r}
    _L0_gnn_all = _L0_gnn_setup()
    _L0_gnn_in = {k: v for k, v in _L0_gnn_all.items() if k in ('W1l', 'b1l', 'W1r', 'W2l', 'b2l', 'W2r')}
    del _L0_gnn_all

    def _L1_gnn_setup():
        import jax, jax.numpy as jnp
        import numpy as np
        N = 50000
        E = 9375
        IN_CH = 128
        HEADS = 8
        HEAD_DIM = 16
        OUT_CH = 128
        NEG_SLOPE = 0.2
        LN_EPS = 1e-05
        key = jax.random.key(seed)
        ks = jax.random.split(key, 9)
        x = jax.random.normal(ks[0], (N, IN_CH), dtype=jnp.float32)
        edge_index = jax.random.randint(ks[1], (2, E), 0, N, dtype=jnp.int64)
        lin_w = jax.random.normal(ks[2], (HEADS * HEAD_DIM, IN_CH), dtype=jnp.float32) * 0.05
        att_src = jax.random.normal(ks[3], (1, HEADS, HEAD_DIM), dtype=jnp.float32) * 0.1
        att_dst = jax.random.normal(ks[4], (1, HEADS, HEAD_DIM), dtype=jnp.float32) * 0.1
        gat_bias = jnp.zeros((HEADS * HEAD_DIM,), dtype=jnp.float32)
        proj_w = jax.random.normal(ks[5], (OUT_CH, HEADS * HEAD_DIM), dtype=jnp.float32) * 0.05
        proj_b = jnp.zeros((OUT_CH,), dtype=jnp.float32)
        ln_gamma = jnp.ones((OUT_CH,), dtype=jnp.float32)
        ln_beta = jnp.zeros((OUT_CH,), dtype=jnp.float32)
        return {'x': x, 'edge_index': edge_index, 'lin_w': lin_w, 'att_src': att_src, 'att_dst': att_dst, 'gat_bias': gat_bias, 'proj_w': proj_w, 'proj_b': proj_b, 'ln_gamma': ln_gamma, 'ln_beta': ln_beta}
    _L1_gnn_all = _L1_gnn_setup()
    _L1_gnn_in = {k: v for k, v in _L1_gnn_all.items() if k in ('lin_w', 'att_src', 'att_dst', 'gat_bias', 'proj_w', 'proj_b', 'ln_gamma', 'ln_beta')}
    del _L1_gnn_all

    def _L2_gnn_setup():
        import jax, jax.numpy as jnp
        import numpy as np
        N_NODE = 50000
        N_EDGE = 625000
        FDIM = 128
        HID = 128
        EPS = 1e-05
        key = jax.random.key(seed)
        ks = jax.random.split(key, 12)
        node_feature = jax.random.normal(ks[0], (N_NODE, FDIM), dtype=jnp.float32)
        edge_matrix = jax.random.randint(ks[1], (2, N_EDGE), 0, N_NODE, dtype=jnp.int32)
        edge_feature = jax.random.normal(ks[2], (N_EDGE, FDIM), dtype=jnp.float32)
        in_dim = FDIM + FDIM
        s1 = 1.0 / np.sqrt(in_dim)
        s2 = 1.0 / np.sqrt(HID)
        W1 = jax.random.uniform(ks[3], (in_dim, HID), jnp.float32, -s1, s1)
        b1 = jax.random.uniform(ks[4], (HID,), jnp.float32, -s1, s1)
        W2 = jax.random.uniform(ks[5], (HID, HID), jnp.float32, -s2, s2)
        b2 = jax.random.uniform(ks[6], (HID,), jnp.float32, -s2, s2)
        W3 = jax.random.uniform(ks[7], (HID, FDIM), jnp.float32, -s2, s2)
        b3 = jax.random.uniform(ks[8], (FDIM,), jnp.float32, -s2, s2)
        gamma = jnp.ones((FDIM,), jnp.float32)
        beta = jnp.zeros((FDIM,), jnp.float32)
        return {'node_feature': node_feature, 'edge_matrix': edge_matrix, 'edge_feature': edge_feature, 'W1': W1, 'b1': b1, 'W2': W2, 'b2': b2, 'W3': W3, 'b3': b3, 'gamma': gamma, 'beta': beta}
    _L2_gnn_all = _L2_gnn_setup()
    _L2_gnn_in = {k: v for k, v in _L2_gnn_all.items() if k in ('W1', 'b1', 'W2', 'b2', 'W3', 'b3', 'gamma', 'beta')}
    del _L2_gnn_all

    def _L3_gnn_setup():
        import jax, jax.numpy as jnp
        import numpy as np
        N, E, H, EH, R, MH = (50000, 12500, 128, 26, 2, 256)
        IN = 2 * H + EH
        OUT = 2 * H
        key = jax.random.key(seed)
        ks = jax.random.split(key, 10)

        def w(k, shape, fan_in):
            return jax.random.normal(k, shape, jnp.float32) / np.float32(np.sqrt(fan_in))
        return {'hv': jax.random.normal(ks[0], (N, H), jnp.float32), 'he': jax.random.normal(ks[1], (E, EH), jnp.float32), 'src': jax.random.randint(ks[2], (E,), 0, N, jnp.int32), 'dst': jax.random.randint(ks[3], (E,), 0, N, jnp.int32), 'mlp_w1': w(ks[4], (R, IN, MH), IN), 'mlp_b1': jnp.zeros((R, MH), jnp.float32), 'mlp_w2': w(ks[5], (R, MH, OUT), MH), 'mlp_b2': jnp.zeros((R, OUT), jnp.float32), 'gru_wih': w(ks[6], (R, 3 * H, OUT), OUT), 'gru_whh': w(ks[7], (R, 3 * H, H), H), 'gru_bih': jnp.zeros((R, 3 * H), jnp.float32), 'gru_bhh': jnp.zeros((R, 3 * H), jnp.float32)}
    _L3_gnn_all = _L3_gnn_setup()
    _L3_gnn_in = {k: v for k, v in _L3_gnn_all.items() if k in ('mlp_w1', 'mlp_b1', 'mlp_w2', 'mlp_b2', 'gru_wih', 'gru_whh', 'gru_bih', 'gru_bhh')}
    del _L3_gnn_all
    return {'x': x, 'src': src, 'dst': dst, 'edge_attr_128': edge_attr_128, 'edge_attr_26': edge_attr_26, 'L0_gnn_W1l': _L0_gnn_in['W1l'], 'L0_gnn_b1l': _L0_gnn_in['b1l'], 'L0_gnn_W1r': _L0_gnn_in['W1r'], 'L0_gnn_W2l': _L0_gnn_in['W2l'], 'L0_gnn_b2l': _L0_gnn_in['b2l'], 'L0_gnn_W2r': _L0_gnn_in['W2r'], 'L1_gnn_lin_w': _L1_gnn_in['lin_w'], 'L1_gnn_att_src': _L1_gnn_in['att_src'], 'L1_gnn_att_dst': _L1_gnn_in['att_dst'], 'L1_gnn_gat_bias': _L1_gnn_in['gat_bias'], 'L1_gnn_proj_w': _L1_gnn_in['proj_w'], 'L1_gnn_proj_b': _L1_gnn_in['proj_b'], 'L1_gnn_ln_gamma': _L1_gnn_in['ln_gamma'], 'L1_gnn_ln_beta': _L1_gnn_in['ln_beta'], 'L2_gnn_W1': _L2_gnn_in['W1'], 'L2_gnn_b1': _L2_gnn_in['b1'], 'L2_gnn_W2': _L2_gnn_in['W2'], 'L2_gnn_b2': _L2_gnn_in['b2'], 'L2_gnn_W3': _L2_gnn_in['W3'], 'L2_gnn_b3': _L2_gnn_in['b3'], 'L2_gnn_gamma': _L2_gnn_in['gamma'], 'L2_gnn_beta': _L2_gnn_in['beta'], 'L3_gnn_mlp_w1': _L3_gnn_in['mlp_w1'], 'L3_gnn_mlp_b1': _L3_gnn_in['mlp_b1'], 'L3_gnn_mlp_w2': _L3_gnn_in['mlp_w2'], 'L3_gnn_mlp_b2': _L3_gnn_in['mlp_b2'], 'L3_gnn_gru_wih': _L3_gnn_in['gru_wih'], 'L3_gnn_gru_whh': _L3_gnn_in['gru_whh'], 'L3_gnn_gru_bih': _L3_gnn_in['gru_bih'], 'L3_gnn_gru_bhh': _L3_gnn_in['gru_bhh']}

def reference(x, src, dst, edge_attr_128, edge_attr_26, L0_gnn_W1l, L0_gnn_b1l, L0_gnn_W1r, L0_gnn_W2l, L0_gnn_b2l, L0_gnn_W2r, L1_gnn_lin_w, L1_gnn_att_src, L1_gnn_att_dst, L1_gnn_gat_bias, L1_gnn_proj_w, L1_gnn_proj_b, L1_gnn_ln_gamma, L1_gnn_ln_beta, L2_gnn_W1, L2_gnn_b1, L2_gnn_W2, L2_gnn_b2, L2_gnn_W3, L2_gnn_b3, L2_gnn_gamma, L2_gnn_beta, L3_gnn_mlp_w1, L3_gnn_mlp_b1, L3_gnn_mlp_w2, L3_gnn_mlp_b2, L3_gnn_gru_wih, L3_gnn_gru_whh, L3_gnn_gru_bih, L3_gnn_gru_bhh):
    import jax
    import jax.numpy as jnp

    def _L0_gnn_ref(x, edge_index, W1l, b1l, W1r, W2l, b2l, W2r):
        import jax, jax.numpy as jnp
        import numpy as np
        N_NODES = 50000
        N_EDGES = 10000
        D_IN = 128
        D_HID = 128

        def _sage_conv(x, src, dst, Wl, bl, Wr, n_nodes):
            agg = jax.ops.segment_sum(x[src], dst, num_segments=n_nodes)
            cnt = jax.ops.segment_sum(jnp.ones((src.shape[0],), x.dtype), dst, num_segments=n_nodes)
            mean = agg / jnp.maximum(cnt, 1.0)[:, None]
            return mean @ Wl.T + bl + x @ Wr.T
        src, dst = (edge_index[0], edge_index[1])
        h = _sage_conv(x, src, dst, W1l, b1l, W1r, N_NODES)
        h = jax.nn.relu(h)
        return _sage_conv(h, src, dst, W2l, b2l, W2r, N_NODES)

    def _L1_gnn_ref(x, edge_index, lin_w, att_src, att_dst, gat_bias, proj_w, proj_b, ln_gamma, ln_beta):
        import jax, jax.numpy as jnp
        import numpy as np
        N = 50000
        E = 9375
        IN_CH = 128
        HEADS = 8
        HEAD_DIM = 16
        OUT_CH = 128
        NEG_SLOPE = 0.2
        LN_EPS = 1e-05
        n = x.shape[0]
        h = (x @ lin_w.T).reshape(n, HEADS, HEAD_DIM)
        a_src = (h * att_src).sum(-1)
        a_dst = (h * att_dst).sum(-1)
        loops = jnp.arange(n, dtype=edge_index.dtype)
        src = jnp.concatenate([edge_index[0], loops])
        dst = jnp.concatenate([edge_index[1], loops])
        logits = jax.nn.leaky_relu(a_src[src] + a_dst[dst], NEG_SLOPE)
        seg_max = jax.ops.segment_max(logits, dst, num_segments=n)
        e = jnp.exp(logits - seg_max[dst])
        denom = jax.ops.segment_sum(e, dst, num_segments=n)
        alpha = e / denom[dst]
        agg = jax.ops.segment_sum(h[src] * alpha[:, :, None], dst, num_segments=n)
        gat_out = agg.reshape(n, HEADS * HEAD_DIM) + gat_bias
        out = gat_out @ proj_w.T + proj_b
        mu = out.mean(-1, keepdims=True)
        var = ((out - mu) ** 2).mean(-1, keepdims=True)
        out = (out - mu) * jax.lax.rsqrt(var + LN_EPS) * ln_gamma + ln_beta
        return out

    def _L2_gnn_ref(node_feature, edge_matrix, edge_feature, W1, b1, W2, b2, W3, b3, gamma, beta):
        import jax, jax.numpy as jnp
        import numpy as np
        N_NODE = 50000
        N_EDGE = 625000
        FDIM = 128
        HID = 128
        EPS = 1e-05
        receiver_idx = edge_matrix[1]
        agg = jax.ops.segment_sum(edge_feature, receiver_idx, num_segments=node_feature.shape[0])
        x = jnp.concatenate([node_feature, agg], axis=-1)
        h = jax.nn.relu(x @ W1 + b1)
        h = jax.nn.relu(h @ W2 + b2)
        h = h @ W3 + b3
        mu = jnp.mean(h, axis=-1, keepdims=True)
        var = jnp.mean((h - mu) ** 2, axis=-1, keepdims=True)
        h = (h - mu) * jax.lax.rsqrt(var + EPS) * gamma + beta
        return h + node_feature

    def _L3_gnn_ref(hv, he, src, dst, mlp_w1, mlp_b1, mlp_w2, mlp_b2, gru_wih, gru_whh, gru_bih, gru_bhh):
        import jax, jax.numpy as jnp
        import numpy as np
        N, E, H, EH, R, MH = (50000, 12500, 128, 26, 2, 256)
        IN = 2 * H + EH
        OUT = 2 * H
        n_nodes, h = hv.shape
        num_rounds = mlp_w1.shape[0]
        for t in range(num_rounds):
            x = jnp.concatenate([hv[dst], hv[src], he], axis=1)
            h1 = jax.nn.relu(x @ mlp_w1[t] + mlp_b1[t])
            m = h1 @ mlp_w2[t] + mlp_b2[t]
            a = jax.ops.segment_sum(m, dst, num_segments=n_nodes)
            gx = a @ gru_wih[t].T + gru_bih[t]
            gh = hv @ gru_whh[t].T + gru_bhh[t]
            r = jax.nn.sigmoid(gx[:, :h] + gh[:, :h])
            z = jax.nn.sigmoid(gx[:, h:2 * h] + gh[:, h:2 * h])
            n = jnp.tanh(gx[:, 2 * h:] + r * gh[:, 2 * h:])
            hv = (1.0 - z) * n + z * hv
        return hv
    edge_index = jnp.stack([src, dst])
    x = _layernorm(x + _L0_gnn_ref(x, edge_index, L0_gnn_W1l, L0_gnn_b1l, L0_gnn_W1r, L0_gnn_W2l, L0_gnn_b2l, L0_gnn_W2r), axis=-1)
    x = _layernorm(x + _L1_gnn_ref(x, edge_index, L1_gnn_lin_w, L1_gnn_att_src, L1_gnn_att_dst, L1_gnn_gat_bias, L1_gnn_proj_w, L1_gnn_proj_b, L1_gnn_ln_gamma, L1_gnn_ln_beta), axis=-1)
    x = _layernorm(x + _L2_gnn_ref(x, edge_index, edge_attr_128, L2_gnn_W1, L2_gnn_b1, L2_gnn_W2, L2_gnn_b2, L2_gnn_W3, L2_gnn_b3, L2_gnn_gamma, L2_gnn_beta), axis=-1)
    x = _layernorm(x + _L3_gnn_ref(x, edge_attr_26, src, dst, L3_gnn_mlp_w1, L3_gnn_mlp_b1, L3_gnn_mlp_w2, L3_gnn_mlp_b2, L3_gnn_gru_wih, L3_gnn_gru_whh, L3_gnn_gru_bih, L3_gnn_gru_bhh), axis=-1)
    return x

_drawn_inputs = setup_inputs


def setup_inputs(seed=0):
    import zlib

    import numpy as np

    out = dict(_drawn_inputs(seed))
    spreads = {'L0_gnn_b1l': (0.0, 0.1),
     'L0_gnn_b2l': (0.0, 0.1),
     'L1_gnn_gat_bias': (0.0, 0.1),
     'L1_gnn_proj_b': (0.0, 0.1),
     'L1_gnn_ln_gamma': (1.0, 0.2),
     'L1_gnn_ln_beta': (0.0, 0.1),
     'L2_gnn_gamma': (1.0, 0.2),
     'L2_gnn_beta': (0.0, 0.1),
     'L3_gnn_mlp_b1': (0.0, 0.327),
     'L3_gnn_mlp_b2': (0.0, 0.1),
     'L3_gnn_gru_bih': (0.0, 0.1),
     'L3_gnn_gru_bhh': (0.0, 0.274)}
    factors = {'L1_gnn_att_dst': 3.856}
    for name, (base, spread) in spreads.items():
        noise = np.random.default_rng([zlib.crc32(name.encode()), seed]).standard_normal(out[name].shape)
        drawn = base * np.exp(spread * noise) if base else spread * noise
        out[name] = jnp.asarray(drawn.astype(out[name].dtype))
    for name, factor in factors.items():
        out[name] = (out[name] * factor).astype(out[name].dtype)
    return out
```

```python
from contextlib import ExitStack

import concourse.bass as bass
from concourse import mybir
from concourse.bass import ds

F32 = mybir.dt.float32
I32 = mybir.dt.int32
ALU = mybir.AluOpType
ACT = mybir.ActivationFunctionType

P = 128
EDGES_PER_TILE = P - 1
LAST_SLOT = 32
QUAD = 4
GROUP = QUAD * P
HEADS, HEAD_DIM = 8, 16
CHUNKS = 8
EPS = 1e-5
SLOPE = 0.2
SKIP = 1.0e6
LOW = -1.0e30
AUG = 144


class Step:

    def __init__(self, i, b, of):
        self.i, self.b, self.of = i, b, of

    def at(self, k):
        i, b = self.i + (self.b + k) // 2, (self.b + k) % 2
        if isinstance(i, int) and not 0 <= 2 * i + b < self.of:
            return None
        return Step(i, b, self.of)

    @property
    def n(self):
        return 2 * self.i + self.b


def run_steps(eng, of, before, after, body):
    lo = (after + 1) // 2 + 1
    hi = (of - before) // 2
    for n in range(-before, 2 * lo):
        body(Step(n // 2, n % 2, of))
    with eng.Fori(lo, hi) as i:
        body(Step(i, 0, of))
        body(Step(i, 1, of))
    for n in range(2 * hi, of + after):
        body(Step(n // 2, n % 2, of))


class Phase:

    def __init__(self, nc, name):
        self.nc, self.name, self.stack, self.held = nc, name, ExitStack(), []

    def __enter__(self):
        return self

    def __exit__(self, *e):
        self.stack.__exit__(*e)
        self.nc.clear_and_free_semaphores(self.held)
        self.nc.all_engine_barrier()

    def sb(self, name, shape, dt=F32):
        return self.stack.enter_context(self.nc.sbuf_tensor(f"{self.name}_{name}", list(shape), dt))

    def ps(self, name, shape=(P, 512)):
        return self.stack.enter_context(self.nc.psum_tensor(f"{self.name}_{name}", list(shape), F32))

    def sem(self, name):
        self.held.append(self.nc.alloc_semaphore(f"{self.name}_{name}"))
        return self.held[-1]

    def sems(self, name, n=2):
        return [self.sem(f"{name}{k}") for k in range(n)]

    def block(self):
        return self.stack.enter_context(self.nc.Block())


def group_rows(table, n, width=P, at=0):
    rows = table[ds(n * GROUP, GROUP), :].rearrange("(p j) d -> p j d", j=QUAD)
    return rows if width is None else rows[:, :, at:at + width]


def hold(eng, turn, sem, value):
    eng.wait_ge(sem, value)
    eng.sem_inc(turn, 1)


def prepare(nc, g, d):
    with Phase(nc, "prep") as ph:
        loaded = ph.sem("loaded")
        zeros = ph.sb("zeros", [P, 4096])
        zeroed = ph.sem("zeroed")
        cleared = ph.sem("cleared")
        dstw, nxtw = ph.sb("dstw", [P, g.ntp], I32), ph.sb("nxtw", [P, g.ntp], I32)
        skip = ph.sb("skip", [P, g.ntp])
        target = ph.sb("target", [P, g.ntp])
        att = ph.sb("att", [P, 2])
        head_of = ph.sb("head_of", [P, HEADS])
        att_mat = ph.sb("att_mat", [P, 2 * HEADS])
        lin = ph.sb("lin", [P, P])
        psum = ph.ps("psum")
        index_step = ph.sem("index_step")
        att_done, prod_done = ph.sem("att_done"), ph.sem("prod_done")
        biases = ph.sb("biases", [P, g.rounds, 6])
        block = ph.block()

        loads = [(dstw[:, :], d["dstw"]), (nxtw[:, :], d["nxtw"]), (g.srcw[:, :], d["srcw"]),
                 (att[:, 0:1], d["att_src"]), (att[:, 1:2], d["att_dst"]),
                 (head_of[:, :], d["head_of"]), (lin[:, :], d["lin_w"]), (g.ident[:, :], d["ident"])]
        for name in ("W1lT", "W1rT", "W2lT", "W2rT", "projT", "W2", "W3"):
            loads.append((g.w[name][:, :], d[name]))
        loads.append((g.w["linT"][:, :], d["linT"]))
        loads.append((g.w["W1"][:, :, :], d["W1"].rearrange("(c p) n -> p c n", p=P)))
        for r in range(g.rounds):
            loads.append((g.w["mw1"][:, r, :, :], d["mlp_w1"][r, 0:2 * P, :].rearrange("(c p) n -> p c n", p=P)))
            loads.append((g.w["mw1e"][:, r, :], d["mlp_w1"][r, 2 * P:, :]))
            loads.append((g.w["mw2"][:, r, :, :], d["mlp_w2"][r].rearrange("(c p) n -> p c n", p=P)))
            loads.append((g.w["wih"][:, r, :, :], d["wihT"][r].rearrange("(c p) n -> p c n", p=P)))
            loads.append((g.w["whh"][:, r, :], d["whhT"][r]))
            loads.append((g.w["mb2"][:, r, :], d["mlp_b2"][r:r + 1, :].broadcast_to([P, 2 * P])))
        for name in g.rows:
            for j in range(QUAD):
                loads.append((g.row[name][:, j * P:(j + 1) * P], d[name].broadcast_to([P, P])))
        loads.append((g.col[:, 0:g.ncols], d["cols"]))

        @block.sync
        def _(sp):
            for dst, src in loads:
                sp.dma_start(dst, src).then_inc(loaded, 16)
            sp.wait_ge(zeroed, 1)
            n = 0
            for table in (g.seg, g.gat):
                flat = table.rearrange("(a p) d -> a p d", p=P)
                rows = 4096 // table.shape[1]
                whole = table.shape[0] // P
                for a in range(0, whole, rows):
                    k = min(rows, whole - a)
                    sp.dma_start(flat[a:a + k, :, :].rearrange("a p d -> p a d"),
                                 zeros[:, 0:k * table.shape[1]].rearrange("p (a d) -> p a d", a=k)
                                 ).then_inc(cleared, 16)
                    n += 1
            sp.wait_ge(cleared, 16 * n)
            sp.wait_ge(loaded, 16 * len(loads))

        @block.vector
        def _(dve):
            dve.memset(zeros[:, :], 0.0).then_inc(zeroed, 1)
            dve.wait_ge(loaded, 16 * len(loads))
            dve.tensor_copy(g.dcol[:, :], dstw[:, :]).then_inc(index_step, 1)
            dve.tensor_tensor(skip[:, :], dstw[:, :], nxtw[:, :], ALU.is_equal).then_inc(index_step, 1)
            dve.wait_ge(index_step, 2)
            dve.scalar_tensor_tensor(target[:, :], skip[:, :], SKIP, g.dcol[:, :], ALU.mult, ALU.add).then_inc(index_step, 1)
            dve.wait_ge(index_step, 3)
            dve.tensor_copy(g.at_node[:, :], target[:, :])
            dve.tensor_scalar(g.at_left[:, :], target[:, :], 2.0, None, ALU.mult)
            dve.tensor_scalar(g.at_right[:, :], target[:, :], 2.0, 1.0, ALU.mult, ALU.add)
            dve.tensor_scalar(g.dstw[:, :], g.dcol[:, :], 0.0, None, ALU.max)
            dve.tensor_scalar(att_mat[:, 0:HEADS], head_of[:, :], att[:, 0:1], None, ALU.mult)
            dve.tensor_scalar(att_mat[:, HEADS:], head_of[:, :], att[:, 1:2], None, ALU.mult).then_inc(att_done, 1)
            for r in range(g.rounds):
                c = g.gate_cols[r]
                dve.tensor_tensor(g.gate_bias[:, r, 0:2], g.col[:, c:c + 2], g.col[:, c + 3:c + 5], ALU.add)
                dve.tensor_copy(g.gate_bias[:, r, 2:3], g.col[:, c + 2:c + 3])
                dve.tensor_copy(g.gate_bias[:, r, 3:4], g.col[:, c + 5:c + 6])
            dve.wait_ge(prod_done, 1)
            dve.tensor_copy(g.w["attT"][:, :], psum[:, 0:2 * HEADS])

        @block.tensor
        def _(pe):
            pe.wait_ge(att_done, 1)
            pe.matmul(psum[:, 0:2 * HEADS], lin[:, :], att_mat[:, :], start=True, stop=True).then_inc(prod_done, 1)


def edge_sums(nc, g, name, target_index, target, width, gather=None, linear=None, mean=False, weights=None):
    cols = width + (1 if mean else 0) + (HEADS if weights else 0)
    out_cols = AUG if weights else width
    bound = g.nodes * (target.shape[0] // g.x.shape[0])
    with Phase(nc, name) as ph:
        src_ix, tgt_ix = ph.sb("src_ix", [P, 2, QUAD], I32), ph.sb("tgt_ix", [P, 2, QUAD], I32)
        drow = ph.sb("drow", [P, 2, QUAD, P], I32)
        msg = ph.sb("msg", [P, 2, QUAD, cols])
        raw = ph.sb("raw", [P, 2, QUAD, P]) if weights else msg
        same = ph.sb("same", [P, 2, QUAD, P])
        res = ph.sb("res", [P, 2, QUAD, out_cols])
        share = ph.sb("share", [P, 2, QUAD])
        count = ph.sb("count", [P, 2, QUAD])
        plain = ph.sb("plain", [P, 2, QUAD, cols if mean else 1])
        banks = ph.ps("sums", [P, QUAD, 2, 256])
        sums = [banks[:, :, b, :] for b in range(2)]
        src_here, tgt_here, drow_here = ph.sems("src_here"), ph.sems("tgt_here"), ph.sems("drow_here")
        rows_here = [ph.sems(f"rows_here{b}_", QUAD) for b in range(2)]
        scattered = [ph.sems(f"scattered{b}_", QUAD) for b in range(2)]
        same_done, msg_done, carried = ph.sems("same_done"), ph.sems("msg_done"), ph.sems("carried")
        summed, share_done, res_done = ph.sems("summed"), ph.sems("share_done"), ph.sems("res_done")
        read_out, maxima_done = ph.sems("read_out"), ph.sems("maxima_done")
        start = ph.sem("start")
        pool_turn, sp_turn = ph.sem("pool_turn"), ph.sem("sp_turn")
        block = ph.block()
        of = g.quads

        def load_quad(sp, s, which):
            if which == "src" and gather is not None:
                sp.dma_start(src_ix[:, s.b, :], g.srcw[:, ds(s.n * QUAD, QUAD)]).then_inc(src_here[s.b], 16)
            if which == "tgt":
                sp.dma_start(tgt_ix[:, s.b, :], target_index[:, ds(s.n * QUAD, QUAD)]).then_inc(tgt_here[s.b], 16)
            if which == "drow":
                sp.dma_start(drow[:, s.b, :, :].rearrange("p t e -> p (t e)"),
                             g.drow[:, ds(s.n * GROUP, GROUP)].broadcast_to([P, GROUP])).then_inc(drow_here[s.b], 16)
            if which == "rows" and linear is not None:
                for u in range(QUAD):
                    sp.dma_start(msg[:, s.b, u, 0:width], linear[ds((s.n * QUAD + u) * P, P), :]).then_inc(rows_here[s.b][u], 16)

        @block.sync
        def _(sp):
            for n in range(2):
                for which in ("src", "drow", "tgt", "rows"):
                    load_quad(sp, Step(0, n, of), which)

            def body(s):
                nxt = Step(s.i + 1, s.b, of)
                if gather is not None:
                    for u in range(QUAD):
                        hold(sp, sp_turn, rows_here[s.b][u], 16 * s.i + 16)
                load_quad(sp, nxt, "src")
                hold(sp, sp_turn, same_done[s.b], QUAD * s.i + QUAD)
                load_quad(sp, nxt, "drow")
                if linear is not None:
                    hold(sp, sp_turn, summed[s.b], QUAD * s.i + QUAD)
                    load_quad(sp, nxt, "rows")
                for u in range(QUAD):
                    hold(sp, sp_turn, scattered[s.b][u], 16 * s.i + 16)
                load_quad(sp, nxt, "tgt")
            run_steps(sp, of, 0, 0, body)
            for b in range(2):
                last = 16 * (of // 2 + 1)
                sp.wait_ge(tgt_here[b], last)
                sp.wait_ge(drow_here[b], last)
                if gather is not None:
                    sp.wait_ge(src_here[b], last)
                if linear is not None:
                    for u in range(QUAD):
                        sp.wait_ge(rows_here[b][u], last)

        @block.gpsimd
        def _(pool):
            def fetch(s):
                hold(pool, pool_turn, src_here[s.b], 16 * s.i + 16)

            def fetch_tile(s, u):
                pool.indirect_dma_start(out=raw[:, s.b, u, 0:P], out_offset=None, in_=gather,
                                        in_offset=bass.IndirectOffsetOnAxis(ap=src_ix[:, s.b, u:u + 1], axis=0)
                                        ).then_inc(rows_here[s.b][u], 16)

            if gather is not None:
                fetch(Step(0, 0, of))
                for u in range(QUAD):
                    fetch_tile(Step(0, 0, of), u)

            def body(s):
                nxt = Step(s.i + (s.b + 1) // 2, (s.b + 1) % 2, of)
                hold(pool, pool_turn, tgt_here[s.b], 16 * s.i + 16)
                if gather is not None:
                    fetch(nxt)
                for u in range(QUAD):
                    if gather is not None:
                        if u == 0:
                            hold(pool, pool_turn, summed[nxt.b], QUAD * nxt.i)
                        fetch_tile(nxt, u)
                    hold(pool, pool_turn, (res_done if mean else read_out)[s.b], QUAD * s.i + u + 1)
                    if weights:
                        hold(pool, pool_turn, maxima_done[s.b], QUAD * s.i + u + 1)
                    pool.indirect_dma_start(out=target, out_offset=bass.IndirectOffsetOnAxis(ap=tgt_ix[:, s.b, u:u + 1], axis=0),
                                            in_=res[:, s.b, u, :], in_offset=None,
                                            bounds_check=bound - 1, oob_is_err=False).then_inc(scattered[s.b][u], 16)
            run_steps(pool, of, 0, 0, body)
            for b in range(2):
                for u in range(QUAD):
                    pool.wait_ge(scattered[b][u], 16 * (of // 2))
            if gather is not None:
                for u in range(QUAD):
                    pool.wait_ge(rows_here[0][u], 16 * (of // 2 + 1))

        @block.scalar
        def _(act):
            act.wait_ge(start, 1)

            def read(s, u):
                act.wait_ge(summed[s.b], QUAD * s.i + u + 1)
                if mean:
                    act.wait_ge(res_done[s.b], QUAD * s.i)
                    act.copy(plain[:, s.b, u, :], sums[s.b][:, u, 0:cols]).then_inc(read_out[s.b], 1)
                else:
                    act.wait_ge(scattered[s.b][u], 16 * s.i)
                    act.copy(res[:, s.b, u, 0:cols], sums[s.b][:, u, 0:cols]).then_inc(read_out[s.b], 1)

            def body(s):
                before, here = s.at(-1), s.at(0)
                for u in range(QUAD):
                    if here:
                        if weights:
                            act.wait_ge(msg_done[s.b], QUAD * s.i + u + 1)
                        else:
                            act.wait_ge(rows_here[s.b][u], 16 * s.i + 16)
                        if u:
                            act.wait_ge(summed[s.b], QUAD * s.i + u)
                        elif before:
                            act.wait_ge(summed[before.b], QUAD * before.i + QUAD)
                        pb, pu = (s.b, u - 1) if u else (1 - s.b, QUAD - 1)
                        act.copy(msg[0:1, s.b, u, :], sums[pb][LAST_SLOT:LAST_SLOT + 1, pu, 0:cols]).then_inc(carried[s.b], 1)
                    if u and here:
                        read(s, u - 1)
                    elif u == 0 and before:
                        read(before, QUAD - 1)
            run_steps(act, of, 0, 1, body)

        @block.vector
        def _(dve):
            if mean:
                dve.memset(msg[:, :, :, width:width + 1], 1.0)
            dve.memset(banks[:, QUAD - 1, :, :], 0.0).then_inc(start, 1)

            def compare(s):
                dve.wait_ge(drow_here[s.b], 16 * s.i + 16)
                dve.wait_ge(summed[s.b], QUAD * s.i)
                for u in range(QUAD):
                    dve.tensor_scalar(same[:, s.b, u, :], drow[:, s.b, u, :], g.dcol[:, ds(s.n * QUAD + u, 1)], None,
                                      ALU.is_equal).then_inc(same_done[s.b], 1)

            def weigh(s):
                for u in range(QUAD):
                    dve.wait_ge(rows_here[s.b][u], 16 * s.i + 16)
                    wts = weights[0][:, ds((s.n * QUAD + u) * HEADS, HEADS)]
                    dve.tensor_copy(msg[:, s.b, u, P:P + HEADS], wts)
                    dve.tensor_tensor(msg[:, s.b, u, 0:P].rearrange("p (h k) -> p h k", k=HEAD_DIM),
                                      raw[:, s.b, u, :].rearrange("p (h k) -> p h k", k=HEAD_DIM),
                                      wts.unsqueeze(2).broadcast_to([P, HEADS, HEAD_DIM]), ALU.mult).then_inc(msg_done[s.b], 1)
                    dve.wait_ge(scattered[s.b][u], 16 * s.i)
                    dve.tensor_copy(res[:, s.b, u, cols:], weights[1][:, ds((s.n * QUAD + u) * HEADS, HEADS)]).then_inc(maxima_done[s.b], 1)

            compare(Step(0, 0, of))

            def body(s):
                compare(Step(s.i + (s.b + 1) // 2, (s.b + 1) % 2, of))
                if weights:
                    weigh(s)
                if mean:
                    dve.wait_ge(read_out[s.b], QUAD * s.i + QUAD)
                    dve.tensor_scalar(count[:, s.b, :], plain[:, s.b, :, width], 1.0, None, ALU.max).then_inc(share_done[s.b], 1)
                    dve.wait_ge(share_done[s.b], 2 * s.i + 1)
                    dve.reciprocal(share[:, s.b, :], count[:, s.b, :]).then_inc(share_done[s.b], 1)
                    dve.wait_ge(share_done[s.b], 2 * s.i + 2)
                    for u in range(QUAD):
                        dve.wait_ge(scattered[s.b][u], 16 * s.i)
                        dve.tensor_scalar(res[:, s.b, u, :], plain[:, s.b, u, 0:width], share[:, s.b, u:u + 1], None,
                                          ALU.mult).then_inc(res_done[s.b], 1)
            run_steps(dve, of, 0, 0, body)

        @block.tensor
        def _(pe):
            def body(s):
                pe.wait_ge(read_out[s.b], QUAD * s.i)
                for u in range(QUAD):
                    pe.wait_ge(same_done[s.b], QUAD * s.i + u + 1)
                    pe.wait_ge(carried[s.b], QUAD * s.i + u + 1)
                    pe.matmul(sums[s.b][:, u, 0:cols], same[:, s.b, u, :], msg[:, s.b, u, :], start=True, stop=True
                              ).then_inc(summed[s.b], 1)
            run_steps(pe, of, 0, 0, body)


def sage_hidden(nc, g):
    with Phase(nc, "hid") as ph:
        x_in, m_in = ph.sb("x_in", [P, 2, QUAD, P]), ph.sb("m_in", [P, 2, QUAD, P])
        xT, mT = ph.sb("xT", [P, 2, GROUP]), ph.sb("mT", [P, 2, GROUP])
        biased, h = ph.sb("biased", [P, 2, GROUP]), ph.sb("h", [P, 2, QUAD, P])
        ps_x, ps_m = [ph.ps(f"ps_x{b}") for b in range(2)], [ph.ps(f"ps_m{b}") for b in range(2)]
        ps_h = [ph.ps(f"ps_h{b}") for b in range(2)]
        x_here, m_here, stored = ph.sems("x_here"), ph.sems("m_here"), ph.sems("stored")
        x_turned, m_turned, xT_done, mT_done = ph.sems("x_turned"), ph.sems("m_turned"), ph.sems("xT_done"), ph.sems("mT_done")
        sp_turn = ph.sem("sp_turn")
        h_summed, biased_done, h_done = ph.sems("h_summed"), ph.sems("biased_done"), ph.sems("h_done")
        block = ph.block()
        of = g.groups

        @block.sync
        def _(sp):
            def body(s):
                if l := s.at(2):
                    hold(sp, sp_turn, x_turned[l.b], l.i)
                    hold(sp, sp_turn, m_turned[l.b], l.i)
                    sp.dma_start(x_in[:, l.b, :, :], group_rows(g.x, l.n)).then_inc(x_here[l.b], 16)
                    sp.dma_start(m_in[:, l.b, :, :], group_rows(g.seg, l.n)).then_inc(m_here[l.b], 16)
                if s.at(0):
                    hold(sp, sp_turn, h_done[s.b], s.i + 1)
                    sp.dma_start(group_rows(g.h1, s.n), h[:, s.b, :, :]).then_inc(stored[s.b], 16)
            run_steps(sp, of, 2, 0, body)
            for b in range(2):
                sp.wait_ge(stored[b], 16 * (of // 2))

        @block.tensor
        def _(pe):
            def body(s):
                if t := s.at(1):
                    pe.wait_ge(x_here[t.b], 16 * t.i + 16)
                    pe.wait_ge(xT_done[t.b], t.i)
                    for j in range(QUAD):
                        turned = pe.transpose(ps_x[t.b][:, j * P:(j + 1) * P], x_in[:, t.b, j, :], g.ident[:, :])
                    turned.then_inc(x_turned[t.b], 1)
                    pe.wait_ge(m_here[t.b], 16 * t.i + 16)
                    pe.wait_ge(mT_done[t.b], t.i)
                    for j in range(QUAD):
                        turned = pe.transpose(ps_m[t.b][:, j * P:(j + 1) * P], m_in[:, t.b, j, :], g.ident[:, :])
                    turned.then_inc(m_turned[t.b], 1)
                if s.at(0):
                    pe.wait_ge(xT_done[s.b], s.i + 1)
                    pe.wait_ge(mT_done[s.b], s.i + 1)
                    pe.wait_ge(biased_done[s.b], s.i)
                    for j in range(QUAD):
                        c = slice(j * P, (j + 1) * P)
                        pe.matmul(ps_h[s.b][:, c], mT[:, s.b, c], g.w["W1lT"][:, :], start=True, stop=False)
                        last = pe.matmul(ps_h[s.b][:, c], xT[:, s.b, c], g.w["W1rT"][:, :], start=False, stop=True)
                    last.then_inc(h_summed[s.b], 1)
            run_steps(pe, of, 1, 0, body)

        @block.scalar
        def _(act):
            def body(s):
                if s.at(0):
                    act.wait_ge(x_turned[s.b], s.i + 1)
                    act.wait_ge(h_summed[s.b], s.i)
                    act.copy(xT[:, s.b, :], ps_x[s.b][:, :]).then_inc(xT_done[s.b], 1)
                if r := s.at(-1):
                    act.wait_ge(biased_done[r.b], r.i + 1)
                    act.wait_ge(stored[r.b], 16 * r.i)
                    act.activation(h[:, r.b, :, :].rearrange("p j d -> p (j d)"), biased[:, r.b, :], ACT.Relu).then_inc(h_done[r.b], 1)
            run_steps(act, of, 0, 1, body)

        @block.vector
        def _(dve):
            def body(s):
                if s.at(0):
                    dve.wait_ge(m_turned[s.b], s.i + 1)
                    dve.wait_ge(h_summed[s.b], s.i)
                    dve.tensor_copy(mT[:, s.b, :], ps_m[s.b][:, :]).then_inc(mT_done[s.b], 1)
                if r := s.at(-1):
                    dve.wait_ge(h_summed[r.b], r.i + 1)
                    dve.wait_ge(h_done[r.b], r.i)
                    dve.tensor_tensor(biased[:, r.b, :], ps_h[r.b][:, :], g.row["b1l"][:, :], ALU.add).then_inc(biased_done[r.b], 1)
            run_steps(dve, of, 0, 1, body)


class Norm:

    def __init__(self, ph, name):
        self.stats = ph.sb(f"{name}_stats", [P, 2, QUAD, 6])
        self.moments = ph.sb(f"{name}_moments", [P, 2, QUAD, 2])
        self.shifted = ph.sb(f"{name}_shifted", [P, 2, QUAD])
        self.rstd = ph.sb(f"{name}_rstd", [P, 2, QUAD])
        self.dve_turn = ph.sem(f"{name}_dve_turn")
        self.stats_done = ph.sems(f"{name}_stats_done")
        self.moments_done = ph.sems(f"{name}_moments_done")
        self.shifted_done = ph.sems(f"{name}_shifted_done")
        self.rstd_done = ph.sems(f"{name}_rstd_done")

    def moments_of(self, dve, s, value):
        dve.wait_ge(self.rstd_done[s.b], s.i)
        for j in range(QUAD):
            dve.bn_stats(self.stats[:, s.b, j, :], value[:, s.b, j, :]).then_inc(self.stats_done[s.b], 1)
        hold(dve, self.dve_turn, self.stats_done[s.b], QUAD * s.i + QUAD)
        for j in range(QUAD):
            dve.bn_aggr(self.moments[:, s.b, j, :], self.stats[:, s.b, j, :]).then_inc(self.moments_done[s.b], 1)

    def deviation(self, pool, s, minus_half):
        pool.wait_ge(self.moments_done[s.b], QUAD * s.i + QUAD)
        pool.tensor_tensor(self.shifted[:, s.b, :], self.moments[:, s.b, :, 1], minus_half[:, QUAD:], ALU.add).then_inc(self.shifted_done[s.b], 1)
        pool.wait_ge(self.shifted_done[s.b], s.i + 1)
        pool.tensor_tensor(self.rstd[:, s.b, :], self.shifted[:, s.b, :], minus_half[:, 0:QUAD], ALU.pow).then_inc(self.rstd_done[s.b], 1)

    def apply(self, dve, s, out, value, done):
        dve.wait_ge(self.rstd_done[s.b], s.i + 1)
        for j in range(QUAD):
            last = dve.tensor_scalar(out[:, s.b, j, :], value[:, s.b, j, :], self.moments[:, s.b, j, 0:1],
                                     self.rstd[:, s.b, j:j + 1], ALU.subtract, ALU.mult)
        last.then_inc(done[s.b], 1)


def power_constants(ph, pool, tile, done):
    pool.memset(tile[:, 0:QUAD], -0.5).then_inc(done, 1)
    pool.memset(tile[:, QUAD:], EPS).then_inc(done, 1)
    pool.wait_ge(done, 2)


def turn_group(pe, psum, tile, s, ident, done):
    for j in range(QUAD):
        last = pe.transpose(psum[:, j * P:(j + 1) * P], tile[:, s.b, j, :], ident[:, :])
    last.then_inc(done[s.b], 1)


def flat(tile, b):
    return tile[:, b, :, :].rearrange("p j d -> p (j d)")


def sage_out(nc, g):
    with Phase(nc, "sageout") as ph:
        x_in, m_in, h_in = (ph.sb(n, [P, 2, QUAD, P]) for n in ("x_in", "m_in", "h_in"))
        mT, hT, x1T = (ph.sb(n, [P, 2, GROUP]) for n in ("mT", "hT", "x1T"))
        resid, value, x1 = (ph.sb(n, [P, 2, QUAD, P]) for n in ("resid", "value", "x1"))
        th, ta = ph.sb("th", [P, 2, QUAD, P]), ph.sb("ta", [P, 2, QUAD, 2 * HEADS])
        minus_half = ph.sb("minus_half", [P, 2 * QUAD])
        ps_m, ps_h, ps_1 = ph.ps("ps_m"), ph.ps("ps_h"), ph.ps("ps_1")
        ps_v, ps_th = [ph.ps(f"ps_v{b}") for b in range(2)], [ph.ps(f"ps_th{b}") for b in range(2)]
        ps_ta = ph.ps("ps_ta", [P, 2, QUAD, 2 * HEADS])
        norm = Norm(ph, "norm")
        x_here, m_here, h_here, x1_stored, th_stored, ta_stored = (ph.sems(n) for n in (
            "x_here", "m_here", "h_here", "x1_stored", "th_stored", "ta_stored"))
        m_turned, h_turned, x1_turned, mT_done, hT_done, x1T_done = (ph.sems(n) for n in (
            "m_turned", "h_turned", "x1_turned", "mT_done", "hT_done", "x1T_done"))
        v_summed, th_summed, resid_done, value_done, x1_done, th_done, ta_done = (ph.sems(n) for n in (
            "v_summed", "th_summed", "resid_done", "value_done", "x1_done", "th_done", "ta_done"))
        sp_turn, consts = ph.sem("sp_turn"), ph.sem("consts")
        block = ph.block()
        of = g.groups

        @block.sync
        def _(sp):
            def body(s):
                if l := s.at(2):
                    hold(sp, sp_turn, resid_done[l.b], l.i)
                    sp.dma_start(x_in[:, l.b, :, :], group_rows(g.x, l.n)).then_inc(x_here[l.b], 16)
                    hold(sp, sp_turn, m_turned[l.b], l.i)
                    sp.dma_start(m_in[:, l.b, :, :], group_rows(g.seg, l.n)).then_inc(m_here[l.b], 16)
                    hold(sp, sp_turn, h_turned[l.b], l.i)
                    sp.dma_start(h_in[:, l.b, :, :], group_rows(g.h1, l.n)).then_inc(h_here[l.b], 16)
                if r := s.at(-1):
                    hold(sp, sp_turn, x1_done[r.b], r.i + 1)
                    sp.dma_start(group_rows(g.x1, r.n), x1[:, r.b, :, :]).then_inc(x1_stored[r.b], 16)
                if r := s.at(-2):
                    hold(sp, sp_turn, th_done[r.b], r.i + 1)
                    sp.dma_start(group_rows(g.th, r.n), th[:, r.b, :, :]).then_inc(th_stored[r.b], 16)
                    hold(sp, sp_turn, ta_done[r.b], r.i + 1)
                    sp.dma_start(group_rows(g.ta, r.n, 2 * HEADS), ta[:, r.b, :, :]).then_inc(ta_stored[r.b], 16)
            run_steps(sp, of, 2, 2, body)
            for b in range(2):
                for stored in (x1_stored, th_stored, ta_stored):
                    sp.wait_ge(stored[b], 16 * (of // 2))

        @block.tensor
        def _(pe):
            def body(s):
                if r := s.at(-2):
                    pe.wait_ge(x1_done[r.b], r.i + 1)
                    q = r.at(-1)
                    if q:
                        pe.wait_ge(x1T_done[q.b], q.i + 1)
                    turn_group(pe, ps_1, x1, r, g.ident, x1_turned)
                if t := s.at(1):
                    q = t.at(-1)
                    pe.wait_ge(m_here[t.b], 16 * t.i + 16)
                    if q:
                        pe.wait_ge(mT_done[q.b], q.i + 1)
                    turn_group(pe, ps_m, m_in, t, g.ident, m_turned)
                    pe.wait_ge(h_here[t.b], 16 * t.i + 16)
                    if q:
                        pe.wait_ge(hT_done[q.b], q.i + 1)
                    turn_group(pe, ps_h, h_in, t, g.ident, h_turned)
                if s.at(0):
                    pe.wait_ge(mT_done[s.b], s.i + 1)
                    pe.wait_ge(hT_done[s.b], s.i + 1)
                    pe.wait_ge(value_done[s.b], s.i)
                    for j in range(QUAD):
                        c = slice(j * P, (j + 1) * P)
                        pe.matmul(ps_v[s.b][:, c], mT[:, s.b, c], g.w["W2lT"][:, :], start=True, stop=False)
                        last = pe.matmul(ps_v[s.b][:, c], hT[:, s.b, c], g.w["W2rT"][:, :], start=False, stop=True)
                    last.then_inc(v_summed[s.b], 1)
                if r := s.at(-2):
                    pe.wait_ge(x1T_done[r.b], r.i + 1)
                    pe.wait_ge(th_done[r.b], r.i)
                    q = r.at(-1)
                    if q:
                        pe.wait_ge(ta_done[q.b], q.i + 1)
                    for j in range(QUAD):
                        c = slice(j * P, (j + 1) * P)
                        pe.matmul(ps_ta[:, r.b, j, :], x1T[:, r.b, c], g.w["attT"][:, :], start=True, stop=True)
                        last = pe.matmul(ps_th[r.b][:, c], x1T[:, r.b, c], g.w["linT"][:, :], start=True, stop=True)
                    last.then_inc(th_summed[r.b], 1)
            run_steps(pe, of, 1, 2, body)

        @block.scalar
        def _(act):
            def body(s):
                if r := s.at(-2):
                    act.wait_ge(x1_turned[r.b], r.i + 1)
                    act.wait_ge(th_summed[r.b], r.i)
                    act.copy(x1T[:, r.b, :], ps_1[:, :]).then_inc(x1T_done[r.b], 1)
                if t := s.at(1):
                    act.wait_ge(h_turned[t.b], t.i + 1)
                    act.wait_ge(v_summed[t.b], t.i)
                    act.copy(hT[:, t.b, :], ps_h[:, :]).then_inc(hT_done[t.b], 1)
                if r := s.at(-2):
                    act.wait_ge(th_summed[r.b], r.i + 1)
                    act.wait_ge(th_stored[r.b], 16 * r.i)
                    act.copy(flat(th, r.b), ps_th[r.b][:, :]).then_inc(th_done[r.b], 1)
                    act.wait_ge(ta_stored[r.b], 16 * r.i)
                    act.copy(ta[:, r.b, :, :], ps_ta[:, r.b, :, :]).then_inc(ta_done[r.b], 1)
            run_steps(act, of, 1, 2, body)

        @block.gpsimd
        def _(pool):
            power_constants(ph, pool, minus_half, consts)

            def body(s):
                if s.at(0):
                    pool.wait_ge(x_here[s.b], 16 * s.i + 16)
                    pool.wait_ge(value_done[s.b], s.i)
                    pool.tensor_tensor(flat(resid, s.b), flat(x_in, s.b), g.row["b2l"][:, :], ALU.add).then_inc(resid_done[s.b], 1)
                if r := s.at(-1):
                    norm.deviation(pool, r, minus_half)
            run_steps(pool, of, 0, 1, body)

        @block.vector
        def _(dve):
            def body(s):
                if t := s.at(1):
                    dve.wait_ge(m_turned[t.b], t.i + 1)
                    dve.wait_ge(v_summed[t.b], t.i)
                    dve.tensor_copy(mT[:, t.b, :], ps_m[:, :]).then_inc(mT_done[t.b], 1)
                if s.at(0):
                    dve.wait_ge(v_summed[s.b], s.i + 1)
                    dve.wait_ge(resid_done[s.b], s.i + 1)
                    dve.wait_ge(x1_done[s.b], s.i)
                    dve.tensor_tensor(flat(value, s.b), ps_v[s.b][:, :], flat(resid, s.b), ALU.add).then_inc(value_done[s.b], 1)
                if r := s.at(-1):
                    dve.wait_ge(x1_stored[r.b], 16 * r.i)
                    dve.wait_ge(x1_turned[r.b], r.i)
                    norm.apply(dve, r, x1, value, x1_done)
                if s.at(0):
                    dve.wait_ge(value_done[s.b], s.i + 1)
                    norm.moments_of(dve, s, value)
            run_steps(dve, of, 1, 1, body)


def edge_scores(nc, g):
    with Phase(nc, "score") as ph:
        src_ix, dst_ix = ph.sb("src_ix", [P, 2, QUAD], I32), ph.sb("dst_ix", [P, 2, QUAD], I32)
        at_src, at_dst = ph.sb("at_src", [P, 2, QUAD, 2 * HEADS]), ph.sb("at_dst", [P, 2, QUAD, 2 * HEADS])
        sums = ph.sb("sums", [P, 2, 2, QUAD, HEADS])
        leaky = ph.sb("leaky", [P, 2, 2, QUAD, HEADS])
        ix_here = ph.sems("ix_here")
        src_rows = [ph.sems(f"src_rows{b}_", QUAD) for b in range(2)]
        dst_rows = [ph.sems(f"dst_rows{b}_", QUAD) for b in range(2)]
        summed, leaky_done, score_done = ph.sems("summed"), ph.sems("leaky_done"), ph.sems("score_done")
        pool_turn, sp_turn = ph.sem("pool_turn"), ph.sem("sp_turn")
        block = ph.block()
        of = g.quads

        @block.sync
        def _(sp):
            def load(s):
                sp.dma_start(src_ix[:, s.b, :], g.srcw[:, ds(s.n * QUAD, QUAD)]).then_inc(ix_here[s.b], 16)
                sp.dma_start(dst_ix[:, s.b, :], g.dstw[:, ds(s.n * QUAD, QUAD)]).then_inc(ix_here[s.b], 16)

            def body(s):
                if l := s.at(2):
                    for u in range(QUAD):
                        hold(sp, sp_turn, src_rows[l.b][u], 16 * l.i)
                        hold(sp, sp_turn, dst_rows[l.b][u], 16 * l.i)
                    load(l)
            run_steps(sp, of, 2, 0, body)

        @block.gpsimd
        def _(pool):
            def body(s):
                hold(pool, pool_turn, ix_here[s.b], 32 * s.i + 32)
                hold(pool, pool_turn, summed[s.b], 2 * s.i)
                for u in range(QUAD):
                    for ix, rows, here in ((src_ix, at_src, src_rows), (dst_ix, at_dst, dst_rows)):
                        pool.indirect_dma_start(out=rows[:, s.b, u, :], out_offset=None, in_=g.ta,
                                                in_offset=bass.IndirectOffsetOnAxis(ap=ix[:, s.b, u:u + 1], axis=0)
                                                ).then_inc(here[s.b][u], 16)
            run_steps(pool, of, 0, 0, body)

        @block.vector
        def _(dve):
            def body(s):
                for u in range(QUAD):
                    dve.wait_ge(src_rows[s.b][u], 16 * s.i + 16)
                    dve.wait_ge(dst_rows[s.b][u], 16 * s.i + 16)
                dve.tensor_tensor(sums[:, s.b, 0, :, :], at_src[:, s.b, :, 0:HEADS], at_dst[:, s.b, :, HEADS:], ALU.add).then_inc(summed[s.b], 1)
                dve.tensor_tensor(sums[:, s.b, 1, :, :], at_dst[:, s.b, :, 0:HEADS], at_dst[:, s.b, :, HEADS:], ALU.add).then_inc(summed[s.b], 1)
                dve.wait_ge(summed[s.b], 2 * s.i + 2)
                both = sums[:, s.b, :, :, :].rearrange("p a t h -> p (a t h)")
                dve.scalar_tensor_tensor(leaky[:, s.b, :, :, :].rearrange("p a t h -> p (a t h)"), both, SLOPE, both,
                                         ALU.mult, ALU.max).then_inc(leaky_done[s.b], 1)
                dve.wait_ge(leaky_done[s.b], s.i + 1)
                dve.tensor_tensor(g.score[:, ds(s.n * QUAD * HEADS, QUAD * HEADS)],
                                  leaky[:, s.b, 0, :, :].rearrange("p t h -> p (t h)"),
                                  leaky[:, s.b, 1, :, :].rearrange("p t h -> p (t h)"), ALU.subtract).then_inc(score_done[s.b], 1)
            run_steps(dve, of, 0, 0, body)
            for b in range(2):
                dve.wait_ge(score_done[b], of // 2)
            dve.memset(g.score[0:1, :], LOW)


def edge_softmax(nc, g):
    runs = g.quads * QUAD // CHUNKS
    ch = CHUNKS * HEADS
    with Phase(nc, "soft") as ph:
        order = ph.sb("order", [ch, runs * P], I32)
        bar_up, bar_down = ph.sb("bar_up", [ch, runs * P]), ph.sb("bar_down", [ch, runs * P])
        line, up, down = (ph.sb(n, [ch, runs, P]) for n in ("line", "up", "down"))
        spare = ph.sb("spare", [ch, 2, runs])
        ends = ph.sb("ends", [ch, 4])
        row = ph.sb("row", [1, 4, CHUNKS, HEADS])
        carry = ph.sb("carry", [1, 2, CHUNKS, HEADS])
        init = ph.sb("init", [ch, 2])
        one = ph.sb("one", [1, 1])
        ps_in = [ph.ps(f"ps_in{k}") for k in range(2)]
        ps_out = [ph.ps(f"ps_out{k}") for k in range(2)]
        ps_row, ps_col = ph.ps("ps_row", [1, 512]), ph.ps("ps_col", [ch, 512])
        order_here, laid, line_read, line_done = ph.sem("order_here"), ph.sem("laid"), ph.sem("line_read"), ph.sem("line_done")
        step, scanned, back, back_read = ph.sem("step"), ph.sem("scanned"), ph.sem("back"), ph.sem("back_read")
        row_done, row_read, col_done, exp_done = ph.sem("row_done"), ph.sem("row_read"), ph.sem("col_done"), ph.sem("exp_done")
        block = ph.block()
        score = ph.sb("score", [P, runs, CHUNKS, HEADS])
        score_done = ph.sem("score_done")
        per = 512 // P
        trips = -(-runs // per)
        per_back = 512 // ch
        trips_back = 2 * -(-runs // per_back)

        @block.sync
        def _(sp):
            for c in range(CHUNKS):
                sp.dma_start(order[c * HEADS:(c + 1) * HEADS, :], g.order[c:c + 1, :].broadcast_to([HEADS, runs * P])).then_inc(order_here, 16)

        @block.tensor
        def _(pe):
            pe.wait_ge(score_done, 1)
            for k in range(trips):
                if k >= 2:
                    pe.wait_ge(line_read, k - 1)
                for r in range(k * per, min(runs, (k + 1) * per)):
                    last = pe.transpose(ps_in[k % 2][0:ch, (r % per) * P:(r % per + 1) * P],
                                        score[:, r, :, :].rearrange("p c h -> p (c h)"), g.ident[:, :])
                last.then_inc(laid, 1)
            pe.wait_ge(scanned, 1)
            for k in range(4):
                last = pe.transpose(ps_row[0:1, k * ch:(k + 1) * ch], ends[:, k:k + 1], g.ident[0:ch, 0:ch])
            last.then_inc(row_done, 1)
            pe.wait_ge(row_read, 1)
            for k in range(2):
                last = pe.matmul(ps_col[:, k:k + 1], carry[0:1, k, :, :].rearrange("p c h -> p (c h)"), one[0:1, 0:1], start=True, stop=True)
            last.then_inc(col_done, 1)
            pe.wait_ge(exp_done, 2)
            k = 0
            for source in (up, down):
                for a in range(0, runs, per_back):
                    if k >= 2:
                        pe.wait_ge(back_read, k - 1)
                    for r in range(a, min(runs, a + per_back)):
                        last = pe.transpose(ps_out[k % 2][:, (r - a) * ch:(r - a + 1) * ch], source[:, r, :], g.ident[0:ch, 0:ch])
                    last.then_inc(back, 1)
                    k += 1

        @block.scalar
        def _(act):
            for k in range(trips):
                act.wait_ge(laid, k + 1)
                a, z = k * per, min(runs, (k + 1) * per)
                act.copy(line[:, a:z, :].rearrange("p r e -> p (r e)"), ps_in[k % 2][0:ch, 0:(z - a) * P]).then_inc(line_read, 1)
            act.wait_ge(exp_done, 1)
            act.activation(up[:, :, :], up[:, :, :], ACT.Exp).then_inc(exp_done, 1)

        @block.vector
        def _(dve):
            done = [0]

            def chain(ins):
                done[0] += 1
                ins.then_inc(step, 1)
                dve.wait_ge(step, done[0])

            def exchange(tile):
                dve.tensor_copy(spare[:, 0, :], tile[:, :, LAST_SLOT])
                chain(dve.tensor_copy(spare[:, 1, :], tile[:, :, P - 1]))
                dve.tensor_copy(tile[:, :, LAST_SLOT], spare[:, 1, :])
                chain(dve.tensor_copy(tile[:, :, P - 1], spare[:, 0, :]))

            dve.tensor_copy(score[:, :, :, :].rearrange("p r c h -> p c r h"),
                            g.score[:, 0:CHUNKS * runs * HEADS].rearrange("p (c r h) -> p c r h", c=CHUNKS, r=runs)).then_inc(score_done, 1)
            dve.memset(one[:, :], 1.0)
            dve.memset(carry[0:1, 0, 0, :], LOW)
            dve.memset(carry[0:1, 1, CHUNKS - 1, :], LOW)
            dve.memset(bar_up[:, 0:1], 0.0)
            dve.memset(bar_down[:, runs * P - 1:], 0.0)
            dve.wait_ge(order_here, 16 * CHUNKS)
            dve.tensor_tensor(bar_up[:, 1:], order[:, 1:], order[:, 0:runs * P - 1], ALU.not_equal)
            chain(dve.tensor_tensor(bar_down[:, 0:runs * P - 1], order[:, 1:], order[:, 0:runs * P - 1], ALU.not_equal))
            dve.tensor_scalar(bar_up[:, :], bar_up[:, :], LOW, None, ALU.mult)
            chain(dve.tensor_scalar(bar_down[:, :], bar_down[:, :], LOW, None, ALU.mult))
            dve.tensor_reduce(ends[:, 2:3], bar_up[:, :], mybir.AxisListType.X, ALU.min)
            chain(dve.tensor_reduce(ends[:, 3:4], bar_down[:, :], mybir.AxisListType.X, ALU.min))
            dve.wait_ge(line_read, trips)
            exchange(line)
            scores = line[:, :, :].rearrange("p r e -> p (r e)")
            ups, downs = up[:, :, :].rearrange("p r e -> p (r e)"), down[:, :, :].rearrange("p r e -> p (r e)")

            def scan(first_up, first_down):
                dve.tensor_tensor_scan(ups, bar_up[:, :], scores, first_up, ALU.add, ALU.max)
                chain(dve.tensor_tensor_scan(downs[:, ::-1], bar_down[:, ::-1], scores[:, ::-1], first_down, ALU.add, ALU.max))

            scan(LOW, LOW)
            dve.tensor_copy(ends[:, 0:1], ups[:, runs * P - 1:])
            chain(dve.tensor_copy(ends[:, 1:2], downs[:, 0:1]))
            dve.sem_inc(scanned, 1)
            dve.wait_ge(row_done, 1)
            chain(dve.tensor_copy(row[0:1, :, :, :].rearrange("p k c h -> p (k c h)"), ps_row[0:1, 0:4 * ch]))
            for c in range(1, CHUNKS):
                z = CHUNKS - 1 - c
                dve.scalar_tensor_tensor(carry[0:1, 0, c, :], carry[0:1, 0, c - 1, :], row[0:1, 2, c - 1, 0:1], row[0:1, 0, c - 1, :],
                                         ALU.add, ALU.max)
                chain(dve.scalar_tensor_tensor(carry[0:1, 1, z, :], carry[0:1, 1, z + 1, :], row[0:1, 3, z + 1, 0:1],
                                               row[0:1, 1, z + 1, :], ALU.add, ALU.max))
            dve.sem_inc(row_read, 1)
            dve.wait_ge(col_done, 1)
            chain(dve.tensor_copy(init[:, :], ps_col[:, 0:2]))
            scan(init[:, 0:1], init[:, 1:2])
            chain(dve.scalar_tensor_tensor(downs, downs, 0.0, ups, ALU.max, ALU.max))
            chain(dve.tensor_tensor(ups, scores, downs, ALU.subtract))
            exchange(down)
            exchange(up)
            dve.sem_inc(exp_done, 1)
            k = 0
            for dst in (g.weight, g.peak):
                into = dst[:, 0:CHUNKS * runs * HEADS].rearrange("p (c r h) -> p c r h", c=CHUNKS, r=runs)
                for a in range(0, runs, per_back):
                    z = min(runs, a + per_back)
                    dve.wait_ge(back, k + 1)
                    for r in range(a, z):
                        last = dve.tensor_copy(into[:, :, r, :], ps_out[k % 2][:, (r - a) * ch:(r - a + 1) * ch].rearrange("p (c h) -> p c h", c=CHUNKS))
                    last.then_inc(back_read, 1)
                    k += 1


def apply_affine(dve, norm, s, between, out, value, gamma, extra, between_done, out_done):
    dve.wait_ge(norm.rstd_done[s.b], s.i + 1)
    for j in range(QUAD):
        dve.scalar_tensor_tensor(between[:, s.b, j, :], value[:, s.b, j, :], norm.moments[:, s.b, j, 0:1],
                                 gamma[:, 0:P], ALU.subtract, ALU.mult).then_inc(between_done[s.b], 1)
    dve.wait_ge(between_done[s.b], QUAD * s.i + QUAD)
    for j in range(QUAD):
        last = dve.scalar_tensor_tensor(out[:, s.b, j, :], between[:, s.b, j, :], norm.rstd[:, s.b, j:j + 1],
                                        extra[:, s.b, j, :], ALU.mult, ALU.add)
    last.then_inc(out_done[s.b], 1)


def gat_out(nc, g):
    with Phase(nc, "gatout") as ph:
        x_in, th_in, s_in = ph.sb("x_in", [P, 2, QUAD, P]), ph.sb("th_in", [P, 2, QUAD, P]), ph.sb("s_in", [P, 2, QUAD, AUG])
        loop_w, total_w, share = (ph.sb(n, [P, 2, QUAD, HEADS]) for n in ("loop_w", "total_w", "share"))
        own, total, mean = (ph.sb(n, [P, 2, QUAD, P]) for n in ("own", "total", "mean"))
        meanT = ph.sb("meanT", [P, 2, GROUP])
        value, between, value2, extra, x2 = (ph.sb(n, [P, 2, QUAD, P]) for n in ("value", "between", "value2", "extra", "x2"))
        minus_half = ph.sb("minus_half", [P, 2 * QUAD])
        ps_m, ps_v = [ph.ps(f"ps_m{b}") for b in range(2)], [ph.ps(f"ps_v{b}") for b in range(2)]
        norm, norm2 = Norm(ph, "norm"), Norm(ph, "norm2")
        x_here, th_here, s_here, stored = (ph.sems(n) for n in ("x_here", "th_here", "s_here", "stored"))
        (loop_done, total_w_done, share_done, own_done, total_done, mean_done, turned, meanT_done, v_summed, value_done,
         between_done, value2_done, extra_done, x2_done) = (ph.sems(n) for n in (
             "loop_done", "total_w_done", "share_done", "own_done", "total_done", "mean_done", "turned", "meanT_done",
             "v_summed", "value_done", "between_done", "value2_done", "extra_done", "x2_done"))
        sp_turn, consts = ph.sem("sp_turn"), ph.sem("consts")
        block = ph.block()
        of = g.groups

        def by_head(tile, b):
            return tile[:, b, :, :].rearrange("p j (h k) -> p (j h) k", k=HEAD_DIM)

        def spread(tile, b):
            return tile[:, b, :, :].rearrange("p j h -> p (j h)").unsqueeze(2).broadcast_to([P, QUAD * HEADS, HEAD_DIM])

        @block.sync
        def _(sp):
            def body(s):
                if l := s.at(2):
                    hold(sp, sp_turn, own_done[l.b], l.i)
                    sp.dma_start(th_in[:, l.b, :, :], group_rows(g.th, l.n)).then_inc(th_here[l.b], 16)
                    hold(sp, sp_turn, total_done[l.b], l.i)
                    sp.dma_start(s_in[:, l.b, :, :], group_rows(g.gat, l.n, AUG)).then_inc(s_here[l.b], 16)
                    hold(sp, sp_turn, extra_done[l.b], l.i)
                    sp.dma_start(x_in[:, l.b, :, :], group_rows(g.x1, l.n)).then_inc(x_here[l.b], 16)
                if r := s.at(-3):
                    hold(sp, sp_turn, x2_done[r.b], r.i + 1)
                    sp.dma_start(group_rows(g.x2, r.n), x2[:, r.b, :, :]).then_inc(stored[r.b], 16)
            run_steps(sp, of, 2, 3, body)
            for b in range(2):
                sp.wait_ge(stored[b], 16 * (of // 2))

        @block.scalar
        def _(act):
            def body(s):
                if s.at(0):
                    act.wait_ge(s_here[s.b], 16 * s.i + 16)
                    act.wait_ge(own_done[s.b], s.i)
                    act.wait_ge(total_w_done[s.b], s.i)
                    act.activation(loop_w[:, s.b, :, :], s_in[:, s.b, :, P + HEADS:], ACT.Exp, scale=-1.0).then_inc(loop_done[s.b], 1)
                if r := s.at(-1):
                    act.wait_ge(turned[r.b], r.i + 1)
                    act.wait_ge(v_summed[r.b], r.i)
                    act.activation(meanT[:, r.b, :], ps_m[r.b][:, :], ACT.Identity, bias=g.col[:, 0:1]).then_inc(meanT_done[r.b], 1)
            run_steps(act, of, 0, 1, body)

        @block.gpsimd
        def _(pool):
            power_constants(ph, pool, minus_half, consts)

            def body(s):
                if s.at(0):
                    pool.wait_ge(th_here[s.b], 16 * s.i + 16)
                    pool.wait_ge(loop_done[s.b], s.i + 1)
                    pool.wait_ge(total_done[s.b], s.i)
                    pool.tensor_tensor(by_head(own, s.b), by_head(th_in, s.b), spread(loop_w, s.b), ALU.mult).then_inc(own_done[s.b], 1)
                if r := s.at(-2):
                    norm2.deviation(pool, r, minus_half)
                if r := s.at(-1):
                    pool.wait_ge(x_here[r.b], 16 * r.i + 16)
                    pool.wait_ge(value2_done[r.b], r.i)
                    pool.tensor_tensor(flat(extra, r.b), flat(x_in, r.b), g.row["ln1_beta"][:, :], ALU.add).then_inc(extra_done[r.b], 1)
                    norm.deviation(pool, r, minus_half)
            run_steps(pool, of, 0, 2, body)

        @block.tensor
        def _(pe):
            def body(s):
                if s.at(0):
                    pe.wait_ge(mean_done[s.b], s.i + 1)
                    pe.wait_ge(meanT_done[s.b], s.i)
                    turn_group(pe, ps_m[s.b], mean, s, g.ident, turned)
                if r := s.at(-1):
                    pe.wait_ge(meanT_done[r.b], r.i + 1)
                    pe.wait_ge(value_done[r.b], r.i)
                    for j in range(QUAD):
                        c = slice(j * P, (j + 1) * P)
                        last = pe.matmul(ps_v[r.b][:, c], meanT[:, r.b, c], g.w["projT"][:, :], start=True, stop=True)
                    last.then_inc(v_summed[r.b], 1)
            run_steps(pe, of, 0, 1, body)

        @block.vector
        def _(dve):
            def body(s):
                if s.at(0):
                    dve.wait_ge(loop_done[s.b], s.i + 1)
                    dve.tensor_tensor(total_w[:, s.b, :, :], loop_w[:, s.b, :, :], s_in[:, s.b, :, P:P + HEADS], ALU.add).then_inc(total_w_done[s.b], 1)
                if r := s.at(-3):
                    dve.wait_ge(stored[r.b], 16 * r.i)
                    norm2.apply(dve, r, x2, value2, x2_done)
                if s.at(0):
                    dve.wait_ge(total_w_done[s.b], s.i + 1)
                    dve.reciprocal(share[:, s.b, :, :], total_w[:, s.b, :, :]).then_inc(share_done[s.b], 1)
                if r := s.at(-2):
                    dve.wait_ge(extra_done[r.b], r.i + 1)
                    dve.wait_ge(x2_done[r.b], r.i)
                    apply_affine(dve, norm, r, between, value2, value, g.row["ln1_gamma"], extra, between_done, value2_done)
                if s.at(0):
                    dve.wait_ge(own_done[s.b], s.i + 1)
                    dve.tensor_tensor(total[:, s.b, :, :], own[:, s.b, :, :], s_in[:, s.b, :, 0:P], ALU.add).then_inc(total_done[s.b], 1)
                if r := s.at(-2):
                    dve.wait_ge(value2_done[r.b], r.i + 1)
                    norm2.moments_of(dve, r, value2)
                if s.at(0):
                    dve.wait_ge(total_done[s.b], s.i + 1)
                    dve.wait_ge(share_done[s.b], s.i + 1)
                    dve.wait_ge(turned[s.b], s.i)
                    dve.tensor_tensor(by_head(mean, s.b), by_head(total, s.b), spread(share, s.b), ALU.mult).then_inc(mean_done[s.b], 1)
                if r := s.at(-1):
                    dve.wait_ge(v_summed[r.b], r.i + 1)
                    dve.wait_ge(between_done[r.b], QUAD * r.i)
                    dve.tensor_tensor(flat(value, r.b), ps_v[r.b][:, :], g.row["proj_b"][:, :], ALU.add).then_inc(value_done[r.b], 1)
                    dve.wait_ge(value_done[r.b], r.i + 1)
                    norm.moments_of(dve, r, value)
            run_steps(dve, of, 0, 3, body)


def edge_mlp(nc, g):
    with Phase(nc, "mlp") as ph:
        x_in, e_in = ph.sb("x_in", [P, 2, QUAD, P]), ph.sb("e_in", [P, 2, QUAD, P])
        xT, eT, hid1, hid2 = (ph.sb(n, [P, 2, GROUP]) for n in ("xT", "eT", "hid1", "hid2"))
        value, between, value2, extra, twice, x3 = (ph.sb(n, [P, 2, QUAD, P]) for n in ("value", "between", "value2", "extra", "twice", "x3"))
        minus_half = ph.sb("minus_half", [P, 2 * QUAD])
        ps_x, ps_e, ps_1, ps_2 = ph.ps("ps_x"), ph.ps("ps_e"), ph.ps("ps_1"), ph.ps("ps_2")
        ps_v = [ph.ps(f"ps_v{b}") for b in range(2)]
        norm, norm2 = Norm(ph, "norm"), Norm(ph, "norm2")
        x_here, e_here, stored = (ph.sems(n) for n in ("x_here", "e_here", "stored"))
        (x_turned, e_turned, xT_done, eT_done, summed1, summed2, hid1_done, hid2_done, v_summed, value_done, twice_done,
         between_done, value2_done, extra_done, x3_done) = (ph.sems(n) for n in (
             "x_turned", "e_turned", "xT_done", "eT_done", "summed1", "summed2", "hid1_done", "hid2_done", "v_summed",
             "value_done", "twice_done", "between_done", "value2_done", "extra_done", "x3_done"))
        sp_turn, consts = ph.sem("sp_turn"), ph.sem("consts")
        block = ph.block()
        of = g.groups

        @block.sync
        def _(sp):
            def body(s):
                if l := s.at(2):
                    hold(sp, sp_turn, x_turned[l.b], l.i)
                    hold(sp, sp_turn, extra_done[l.b], l.i)
                    sp.dma_start(x_in[:, l.b, :, :], group_rows(g.x2, l.n)).then_inc(x_here[l.b], 16)
                    hold(sp, sp_turn, e_turned[l.b], l.i)
                    sp.dma_start(e_in[:, l.b, :, :], group_rows(g.seg, l.n, P, P)).then_inc(e_here[l.b], 16)
                if r := s.at(-3):
                    hold(sp, sp_turn, x3_done[r.b], r.i + 1)
                    sp.dma_start(group_rows(g.x3, r.n), x3[:, r.b, :, :]).then_inc(stored[r.b], 16)
            run_steps(sp, of, 2, 3, body)
            for b in range(2):
                sp.wait_ge(stored[b], 16 * (of // 2))

        @block.tensor
        def _(pe):
            def body(s):
                if t := s.at(1):
                    q = t.at(-1)
                    pe.wait_ge(x_here[t.b], 16 * t.i + 16)
                    if q:
                        pe.wait_ge(xT_done[q.b], q.i + 1)
                    turn_group(pe, ps_x, x_in, t, g.ident, x_turned)
                    pe.wait_ge(e_here[t.b], 16 * t.i + 16)
                    if q:
                        pe.wait_ge(eT_done[q.b], q.i + 1)
                    turn_group(pe, ps_e, e_in, t, g.ident, e_turned)
                if s.at(0):
                    pe.wait_ge(xT_done[s.b], s.i + 1)
                    pe.wait_ge(eT_done[s.b], s.i + 1)
                    if q := s.at(-1):
                        pe.wait_ge(hid1_done[q.b], q.i + 1)
                    pe.matmul(ps_1[:, :], g.w["W1"][:, 0, :], xT[:, s.b, :], start=True, stop=False)
                    pe.matmul(ps_1[:, :], g.w["W1"][:, 1, :], eT[:, s.b, :], start=False, stop=True).then_inc(summed1[s.b], 1)
                if r := s.at(-1):
                    pe.wait_ge(hid2_done[r.b], r.i + 1)
                    pe.wait_ge(value_done[r.b], r.i)
                    for j in range(QUAD):
                        c = slice(j * P, (j + 1) * P)
                        last = pe.matmul(ps_v[r.b][:, c], hid2[:, r.b, c], g.w["W3"][:, :], start=True, stop=True)
                    last.then_inc(v_summed[r.b], 1)
                if s.at(0):
                    pe.wait_ge(hid1_done[s.b], s.i + 1)
                    if q := s.at(-1):
                        pe.wait_ge(hid2_done[q.b], q.i + 1)
                    pe.matmul(ps_2[:, :], g.w["W2"][:, :], hid1[:, s.b, :], start=True, stop=True).then_inc(summed2[s.b], 1)
            run_steps(pe, of, 1, 1, body)

        @block.scalar
        def _(act):
            def body(s):
                if t := s.at(1):
                    act.wait_ge(x_turned[t.b], t.i + 1)
                    act.wait_ge(summed1[t.b], t.i)
                    act.copy(xT[:, t.b, :], ps_x[:, :]).then_inc(xT_done[t.b], 1)
                if s.at(0):
                    act.wait_ge(summed1[s.b], s.i + 1)
                    act.wait_ge(summed2[s.b], s.i)
                    act.activation(hid1[:, s.b, :], ps_1[:, :], ACT.Relu, bias=g.col[:, 1:2]).then_inc(hid1_done[s.b], 1)
                    act.wait_ge(x_here[s.b], 16 * s.i + 16)
                    act.wait_ge(extra_done[s.b], s.i)
                    act.mul(flat(twice, s.b), flat(x_in, s.b), 2.0).then_inc(twice_done[s.b], 1)
                    act.wait_ge(summed2[s.b], s.i + 1)
                    act.wait_ge(v_summed[s.b], s.i)
                    act.activation(hid2[:, s.b, :], ps_2[:, :], ACT.Relu, bias=g.col[:, 2:3]).then_inc(hid2_done[s.b], 1)
            run_steps(act, of, 1, 0, body)

        @block.gpsimd
        def _(pool):
            power_constants(ph, pool, minus_half, consts)

            def body(s):
                if r := s.at(-2):
                    norm2.deviation(pool, r, minus_half)
                if s.at(0):
                    pool.wait_ge(twice_done[s.b], s.i + 1)
                    pool.wait_ge(value2_done[s.b], s.i)
                    pool.tensor_tensor(flat(extra, s.b), flat(twice, s.b), g.row["ln2_beta"][:, :], ALU.add).then_inc(extra_done[s.b], 1)
                if r := s.at(-1):
                    norm.deviation(pool, r, minus_half)
            run_steps(pool, of, 0, 2, body)

        @block.vector
        def _(dve):
            def body(s):
                if t := s.at(1):
                    dve.wait_ge(e_turned[t.b], t.i + 1)
                    dve.wait_ge(summed1[t.b], t.i)
                    dve.tensor_copy(eT[:, t.b, :], ps_e[:, :]).then_inc(eT_done[t.b], 1)
                if r := s.at(-3):
                    dve.wait_ge(stored[r.b], 16 * r.i)
                    norm2.apply(dve, r, x3, value2, x3_done)
                if r := s.at(-2):
                    dve.wait_ge(extra_done[r.b], r.i + 1)
                    dve.wait_ge(x3_done[r.b], r.i)
                    apply_affine(dve, norm, r, between, value2, value, g.row["ln2_gamma"], extra, between_done, value2_done)
                if r := s.at(-1):
                    dve.wait_ge(v_summed[r.b], r.i + 1)
                    dve.wait_ge(between_done[r.b], QUAD * r.i)
                    dve.tensor_tensor(flat(value, r.b), ps_v[r.b][:, :], g.row["b3"][:, :], ALU.add).then_inc(value_done[r.b], 1)
                if r := s.at(-2):
                    dve.wait_ge(value2_done[r.b], r.i + 1)
                    norm2.moments_of(dve, r, value2)
                if r := s.at(-1):
                    dve.wait_ge(value_done[r.b], r.i + 1)
                    norm.moments_of(dve, r, value)
            run_steps(dve, of, 1, 3, body)


def messages(nc, g, t, hv):
    wide = 2 * P
    edge_dim = g.edge_t.shape[0]
    with Phase(nc, f"msg{t}") as ph:
        src_ix, dst_ix, tgt_ix = (ph.sb(n, [P, 2, QUAD], I32) for n in ("src_ix", "dst_ix", "tgt_ix"))
        drow = ph.sb("drow", [P, 2, QUAD, P], I32)
        edge = ph.sb("edge", [edge_dim, 2, GROUP])
        at_dst, at_src = ph.sb("at_dst", [P, 2, QUAD, P]), ph.sb("at_src", [P, 2, QUAD, P])
        dstT, srcT = ph.sb("dstT", [P, 2, GROUP]), ph.sb("srcT", [P, 2, GROUP])
        hidT = ph.sb("hidT", [P, 2, 2, GROUP])
        msg, same, res = ph.sb("msg", [P, 2, QUAD, wide]), ph.sb("same", [P, 2, QUAD, P]), ph.sb("res", [P, 2, QUAD, wide])
        ps_d, ps_s = ph.ps("ps_d"), ph.ps("ps_s")
        ps_h = [ph.ps(f"ps_h{m}") for m in range(2)]
        ps_msg = ph.ps("ps_msg", [P, QUAD, wide])
        banks = ph.ps("sums", [P, 2, 2, wide])
        sums = [banks[:, u % 2, u // 2, :] for u in range(QUAD)]
        src_here, dst_here, tgt_here, drow_here, edge_here = (ph.sems(n) for n in ("src_here", "dst_here", "tgt_here", "drow_here", "edge_here"))
        dst_rows = [ph.sems(f"dst_rows{b}_", QUAD) for b in range(2)]
        src_rows = [ph.sems(f"src_rows{b}_", QUAD) for b in range(2)]
        scattered = [ph.sems(f"scattered{b}_", QUAD) for b in range(2)]
        (dst_turned, src_turned, dstT_done, srcT_done, hid_summed, hid_done, msg_summed, msg_done, same_done, carried, summed,
         read_out) = (ph.sems(n) for n in (
             "dst_turned", "src_turned", "dstT_done", "srcT_done", "hid_summed", "hid_done", "msg_summed", "msg_done",
             "same_done", "carried", "summed", "read_out"))
        start, pool_turn, sp_turn = ph.sem("start"), ph.sem("pool_turn"), ph.sem("sp_turn")
        block = ph.block()
        of = g.quads

        @block.sync
        def _(sp):
            def body(s):
                if l := s.at(4):
                    for u in range(QUAD):
                        hold(sp, sp_turn, src_rows[l.b][u], 16 * l.i)
                        hold(sp, sp_turn, dst_rows[l.b][u], 16 * l.i)
                    sp.dma_start(dst_ix[:, l.b, :], g.dstw[:, ds(l.n * QUAD, QUAD)]).then_inc(dst_here[l.b], 16)
                    sp.dma_start(src_ix[:, l.b, :], g.srcw[:, ds(l.n * QUAD, QUAD)]).then_inc(src_here[l.b], 16)
                if l := s.at(2):
                    hold(sp, sp_turn, same_done[l.b], QUAD * l.i)
                    sp.dma_start(drow[:, l.b, :, :].rearrange("p t e -> p (t e)"),
                                 g.drow[:, ds(l.n * GROUP, GROUP)].broadcast_to([P, GROUP])).then_inc(drow_here[l.b], 16)
                    hold(sp, sp_turn, hid_summed[l.b], 2 * l.i)
                    sp.dma_start(edge[:, l.b, :], g.edge_t[:, ds(l.n * GROUP, GROUP)]).then_inc(edge_here[l.b], 16)
                    for u in range(QUAD):
                        hold(sp, sp_turn, scattered[l.b][u], 16 * l.i)
                    sp.dma_start(tgt_ix[:, l.b, :], g.at_node[:, ds(l.n * QUAD, QUAD)]).then_inc(tgt_here[l.b], 16)
            run_steps(sp, of, 4, 0, body)

        @block.gpsimd
        def _(pool):
            def body(s):
                if n := s.at(2):
                    hold(pool, pool_turn, dst_here[n.b], 16 * n.i + 16)
                    hold(pool, pool_turn, src_here[n.b], 16 * n.i + 16)
                    hold(pool, pool_turn, dst_turned[n.b], n.i)
                    hold(pool, pool_turn, src_turned[n.b], n.i)
                    for ix, rows, landed in ((dst_ix, at_dst, dst_rows), (src_ix, at_src, src_rows)):
                        for u in range(QUAD):
                            pool.indirect_dma_start(out=rows[:, n.b, u, :], out_offset=None, in_=hv,
                                                    in_offset=bass.IndirectOffsetOnAxis(ap=ix[:, n.b, u:u + 1], axis=0)
                                                    ).then_inc(landed[n.b][u], 16)
                if s.at(0):
                    hold(pool, pool_turn, tgt_here[s.b], 16 * s.i + 16)
                    for u in range(QUAD):
                        hold(pool, pool_turn, read_out[s.b], QUAD * s.i + u + 1)
                        pool.indirect_dma_start(out=g.seg, out_offset=bass.IndirectOffsetOnAxis(ap=tgt_ix[:, s.b, u:u + 1], axis=0),
                                                in_=res[:, s.b, u, :], in_offset=None,
                                                bounds_check=g.nodes - 1, oob_is_err=False).then_inc(scattered[s.b][u], 16)
            run_steps(pool, of, 2, 0, body)
            for b in range(2):
                for u in range(QUAD):
                    pool.wait_ge(scattered[b][u], 16 * (of // 2))

        @block.tensor
        def _(pe):
            def hid_product(n, k):
                m, part = divmod(k, 3)
                c = slice(m * P, (m + 1) * P)
                lhs, rhs = ((g.w["mw1"][:, t, 0, c], dstT[:, n.b, :]), (g.w["mw1"][:, t, 1, c], srcT[:, n.b, :]),
                            (g.w["mw1e"][:, t, c], edge[:, n.b, :]))[part]
                if part == 0:
                    if q := n.at(-1):
                        pe.wait_ge(hid_done[q.b], 2 * q.i + m + 1)
                ins = pe.matmul(ps_h[m][:, :], lhs, rhs, start=part == 0, stop=part == 2)
                if part == 2:
                    ins.then_inc(hid_summed[n.b], 1)

            def body(s):
                nxt, here = s.at(1), s.at(0)
                if nxt:
                    for u in range(QUAD):
                        pe.wait_ge(dst_rows[nxt.b][u], 16 * nxt.i + 16)
                    if here:
                        pe.wait_ge(dstT_done[s.b], s.i + 1)
                    turn_group(pe, ps_d, at_dst, nxt, g.ident, dst_turned)
                    for u in range(QUAD):
                        pe.wait_ge(src_rows[nxt.b][u], 16 * nxt.i + 16)
                    if here:
                        pe.wait_ge(srcT_done[s.b], s.i + 1)
                    turn_group(pe, ps_s, at_src, nxt, g.ident, src_turned)
                if here:
                    pe.wait_ge(hid_done[s.b], 2 * s.i + 2)
                    if q := s.at(-1):
                        pe.wait_ge(msg_done[q.b], 2 * q.i + 2)
                    for u in range(QUAD):
                        c = slice(u * P, (u + 1) * P)
                        pe.matmul(ps_msg[:, u, :], hidT[:, s.b, 0, c], g.w["mw2"][:, t, 0, :], start=True, stop=False)
                        last = pe.matmul(ps_msg[:, u, :], hidT[:, s.b, 1, c], g.w["mw2"][:, t, 1, :], start=False, stop=True)
                        if u % 2:
                            last.then_inc(msg_summed[s.b], 1)
                if nxt:
                    pe.wait_ge(dstT_done[nxt.b], nxt.i + 1)
                    pe.wait_ge(srcT_done[nxt.b], nxt.i + 1)
                    pe.wait_ge(edge_here[nxt.b], 16 * nxt.i + 16)
                    hid_product(nxt, 0)
                for u in range(QUAD):
                    if nxt:
                        hid_product(nxt, u + 1)
                    if here:
                        if u == 0:
                            pe.wait_ge(read_out[1 - s.b], QUAD * (s.i + s.b) - (1 if s.at(-1) else 0))
                        pe.wait_ge(same_done[s.b], QUAD * s.i + u + 1)
                        pe.wait_ge(carried[s.b], QUAD * s.i + u + 1)
                        pe.matmul(sums[u], same[:, s.b, u, :], msg[:, s.b, u, :], start=True, stop=True).then_inc(summed[s.b], 1)
                if nxt:
                    hid_product(nxt, 5)
            run_steps(pe, of, 1, 0, body)

        @block.scalar
        def _(act):
            act.wait_ge(start, 1)

            def relu(n, m):
                act.wait_ge(hid_summed[n.b], 2 * n.i + m + 1)
                act.wait_ge(msg_summed[n.b], 2 * n.i)
                c = g.mlp_cols[t] + m
                act.activation(hidT[:, n.b, m, :], ps_h[m][:, :], ACT.Relu, bias=g.col[:, c:c + 1]).then_inc(hid_done[n.b], 1)

            def read(s, u):
                act.wait_ge(summed[s.b], QUAD * s.i + u + 1)
                act.wait_ge(scattered[s.b][u], 16 * s.i)
                act.copy(res[:, s.b, u, :], sums[u]).then_inc(read_out[s.b], 1)

            def body(s):
                nxt, here, before = s.at(1), s.at(0), s.at(-1)
                if nxt:
                    act.wait_ge(src_turned[nxt.b], nxt.i + 1)
                    act.wait_ge(hid_summed[nxt.b], 2 * nxt.i)
                    act.copy(srcT[:, nxt.b, :], ps_s[:, :]).then_inc(srcT_done[nxt.b], 1)
                for u in range(QUAD):
                    if here:
                        if u % 2 == 0:
                            act.wait_ge(msg_done[s.b], 2 * s.i + u // 2 + 1)
                        if u:
                            act.wait_ge(summed[s.b], QUAD * s.i + u)
                        elif before:
                            act.wait_ge(summed[before.b], QUAD * before.i + QUAD)
                        act.copy(msg[0:1, s.b, u, :], sums[(u - 1) % QUAD][LAST_SLOT:LAST_SLOT + 1, :]).then_inc(carried[s.b], 1)
                    if u and here:
                        read(s, u - 1)
                    elif u == 0 and before:
                        read(before, QUAD - 1)
                    if nxt and u == 1:
                        relu(nxt, 0)
                if nxt:
                    relu(nxt, 1)
            run_steps(act, of, 1, 1, body)

        @block.vector
        def _(dve):
            dve.memset(sums[QUAD - 1], 0.0).then_inc(start, 1)

            def body(s):
                nxt, here = s.at(1), s.at(0)
                if nxt:
                    dve.wait_ge(dst_turned[nxt.b], nxt.i + 1)
                    dve.wait_ge(hid_summed[nxt.b], 2 * nxt.i)
                    dve.tensor_copy(dstT[:, nxt.b, :], ps_d[:, :]).then_inc(dstT_done[nxt.b], 1)
                if here:
                    dve.wait_ge(summed[s.b], QUAD * s.i)
                    for pair in range(2):
                        u = slice(2 * pair, 2 * pair + 2)
                        dve.wait_ge(msg_summed[s.b], 2 * s.i + pair + 1)
                        dve.tensor_tensor(msg[:, s.b, u, :], ps_msg[:, u, :],
                                          g.w["mb2"][:, t, :].unsqueeze(1).broadcast_to([P, 2, wide]), ALU.add).then_inc(msg_done[s.b], 1)
                if nxt:
                    dve.wait_ge(drow_here[nxt.b], 16 * nxt.i + 16)
                    dve.wait_ge(summed[nxt.b], QUAD * nxt.i)
                    for u in range(QUAD):
                        dve.tensor_scalar(same[:, nxt.b, u, :], drow[:, nxt.b, u, :], g.dcol[:, ds(nxt.n * QUAD + u, 1)], None,
                                          ALU.is_equal).then_inc(same_done[nxt.b], 1)
            run_steps(dve, of, 1, 0, body)


def gated_update(nc, g, t, hv, into, last_round):
    with Phase(nc, f"gru{t}") as ph:
        v_in, a_in = ph.sb("v_in", [P, 2, QUAD, P]), ph.sb("a_in", [P, 2, QUAD, 2 * P])
        vT, aT = ph.sb("vT", [P, 2, GROUP]), ph.sb("aT", [P, 2, 2, GROUP])
        reset, update, cand_h, cand_s, cand, diff, part, newT = (ph.sb(n, [P, 2, GROUP]) for n in (
            "reset", "update", "cand_h", "cand_s", "cand", "diff", "part", "newT"))
        x_in, value, new = (ph.sb(n, [P, 2, QUAD, P]) for n in ("x_in", "value", "new"))
        minus_half = ph.sb("minus_half", [P, 2 * QUAD])
        ps_v, ps_a, ps_out = ph.ps("ps_v"), [ph.ps(f"ps_a{k}") for k in range(2)], ph.ps("ps_out")
        ps_r, ps_z, ps_h, ps_x = (ph.ps(n) for n in ("ps_r", "ps_z", "ps_h", "ps_x"))
        norm = Norm(ph, "norm")
        v_here, a_here, x_here, stored = (ph.sems(n) for n in ("v_here", "a_here", "x_here", "stored"))
        (v_turned, a_turned, vT_done, aT_done, r_summed, z_summed, h_summed, x_summed, reset_done, update_done, cand_h_done,
         cand_s_done, cand_done, diff_done, part_done, newT_done, new_turned, new_done, value_done) = (ph.sems(n) for n in (
             "v_turned", "a_turned", "vT_done", "aT_done", "r_summed", "z_summed", "h_summed", "x_summed", "reset_done",
             "update_done", "cand_h_done", "cand_s_done", "cand_done", "diff_done", "part_done", "newT_done", "new_turned",
             "new_done", "value_done"))
        sp_turn, consts = ph.sem("sp_turn"), ph.sem("consts")
        block = ph.block()
        of = g.groups
        lag = 3 if last_round else 2

        @block.sync
        def _(sp):
            def body(s):
                if l := s.at(2):
                    hold(sp, sp_turn, v_turned[l.b], l.i)
                    sp.dma_start(v_in[:, l.b, :, :], group_rows(hv, l.n)).then_inc(v_here[l.b], 16)
                    hold(sp, sp_turn, a_turned[l.b], 2 * l.i)
                    sp.dma_start(a_in[:, l.b, :, :], group_rows(g.seg, l.n, 2 * P)).then_inc(a_here[l.b], 16)
                if last_round and s.at(0):
                    hold(sp, sp_turn, value_done[s.b], s.i)
                    sp.dma_start(x_in[:, s.b, :, :], group_rows(g.x3, s.n)).then_inc(x_here[s.b], 16)
                if r := s.at(-lag):
                    hold(sp, sp_turn, new_done[r.b], r.i + 1)
                    sp.dma_start(group_rows(into, r.n), new[:, r.b, :, :]).then_inc(stored[r.b], 16)
            run_steps(sp, of, 2, lag, body)
            for b in range(2):
                sp.wait_ge(stored[b], 16 * (of // 2))

        @block.tensor
        def _(pe):
            wih, whh = g.w["wih"], g.w["whh"]

            def body(s):
                if n := s.at(1):
                    q = n.at(-1)
                    pe.wait_ge(v_here[n.b], 16 * n.i + 16)
                    if q:
                        pe.wait_ge(vT_done[q.b], q.i + 1)
                    turn_group(pe, ps_v, v_in, n, g.ident, v_turned)
                    pe.wait_ge(a_here[n.b], 16 * n.i + 16)
                    if q:
                        pe.wait_ge(aT_done[q.b], 2 * q.i + 2)
                    for k in range(2):
                        for j in range(QUAD):
                            turned = pe.transpose(ps_a[k][:, j * P:(j + 1) * P], a_in[:, n.b, j, k * P:(k + 1) * P], g.ident[:, :])
                        turned.then_inc(a_turned[n.b], 1)
                if s.at(0):
                    pe.wait_ge(vT_done[s.b], s.i + 1)
                    pe.wait_ge(aT_done[s.b], 2 * s.i + 2)
                    q = s.at(-1)
                    for bank, gate, free, done in ((ps_r, 0, reset_done, r_summed), (ps_z, 1, update_done, z_summed)):
                        c = slice(gate * P, (gate + 1) * P)
                        if q:
                            pe.wait_ge(free[q.b], q.i + 1)
                        pe.matmul(bank[:, :], whh[:, t, c], vT[:, s.b, :], start=True, stop=False)
                        pe.matmul(bank[:, :], wih[:, t, 0, c], aT[:, s.b, 0, :], start=False, stop=False)
                        pe.matmul(bank[:, :], wih[:, t, 1, c], aT[:, s.b, 1, :], start=False, stop=True).then_inc(done[s.b], 1)
                        if gate == 0:
                            if q:
                                pe.wait_ge(cand_h_done[q.b], q.i + 1)
                            pe.matmul(ps_h[:, :], whh[:, t, 2 * P:], vT[:, s.b, :], start=True, stop=True).then_inc(h_summed[s.b], 1)
                    if q:
                        pe.wait_ge(cand_s_done[q.b], q.i + 1)
                    pe.matmul(ps_x[:, :], wih[:, t, 0, 2 * P:], aT[:, s.b, 0, :], start=True, stop=False)
                    pe.matmul(ps_x[:, :], wih[:, t, 1, 2 * P:], aT[:, s.b, 1, :], start=False, stop=True).then_inc(x_summed[s.b], 1)
                if r := s.at(-1):
                    pe.wait_ge(newT_done[r.b], r.i + 1)
                    if q := r.at(-1):
                        pe.wait_ge((value_done if last_round else new_done)[q.b], q.i + 1)
                    for j in range(QUAD):
                        turned = pe.transpose(ps_out[:, j * P:(j + 1) * P], newT[:, r.b, j * P:(j + 1) * P], g.ident[:, :])
                    turned.then_inc(new_turned[r.b], 1)
            run_steps(pe, of, 1, 1, body)

        @block.scalar
        def _(act):
            bias = g.gate_bias

            def body(s):
                if n := s.at(1):
                    act.wait_ge(v_turned[n.b], n.i + 1)
                    act.wait_ge(diff_done[n.b], n.i)
                    act.copy(vT[:, n.b, :], ps_v[:, :]).then_inc(vT_done[n.b], 1)
                if s.at(0):
                    act.wait_ge(r_summed[s.b], s.i + 1)
                    act.wait_ge(cand_h_done[s.b], s.i)
                    act.activation(reset[:, s.b, :], ps_r[:, :], ACT.Sigmoid, bias=bias[:, t, 0:1]).then_inc(reset_done[s.b], 1)
                    act.wait_ge(z_summed[s.b], s.i + 1)
                    act.wait_ge(part_done[s.b], s.i)
                    act.activation(update[:, s.b, :], ps_z[:, :], ACT.Sigmoid, bias=bias[:, t, 1:2]).then_inc(update_done[s.b], 1)
                    act.wait_ge(cand_s_done[s.b], s.i + 1)
                    act.wait_ge(newT_done[s.b], s.i)
                    act.activation(cand[:, s.b, :], cand_s[:, s.b, :], ACT.Tanh, bias=bias[:, t, 2:3]).then_inc(cand_done[s.b], 1)
                if not last_round:
                    if r := s.at(-1):
                        act.wait_ge(new_turned[r.b], r.i + 1)
                        act.wait_ge(stored[r.b], 16 * r.i)
                        act.copy(flat(new, r.b), ps_out[:, :]).then_inc(new_done[r.b], 1)
            run_steps(act, of, 1, 1, body)

        @block.gpsimd
        def _(pool):
            power_constants(ph, pool, minus_half, consts)

            def body(s):
                if s.at(0):
                    pool.wait_ge(cand_done[s.b], s.i + 1)
                    pool.wait_ge(part_done[s.b], s.i)
                    pool.tensor_tensor(diff[:, s.b, :], vT[:, s.b, :], cand[:, s.b, :], ALU.subtract).then_inc(diff_done[s.b], 1)
                    pool.wait_ge(diff_done[s.b], s.i + 1)
                    pool.wait_ge(newT_done[s.b], s.i)
                    pool.tensor_tensor(part[:, s.b, :], diff[:, s.b, :], update[:, s.b, :], ALU.mult).then_inc(part_done[s.b], 1)
                if last_round:
                    if r := s.at(-1):
                        norm.deviation(pool, r, minus_half)
            run_steps(pool, of, 0, 1, body)

        @block.vector
        def _(dve):
            bias = g.gate_bias

            def body(s):
                if n := s.at(1):
                    for k in range(2):
                        dve.wait_ge(a_turned[n.b], 2 * n.i + k + 1)
                        dve.wait_ge(x_summed[n.b], n.i)
                        dve.tensor_copy(aT[:, n.b, k, :], ps_a[k][:, :]).then_inc(aT_done[n.b], 1)
                if s.at(0):
                    dve.wait_ge(h_summed[s.b], s.i + 1)
                    dve.wait_ge(reset_done[s.b], s.i + 1)
                    dve.scalar_tensor_tensor(cand_h[:, s.b, :], ps_h[:, :], bias[:, t, 3:4], reset[:, s.b, :],
                                             ALU.add, ALU.mult).then_inc(cand_h_done[s.b], 1)
                    dve.wait_ge(x_summed[s.b], s.i + 1)
                    dve.wait_ge(cand_h_done[s.b], s.i + 1)
                    dve.wait_ge(cand_done[s.b], s.i)
                    dve.tensor_tensor(cand_s[:, s.b, :], ps_x[:, :], cand_h[:, s.b, :], ALU.add).then_inc(cand_s_done[s.b], 1)
                if last_round:
                    if r := s.at(-1):
                        dve.wait_ge(new_turned[r.b], r.i + 1)
                        dve.wait_ge(x_here[r.b], 16 * r.i + 16)
                        dve.wait_ge(new_done[r.b], r.i)
                        dve.tensor_tensor(flat(value, r.b), ps_out[:, :], flat(x_in, r.b), ALU.add).then_inc(value_done[r.b], 1)
                    if r := s.at(-2):
                        dve.wait_ge(stored[r.b], 16 * r.i)
                        norm.apply(dve, r, new, value, new_done)
                    if r := s.at(-1):
                        dve.wait_ge(value_done[r.b], r.i + 1)
                        norm.moments_of(dve, r, value)
                if s.at(0):
                    dve.wait_ge(part_done[s.b], s.i + 1)
                    dve.wait_ge(new_turned[s.b], s.i)
                    dve.tensor_tensor(newT[:, s.b, :], part[:, s.b, :], cand[:, s.b, :], ALU.add).then_inc(newT_done[s.b], 1)
            run_steps(dve, of, 1, 2, body)


class Graph:
    pass


def build(nc, d, out, nodes, upto=99):
    g = Graph()
    g.nodes = nodes
    g.groups = d["x"].shape[0] // GROUP
    g.ntp = d["srcw"].shape[1]
    g.quads = g.ntp // QUAD - 2
    g.rounds = d["mlp_w1"].shape[0]
    np_ = d["x"].shape[0]
    g.x, g.drow, g.order, g.edge, g.edge_t, g.out = d["x"], d["drow"], d["order"], d["edge"], d["edge_t"], out
    with ExitStack() as stack:
        def sb(name, shape, dt=F32):
            return stack.enter_context(nc.sbuf_tensor(name, list(shape), dt))

        def table(name, width):
            return nc.dram_tensor(name, (np_, width), F32).ap()

        g.seg, g.gat = table("seg", 2 * P), table("gat", AUG)
        g.h1, g.x1, g.th, g.ta = table("h1", P), table("x1", P), table("th", P), table("ta", 2 * HEADS)
        g.x2, g.x3, g.x4 = table("x2", P), table("x3", P), table("x4", P)
        g.ident = sb("ident", [P, P])
        g.srcw, g.dstw = sb("srcw_s", [P, g.ntp], I32), sb("dst_rows", [P, g.ntp], I32)
        g.at_node, g.at_left, g.at_right = (sb(n, [P, g.ntp], I32) for n in ("at_node", "at_left", "at_right"))
        g.dcol = sb("dcol", [P, g.ntp])
        g.w = {n: sb(f"w_{n}", [P, P]) for n in ("W1lT", "W1rT", "W2lT", "W2rT", "linT", "projT", "W2", "W3")}
        g.w["attT"] = sb("w_attT", [P, 2 * HEADS])
        g.w["W1"] = sb("w_W1", [P, 2, P])
        g.w["mw1"] = sb("w_mw1", [P, g.rounds, 2, 2 * P])
        g.w["mw1e"] = sb("w_mw1e", [d["mlp_w1"].shape[1] - 2 * P, g.rounds, 2 * P])
        g.w["mw2"] = sb("w_mw2", [P, g.rounds, 2, 2 * P])
        g.w["mb2"] = sb("w_mb2", [P, g.rounds, 2 * P])
        g.w["wih"] = sb("w_wih", [P, g.rounds, 2, 3 * P])
        g.w["whh"] = sb("w_whh", [P, g.rounds, 3 * P])
        g.rows = ("b1l", "b2l", "proj_b", "ln1_gamma", "ln1_beta", "b3", "ln2_gamma", "ln2_beta")
        g.row = {n: sb(f"row_{n}", [P, GROUP]) for n in g.rows}
        g.ncols = d["cols"].shape[1]
        g.col = sb("cols_s", [P, g.ncols])
        g.mlp_cols = [3 + 8 * r for r in range(g.rounds)]
        g.gate_cols = [5 + 8 * r for r in range(g.rounds)]
        g.gate_bias = sb("gate_bias", [P, g.rounds, 4])
        halves = g.seg.rearrange("n (c d) -> (n c) d", d=P)
        prepare(nc, g, d)
        if upto >= 1:
            edge_sums(nc, g, "sage1", g.at_left, halves, P, gather=g.x, mean=True)
        if upto >= 2:
            sage_hidden(nc, g)
        if upto >= 3:
            edge_sums(nc, g, "sage2", g.at_left, halves, P, gather=g.h1, mean=True)
        if upto >= 4:
            sage_out(nc, g)
        with ExitStack() as inner:
            slots = g.ntp * HEADS
            g.score, g.weight, g.peak = (inner.enter_context(nc.sbuf_tensor(n, [P, slots], F32)) for n in ("score", "weight", "peak"))
            if upto >= 5:
                edge_scores(nc, g)
                edge_softmax(nc, g)
            if upto >= 6:
                edge_sums(nc, g, "gat", g.at_node, g.gat, P, gather=g.th, weights=(g.weight, g.peak))
        if upto >= 7:
            edge_sums(nc, g, "edges", g.at_right, halves, P, linear=g.edge)
            gat_out(nc, g)
        if upto >= 8:
            edge_mlp(nc, g)
        if upto >= 9:
            messages(nc, g, 0, g.x3)
        if upto >= 10:
            gated_update(nc, g, 0, g.x3, g.x4, False)
        if upto >= 11:
            messages(nc, g, 1, g.x4)
            gated_update(nc, g, 1, g.x4, out, True)


def arrange(inputs):
    import numpy as np
    a = {k: np.asarray(v) for k, v in inputs.items()}
    nodes, edges = a["x"].shape[0], a["src"].shape[0]
    tiles = -(-edges // EDGES_PER_TILE)
    quads = 2 * -(-tiles // (2 * QUAD))
    ntp = QUAD * (quads + 2)
    place = np.arange(P)
    place[[LAST_SLOT, P - 1]] = place[[P - 1, LAST_SLOT]]
    inorder = np.arange(ntp)[:, None] * EDGES_PER_TILE + np.arange(P)[None, :]
    slots = inorder[:, place]

    def padded(v, fill):
        p = np.full((inorder.max() + 2,) + v.shape[1:], fill, v.dtype)
        p[1:1 + edges] = v
        return p
    src, dst = padded(a["src"], 0), padded(a["dst"], -1)
    d = {}
    rows = -(-nodes // (2 * GROUP)) * 2 * GROUP
    d["x"] = np.zeros((rows, P), np.float32)
    d["x"][:nodes] = a["x"]
    d["srcw"], d["dstw"] = src[slots].T, dst[slots].T
    nxt = dst[slots + 1].T.copy()
    nxt[0] = d["dstw"][0]
    d["nxtw"] = nxt
    d["drow"] = dst[slots].reshape(1, -1)
    d["order"] = dst[inorder[:quads * QUAD]].reshape(CHUNKS, -1)
    d["edge"] = padded(a["edge_attr_128"], 0)[slots].reshape(-1, P)
    d["edge_t"] = padded(a["edge_attr_26"], 0)[slots].reshape(ntp * P, -1).T
    for k, n in (("W1lT", "L0_gnn_W1l"), ("W1rT", "L0_gnn_W1r"), ("W2lT", "L0_gnn_W2l"), ("W2rT", "L0_gnn_W2r"),
                 ("linT", "L1_gnn_lin_w"), ("projT", "L1_gnn_proj_w")):
        d[k] = a[n].T
    d["lin_w"] = a["L1_gnn_lin_w"]
    d["W1"], d["W2"], d["W3"] = a["L2_gnn_W1"], a["L2_gnn_W2"], a["L2_gnn_W3"]
    d["att_src"], d["att_dst"] = a["L1_gnn_att_src"].reshape(P, 1), a["L1_gnn_att_dst"].reshape(P, 1)
    d["head_of"] = np.repeat(np.eye(HEADS, dtype=np.float32), HEAD_DIM, axis=0)
    d["ident"] = np.eye(P, dtype=np.float32)
    for k, n in (("b1l", "L0_gnn_b1l"), ("b2l", "L0_gnn_b2l"), ("proj_b", "L1_gnn_proj_b"),
                 ("ln1_gamma", "L1_gnn_ln_gamma"), ("ln1_beta", "L1_gnn_ln_beta"), ("b3", "L2_gnn_b3"),
                 ("ln2_gamma", "L2_gnn_gamma"), ("ln2_beta", "L2_gnn_beta")):
        d[k] = a[n].reshape(1, P)
    cols = [a["L1_gnn_gat_bias"], a["L2_gnn_b1"], a["L2_gnn_b2"]]
    for r in range(a["L3_gnn_mlp_w1"].shape[0]):
        cols += [*a["L3_gnn_mlp_b1"][r].reshape(2, P), *a["L3_gnn_gru_bih"][r].reshape(3, P),
                 *a["L3_gnn_gru_bhh"][r].reshape(3, P)]
    d["cols"] = np.stack(cols, axis=1)
    d["mlp_w1"], d["mlp_w2"], d["mlp_b2"] = a["L3_gnn_mlp_w1"], a["L3_gnn_mlp_w2"], a["L3_gnn_mlp_b2"]
    d["wihT"], d["whhT"] = a["L3_gnn_gru_wih"].transpose(0, 2, 1), a["L3_gnn_gru_whh"].transpose(0, 2, 1)
    return {k: np.ascontiguousarray(v) for k, v in d.items()}, nodes


def kernel(**inputs):
    import concourse.bacc as bacc
    from concourse.bass_utils import run_bass_kernel_spmd

    arrays, nodes = arrange(inputs)
    nc = bacc.Bacc("TRN2", target_bir_lowering=False, num_devices=1)
    d = {k: nc.dram_tensor(f"in_{k}", v.shape, mybir.dt.from_np(v.dtype), kind="ExternalInput").ap()
         for k, v in arrays.items()}
    out = nc.dram_tensor("out", arrays["x"].shape, F32, kind="ExternalOutput").ap()
    build(nc, d, out, nodes)
    r = run_bass_kernel_spmd(nc, [{f"in_{k}": v for k, v in arrays.items()}], core_ids=[0])
    return r.results[0]["out"][:nodes]
```

```python
from contextlib import ExitStack

import concourse.bass as bass
from concourse import mybir
from concourse.bass import ds

F32 = mybir.dt.float32
I32 = mybir.dt.int32
ALU = mybir.AluOpType
ACT = mybir.ActivationFunctionType

P = 128
EDGES_PER_TILE = P - 1
LAST_SLOT = 32
QUAD = 4
GROUP = QUAD * P
HEADS, HEAD_DIM = 8, 16
CHUNKS = 8
EPS = 1e-5
SLOPE = 0.2
SKIP = 1.0e6
LOW = -1.0e30
AUG = 144


class Step:

    def __init__(self, i, b, of):
        self.i, self.b, self.of = i, b, of

    def at(self, k):
        i, b = self.i + (self.b + k) // 2, (self.b + k) % 2
        if isinstance(i, int) and not 0 <= 2 * i + b < self.of:
            return None
        return Step(i, b, self.of)

    @property
    def n(self):
        return 2 * self.i + self.b


def run_steps(eng, of, before, after, body):
    lo = (after + 1) // 2 + 1
    hi = (of - before) // 2
    for n in range(-before, 2 * lo):
        body(Step(n // 2, n % 2, of))
    with eng.Fori(lo, hi) as i:
        body(Step(i, 0, of))
        body(Step(i, 1, of))
    for n in range(2 * hi, of + after):
        body(Step(n // 2, n % 2, of))


class Phase:

    def __init__(self, nc, name):
        self.nc, self.name, self.stack, self.held = nc, name, ExitStack(), []

    def __enter__(self):
        return self

    def __exit__(self, *e):
        self.stack.__exit__(*e)
        self.nc.clear_and_free_semaphores(self.held)
        self.nc.all_engine_barrier()

    def sb(self, name, shape, dt=F32):
        return self.stack.enter_context(self.nc.sbuf_tensor(f"{self.name}_{name}", list(shape), dt))

    def ps(self, name, shape=(P, 512)):
        return self.stack.enter_context(self.nc.psum_tensor(f"{self.name}_{name}", list(shape), F32))

    def sem(self, name):
        self.held.append(self.nc.alloc_semaphore(f"{self.name}_{name}"))
        return self.held[-1]

    def sems(self, name, n=2):
        return [self.sem(f"{name}{k}") for k in range(n)]

    def block(self):
        return self.stack.enter_context(self.nc.Block())


def group_rows(table, n, width=P, at=0):
    rows = table[ds(n * GROUP, GROUP), :].rearrange("(p j) d -> p j d", j=QUAD)
    return rows if width is None else rows[:, :, at:at + width]


def hold(eng, turn, sem, value):
    eng.wait_ge(sem, value)
    eng.sem_inc(turn, 1)


def clear_table(eng, table, zeros, cleared):
    rows, width = table.shape
    per = rows // P
    flat = table.rearrange("(p a) d -> p (a d)", p=P)
    starts = range(0, per * width, zeros.shape[1])
    for a in starts:
        z = min(a + zeros.shape[1], per * width)
        eng.dma_start(flat[:, a:z], zeros[:, 0:z - a]).then_inc(cleared, 16)
    return len(starts)


def prepare(nc, g, d):
    with Phase(nc, "prep") as ph:
        loaded = ph.sem("loaded")
        zeros = ph.sb("zeros", [P, 4096])
        zeroed = ph.sem("zeroed")
        cleared = ph.sem("cleared")
        dstw, nxtw = ph.sb("dstw", [P, g.ntp], I32), ph.sb("nxtw", [P, g.ntp], I32)
        skip = ph.sb("skip", [P, g.ntp])
        target = ph.sb("target", [P, g.ntp])
        att = ph.sb("att", [P, 2])
        head_of = ph.sb("head_of", [P, HEADS])
        att_mat = ph.sb("att_mat", [P, 2 * HEADS])
        lin = ph.sb("lin", [P, P])
        psum = ph.ps("psum")
        index_step = ph.sem("index_step")
        att_done, prod_done = ph.sem("att_done"), ph.sem("prod_done")
        biases = ph.sb("biases", [P, g.rounds, 6])
        block = ph.block()

        loads = [(dstw[:, :], d["dstw"]), (nxtw[:, :], d["nxtw"]), (g.srcw[:, :], d["srcw"]),
                 (att[:, 0:1], d["att_src"]), (att[:, 1:2], d["att_dst"]),
                 (head_of[:, :], d["head_of"]), (lin[:, :], d["lin_w"]), (g.ident[:, :], d["ident"])]
        for name in ("W1lT", "W1rT", "W2lT", "W2rT", "projT", "W2", "W3"):
            loads.append((g.w[name][:, :], d[name]))
        loads.append((g.w["linT"][:, :], d["linT"]))
        loads.append((g.w["W1"][:, :, :], d["W1"].rearrange("(c p) n -> p c n", p=P)))
        for r in range(g.rounds):
            loads.append((g.w["mw1"][:, r, :, :], d["mlp_w1"][r, 0:2 * P, :].rearrange("(c p) n -> p c n", p=P)))
            loads.append((g.w["mw1e"][:, r, :], d["mlp_w1"][r, 2 * P:, :]))
            loads.append((g.w["mw2"][:, r, :, :], d["mlp_w2"][r].rearrange("(c p) n -> p c n", p=P)))
            loads.append((g.w["wih"][:, r, :, :], d["wihT"][r].rearrange("(c p) n -> p c n", p=P)))
            loads.append((g.w["whh"][:, r, :], d["whhT"][r]))
            loads.append((g.w["mb2"][:, r, :], d["mlp_b2"][r:r + 1, :].broadcast_to([P, 2 * P])))
        for name in g.rows:
            for j in range(QUAD):
                loads.append((g.row[name][:, j * P:(j + 1) * P], d[name].broadcast_to([P, P])))
        loads.append((g.col[:, 0:g.ncols], d["cols"]))

        @block.sync
        def _(sp):
            for dst, src in loads:
                sp.dma_start(dst, src).then_inc(loaded, 16)
            sp.wait_ge(zeroed, 1)
            n = 0
            n = clear_table(sp, g.seg, zeros, cleared)
            sp.wait_ge(cleared, 16 * n)
            sp.wait_ge(loaded, 16 * len(loads))

        @block.vector
        def _(dve):
            dve.memset(zeros[:, :], 0.0).then_inc(zeroed, 1)
            dve.memset(g.ones[:, :], 1.0)
            dve.wait_ge(loaded, 16 * len(loads))
            dve.tensor_copy(g.dcol[:, :], dstw[:, :]).then_inc(index_step, 1)
            dve.tensor_tensor(skip[:, :], dstw[:, :], nxtw[:, :], ALU.is_equal).then_inc(index_step, 1)
            dve.wait_ge(index_step, 2)
            dve.scalar_tensor_tensor(target[:, :], skip[:, :], SKIP, g.dcol[:, :], ALU.mult, ALU.add).then_inc(index_step, 1)
            dve.wait_ge(index_step, 3)
            dve.tensor_copy(g.at_node[:, :], target[:, :])
            dve.tensor_scalar(g.at_left[:, :], target[:, :], 2.0, None, ALU.mult)
            dve.tensor_scalar(g.dstw[:, :], g.dcol[:, :], 0.0, None, ALU.max)
            dve.tensor_scalar(att_mat[:, 0:HEADS], head_of[:, :], att[:, 0:1], None, ALU.mult)
            dve.tensor_scalar(att_mat[:, HEADS:], head_of[:, :], att[:, 1:2], None, ALU.mult).then_inc(att_done, 1)
            for r in range(g.rounds):
                c = g.gate_cols[r]
                dve.tensor_tensor(g.gate_bias[:, r, 0:2], g.col[:, c:c + 2], g.col[:, c + 3:c + 5], ALU.add)
                dve.tensor_copy(g.gate_bias[:, r, 2:3], g.col[:, c + 2:c + 3])
                dve.tensor_copy(g.gate_bias[:, r, 3:4], g.col[:, c + 5:c + 6])
            dve.wait_ge(prod_done, 1)
            dve.tensor_copy(g.w["attT"][:, :], psum[:, 0:2 * HEADS])

        @block.tensor
        def _(pe):
            pe.wait_ge(att_done, 1)
            pe.matmul(psum[:, 0:2 * HEADS], lin[:, :], att_mat[:, :], start=True, stop=True).then_inc(prod_done, 1)


def edge_sums(nc, g, name, target_index, target, gather, linear=None, mean=False, weights=None, clear=None):
    width = 2 * P if linear is not None else P
    cols = width + (1 if mean else 0) + (HEADS if weights else 0)
    out_cols = AUG if weights else width
    bound = g.nodes * (target.shape[0] // g.x.shape[0])
    with Phase(nc, name) as ph:
        src_ix, tgt_ix = ph.sb("src_ix", [P, 2, QUAD], I32), ph.sb("tgt_ix", [P, 2, QUAD], I32)
        drow = ph.sb("drow", [P, 2, QUAD, P], I32)
        msg = ph.sb("msg", [P, 2, QUAD, cols])
        raw = ph.sb("raw", [P, 2, QUAD, P]) if weights else msg
        same = ph.sb("same", [P, 2, QUAD, P])
        res = ph.sb("res", [P, 2, QUAD, out_cols])
        share = ph.sb("share", [P, 2, QUAD])
        count = ph.sb("count", [P, 2, QUAD])
        plain = ph.sb("plain", [P, 2, QUAD, cols if mean else 1])
        banks = ph.ps("sums", [P, QUAD, 2, 512 if cols > 256 else 256])
        sums = [banks[:, :, b, :] for b in range(2)]
        src_here, tgt_here, drow_here = ph.sems("src_here"), ph.sems("tgt_here"), ph.sems("drow_here")
        edge_here = ph.sems("edge_here")
        zeros = ph.sb("zeros", [P, 4096]) if clear is not None else None
        zeroed, cleared = ph.sem("zeroed"), ph.sem("cleared")
        rows_here = [ph.sems(f"rows_here{b}_", QUAD) for b in range(2)]
        scattered = [ph.sems(f"scattered{b}_", QUAD) for b in range(2)]
        same_done, msg_done, carried = ph.sems("same_done"), ph.sems("msg_done"), ph.sems("carried")
        summed, share_done, res_done = ph.sems("summed"), ph.sems("share_done"), ph.sems("res_done")
        read_out, maxima_done = ph.sems("read_out"), ph.sems("maxima_done")
        start = ph.sem("start")
        pool_turn, sp_turn = ph.sem("pool_turn"), ph.sem("sp_turn")
        block = ph.block()
        of = g.quads

        def load_quad(sp, s, which):
            if which == "src":
                sp.dma_start(src_ix[:, s.b, :], g.srcw[:, ds(s.n * QUAD, QUAD)]).then_inc(src_here[s.b], 16)
            if which == "tgt":
                sp.dma_start(tgt_ix[:, s.b, :], target_index[:, ds(s.n * QUAD, QUAD)]).then_inc(tgt_here[s.b], 16)
            if which == "drow":
                sp.dma_start(drow[:, s.b, :, :].rearrange("p t e -> p (t e)"),
                             g.drow[:, ds(s.n * GROUP, GROUP)].broadcast_to([P, GROUP])).then_inc(drow_here[s.b], 16)
            if which == "edge" and linear is not None:
                sp.dma_start(msg[:, s.b, :, P:2 * P], linear[ds(s.n * GROUP, GROUP), :].rearrange("(u p) d -> p u d", p=P)
                             ).then_inc(edge_here[s.b], 16)

        @block.sync
        def _(sp):
            def body(s):
                if n := s.at(3):
                    for u in range(QUAD):
                        hold(sp, sp_turn, rows_here[n.b][u], 16 * n.i)
                    load_quad(sp, n, "src")
                if n := s.at(2):
                    hold(sp, sp_turn, same_done[n.b], QUAD * n.i)
                    load_quad(sp, n, "drow")
                    if linear is not None:
                        hold(sp, sp_turn, summed[n.b], QUAD * n.i)
                        load_quad(sp, n, "edge")
                if n := s.at(1):
                    for u in range(QUAD):
                        hold(sp, sp_turn, scattered[n.b][u], 16 * n.i)
                    load_quad(sp, n, "tgt")
            run_steps(sp, of, 3, 0, body)

        @block.gpsimd
        def _(pool):
            def fetch(s):
                hold(pool, pool_turn, src_here[s.b], 16 * s.i + 16)

            def fetch_tile(s, u):
                pool.indirect_dma_start(out=raw[:, s.b, u, 0:P], out_offset=None, in_=gather,
                                        in_offset=bass.IndirectOffsetOnAxis(ap=src_ix[:, s.b, u:u + 1], axis=0)
                                        ).then_inc(rows_here[s.b][u], 16)

            def body(s):
                if n := s.at(1):
                    fetch(n)
                    hold(pool, pool_turn, summed[n.b], QUAD * n.i)
                    for u in range(QUAD):
                        fetch_tile(n, u)
                if r := s.at(-1):
                    hold(pool, pool_turn, tgt_here[r.b], 16 * r.i + 16)
                    for u in range(QUAD):
                        hold(pool, pool_turn, (res_done if mean else read_out)[r.b], QUAD * r.i + u + 1)
                        if weights:
                            hold(pool, pool_turn, maxima_done[r.b], QUAD * r.i + u + 1)
                        pool.indirect_dma_start(out=target, out_offset=bass.IndirectOffsetOnAxis(ap=tgt_ix[:, r.b, u:u + 1], axis=0),
                                                in_=res[:, r.b, u, :], in_offset=None,
                                                bounds_check=bound - 1, oob_is_err=False).then_inc(scattered[r.b][u], 16)
            run_steps(pool, of, 1, 1, body)
            for b in range(2):
                for u in range(QUAD):
                    pool.wait_ge(scattered[b][u], 16 * (of // 2))

        @block.scalar
        def _(act):
            act.wait_ge(start, 1)
            if clear is not None:
                act.wait_ge(zeroed, 1)
                transfers = clear_table(act, clear, zeros, cleared)

            def read(s, u):
                act.wait_ge(summed[s.b], QUAD * s.i + u + 1)
                if mean:
                    act.wait_ge(res_done[s.b], QUAD * s.i)
                    act.copy(plain[:, s.b, u, :], sums[s.b][:, u, 0:cols]).then_inc(read_out[s.b], 1)
                else:
                    act.wait_ge(scattered[s.b][u], 16 * s.i)
                    act.copy(res[:, s.b, u, 0:cols], sums[s.b][:, u, 0:cols]).then_inc(read_out[s.b], 1)

            def body(s):
                before, here = s.at(-1), s.at(0)
                for u in range(QUAD):
                    if here:
                        if linear is not None and u == 0:
                            act.wait_ge(edge_here[s.b], 16 * s.i + 16)
                        if weights:
                            act.wait_ge(msg_done[s.b], QUAD * s.i + u + 1)
                        else:
                            act.wait_ge(rows_here[s.b][u], 16 * s.i + 16)
                        if u:
                            act.wait_ge(summed[s.b], QUAD * s.i + u)
                        elif before:
                            act.wait_ge(summed[before.b], QUAD * before.i + QUAD)
                        pb, pu = (s.b, u - 1) if u else (1 - s.b, QUAD - 1)
                        act.copy(msg[0:1, s.b, u, :], sums[pb][LAST_SLOT:LAST_SLOT + 1, pu, 0:cols]).then_inc(carried[s.b], 1)
                    if u and here:
                        read(s, u - 1)
                    elif u == 0 and before:
                        read(before, QUAD - 1)
            run_steps(act, of, 0, 1, body)
            if clear is not None:
                act.wait_ge(cleared, 16 * transfers)

        @block.vector
        def _(dve):
            if mean:
                dve.memset(msg[:, :, :, width:width + 1], 1.0)
            if clear is not None:
                dve.memset(zeros[:, :], 0.0).then_inc(zeroed, 1)
            dve.memset(banks[:, QUAD - 1, :, :], 0.0).then_inc(start, 1)

            def compare(s):
                dve.wait_ge(drow_here[s.b], 16 * s.i + 16)
                dve.wait_ge(summed[s.b], QUAD * s.i)
                for u in range(QUAD):
                    dve.tensor_scalar(same[:, s.b, u, :], drow[:, s.b, u, :], g.dcol[:, ds(s.n * QUAD + u, 1)], None,
                                      ALU.is_equal).then_inc(same_done[s.b], 1)

            def weigh(s):
                for u in range(QUAD):
                    dve.wait_ge(rows_here[s.b][u], 16 * s.i + 16)
                    wts = weights[0][:, ds((s.n * QUAD + u) * HEADS, HEADS)]
                    dve.tensor_copy(msg[:, s.b, u, P:P + HEADS], wts)
                    dve.tensor_tensor(msg[:, s.b, u, 0:P].rearrange("p (h k) -> p h k", k=HEAD_DIM),
                                      raw[:, s.b, u, :].rearrange("p (h k) -> p h k", k=HEAD_DIM),
                                      wts.unsqueeze(2).broadcast_to([P, HEADS, HEAD_DIM]), ALU.mult).then_inc(msg_done[s.b], 1)
                    dve.wait_ge(scattered[s.b][u], 16 * s.i)
                    dve.tensor_copy(res[:, s.b, u, cols:], weights[1][:, ds((s.n * QUAD + u) * HEADS, HEADS)]).then_inc(maxima_done[s.b], 1)

            def body(s):
                if n := s.at(1):
                    compare(n)
                if weights and s.at(0):
                    weigh(s)
                if mean and s.at(0):
                    dve.wait_ge(read_out[s.b], QUAD * s.i + QUAD)
                    dve.tensor_scalar(count[:, s.b, :], plain[:, s.b, :, width], 1.0, None, ALU.max).then_inc(share_done[s.b], 1)
                    dve.wait_ge(share_done[s.b], 2 * s.i + 1)
                    dve.reciprocal(share[:, s.b, :], count[:, s.b, :]).then_inc(share_done[s.b], 1)
                    dve.wait_ge(share_done[s.b], 2 * s.i + 2)
                    for u in range(QUAD):
                        dve.wait_ge(scattered[s.b][u], 16 * s.i)
                        if linear is not None:
                            dve.tensor_copy(res[:, s.b, u, P:], plain[:, s.b, u, P:2 * P])
                        dve.tensor_scalar(res[:, s.b, u, 0:P], plain[:, s.b, u, 0:P], share[:, s.b, u:u + 1], None,
                                          ALU.mult).then_inc(res_done[s.b], 1)
            run_steps(dve, of, 1, 0, body)

        @block.tensor
        def _(pe):
            def body(s):
                pe.wait_ge(read_out[s.b], QUAD * s.i)
                for u in range(QUAD):
                    pe.wait_ge(same_done[s.b], QUAD * s.i + u + 1)
                    pe.wait_ge(carried[s.b], QUAD * s.i + u + 1)
                    pe.matmul(sums[s.b][:, u, 0:cols], same[:, s.b, u, :], msg[:, s.b, u, :], start=True, stop=True
                              ).then_inc(summed[s.b], 1)
            run_steps(pe, of, 0, 0, body)


def sage_hidden(nc, g):
    with Phase(nc, "hid") as ph:
        x_in, m_in = ph.sb("x_in", [P, 2, QUAD, P]), ph.sb("m_in", [P, 2, QUAD, P])
        xT, mT = ph.sb("xT", [P, 2, GROUP]), ph.sb("mT", [P, 2, GROUP])
        biased, h = ph.sb("biased", [P, 2, GROUP]), ph.sb("h", [P, 2, QUAD, P])
        ps_x, ps_m = [ph.ps(f"ps_x{b}") for b in range(2)], [ph.ps(f"ps_m{b}") for b in range(2)]
        ps_h = [ph.ps(f"ps_h{b}") for b in range(2)]
        x_here, m_here, stored = ph.sems("x_here"), ph.sems("m_here"), ph.sems("stored")
        x_turned, m_turned, xT_done, mT_done = ph.sems("x_turned"), ph.sems("m_turned"), ph.sems("xT_done"), ph.sems("mT_done")
        sp_turn = ph.sem("sp_turn")
        h_summed, biased_done, h_done = ph.sems("h_summed"), ph.sems("biased_done"), ph.sems("h_done")
        block = ph.block()
        of = g.groups

        @block.sync
        def _(sp):
            def body(s):
                if l := s.at(2):
                    hold(sp, sp_turn, x_turned[l.b], l.i)
                    hold(sp, sp_turn, m_turned[l.b], l.i)
                    sp.dma_start(x_in[:, l.b, :, :], group_rows(g.x, l.n)).then_inc(x_here[l.b], 16)
                    sp.dma_start(m_in[:, l.b, :, :], group_rows(g.seg, l.n)).then_inc(m_here[l.b], 16)
                if r := s.at(-1):
                    hold(sp, sp_turn, h_done[r.b], r.i + 1)
                    sp.dma_start(group_rows(g.h1, r.n), h[:, r.b, :, :]).then_inc(stored[r.b], 16)
            run_steps(sp, of, 2, 1, body)
            for b in range(2):
                sp.wait_ge(stored[b], 16 * (of // 2))

        @block.tensor
        def _(pe):
            def body(s):
                if t := s.at(1):
                    pe.wait_ge(x_here[t.b], 16 * t.i + 16)
                    pe.wait_ge(xT_done[t.b], t.i)
                    for j in range(QUAD):
                        turned = pe.transpose(ps_x[t.b][:, j * P:(j + 1) * P], x_in[:, t.b, j, :], g.ident[:, :])
                    turned.then_inc(x_turned[t.b], 1)
                    pe.wait_ge(m_here[t.b], 16 * t.i + 16)
                    pe.wait_ge(mT_done[t.b], t.i)
                    for j in range(QUAD):
                        turned = pe.transpose(ps_m[t.b][:, j * P:(j + 1) * P], m_in[:, t.b, j, :], g.ident[:, :])
                    turned.then_inc(m_turned[t.b], 1)
                if s.at(0):
                    pe.wait_ge(xT_done[s.b], s.i + 1)
                    pe.wait_ge(mT_done[s.b], s.i + 1)
                    pe.wait_ge(biased_done[s.b], s.i)
                    for j in range(QUAD):
                        c = slice(j * P, (j + 1) * P)
                        pe.matmul(ps_h[s.b][:, c], mT[:, s.b, c], g.w["W1lT"][:, :], start=True, stop=False)
                        last = pe.matmul(ps_h[s.b][:, c], xT[:, s.b, c], g.w["W1rT"][:, :], start=False, stop=True)
                    last.then_inc(h_summed[s.b], 1)
            run_steps(pe, of, 1, 0, body)

        @block.scalar
        def _(act):
            def body(s):
                if n := s.at(1):
                    act.wait_ge(x_turned[n.b], n.i + 1)
                    act.wait_ge(h_summed[n.b], n.i)
                    act.copy(xT[:, n.b, :], ps_x[n.b][:, :]).then_inc(xT_done[n.b], 1)
                if r := s.at(0):
                    act.wait_ge(biased_done[r.b], r.i + 1)
                    act.wait_ge(stored[r.b], 16 * r.i)
                    act.activation(h[:, r.b, :, :].rearrange("p j d -> p (j d)"), biased[:, r.b, :], ACT.Relu).then_inc(h_done[r.b], 1)
            run_steps(act, of, 1, 0, body)

        @block.vector
        def _(dve):
            def body(s):
                if n := s.at(1):
                    dve.wait_ge(m_turned[n.b], n.i + 1)
                    dve.wait_ge(h_summed[n.b], n.i)
                    dve.tensor_copy(mT[:, n.b, :], ps_m[n.b][:, :]).then_inc(mT_done[n.b], 1)
                if r := s.at(0):
                    dve.wait_ge(h_summed[r.b], r.i + 1)
                    dve.wait_ge(h_done[r.b], r.i)
                    dve.tensor_tensor(biased[:, r.b, :], ps_h[r.b][:, :], g.row["b1l"][:, :], ALU.add).then_inc(biased_done[r.b], 1)
            run_steps(dve, of, 1, 0, body)


class Norm:

    def __init__(self, ph, name):
        self.stats = ph.sb(f"{name}_stats", [P, 2, QUAD, 6])
        self.moments = ph.sb(f"{name}_moments", [P, 2, QUAD, 2])
        self.shifted = ph.sb(f"{name}_shifted", [P, 2, QUAD])
        self.rstd = ph.sb(f"{name}_rstd", [P, 2, QUAD])
        self.offset = ph.sb(f"{name}_offset", [P, 2, QUAD])
        self.dve_turn = ph.sem(f"{name}_dve_turn")
        self.offset_done = ph.sems(f"{name}_offset_done")
        self.stats_done = ph.sems(f"{name}_stats_done")
        self.moments_done = ph.sems(f"{name}_moments_done")
        self.shifted_done = ph.sems(f"{name}_shifted_done")
        self.rstd_done = ph.sems(f"{name}_rstd_done")

    def stats_of(self, dve, s, tiles):
        for j in range(QUAD):
            dve.bn_stats(self.stats[:, s.b, j, :], tiles[:, j, :]).then_inc(self.stats_done[s.b], 1)

    def moments_of(self, dve, s):
        dve.wait_ge(self.rstd_done[s.b], s.i)
        hold(dve, self.dve_turn, self.stats_done[s.b], QUAD * s.i + QUAD)
        for j in range(QUAD):
            dve.bn_aggr(self.moments[:, s.b, j, :], self.stats[:, s.b, j, :]).then_inc(self.moments_done[s.b], 1)

    def deviation(self, pool, s, minus_half):
        pool.wait_ge(self.moments_done[s.b], QUAD * s.i + QUAD)
        pool.tensor_tensor(self.shifted[:, s.b, :], self.moments[:, s.b, :, 1], minus_half[:, QUAD:], ALU.add).then_inc(self.shifted_done[s.b], 1)
        pool.wait_ge(self.shifted_done[s.b], s.i + 1)
        pool.tensor_tensor(self.rstd[:, s.b, :], self.shifted[:, s.b, :], minus_half[:, 0:QUAD], ALU.pow).then_inc(self.rstd_done[s.b], 1)

    def offset_of(self, dve, s):
        dve.wait_ge(self.rstd_done[s.b], s.i + 1)
        dve.scalar_tensor_tensor(self.offset[:, s.b, :], self.moments[:, s.b, :, 0], -1.0, self.rstd[:, s.b, :],
                                 ALU.mult, ALU.mult).then_inc(self.offset_done[s.b], 1)

    def apply(self, act, s, out, value, done):
        act.wait_ge(self.offset_done[s.b], s.i + 1)
        for j in range(QUAD):
            last = act.activation(out[:, s.b, j, :], value[:, s.b, j, :], ACT.Identity,
                                  bias=self.offset[:, s.b, j:j + 1], scale=self.rstd[:, s.b, j:j + 1])
        last.then_inc(done[s.b], 1)


def power_constants(ph, pool, tile, done):
    pool.memset(tile[:, 0:QUAD], -0.5).then_inc(done, 1)
    pool.memset(tile[:, QUAD:], EPS).then_inc(done, 1)
    pool.wait_ge(done, 2)


def turn_group(pe, psum, tile, s, ident, done):
    for j in range(QUAD):
        last = pe.transpose(psum[:, j * P:(j + 1) * P], tile[:, s.b, j, :], ident[:, :])
    last.then_inc(done[s.b], 1)


def flat(tile, b):
    return tile[:, b, :, :].rearrange("p j d -> p (j d)")


def sage_out(nc, g):
    with Phase(nc, "sageout") as ph:
        x_in, m_in, h_in = (ph.sb(n, [P, 2, QUAD, P]) for n in ("x_in", "m_in", "h_in"))
        mT, hT, x1T = (ph.sb(n, [P, 2, GROUP]) for n in ("mT", "hT", "x1T"))
        resid, value, x1 = (ph.sb(n, [P, 2, QUAD, P]) for n in ("resid", "value", "x1"))
        th, ta = ph.sb("th", [P, 2, QUAD, P]), ph.sb("ta", [P, 2, QUAD, 2 * HEADS])
        minus_half = ph.sb("minus_half", [P, 2 * QUAD])
        ps_m, ps_h, ps_1 = ph.ps("ps_m"), ph.ps("ps_h"), ph.ps("ps_1")
        ps_v, ps_th = [ph.ps(f"ps_v{b}") for b in range(2)], [ph.ps(f"ps_th{b}") for b in range(2)]
        ps_ta = ph.ps("ps_ta", [P, 2, QUAD, 2 * HEADS])
        norm = Norm(ph, "norm")
        x_here, m_here, h_here, x1_stored, th_stored, ta_stored = (ph.sems(n) for n in (
            "x_here", "m_here", "h_here", "x1_stored", "th_stored", "ta_stored"))
        m_turned, h_turned, x1_turned, mT_done, hT_done, x1T_done = (ph.sems(n) for n in (
            "m_turned", "h_turned", "x1_turned", "mT_done", "hT_done", "x1T_done"))
        v_summed, th_summed, resid_done, value_done, x1_done, th_done, ta_done = (ph.sems(n) for n in (
            "v_summed", "th_summed", "resid_done", "value_done", "x1_done", "th_done", "ta_done"))
        sp_turn, consts = ph.sem("sp_turn"), ph.sem("consts")
        block = ph.block()
        of = g.groups

        @block.sync
        def _(sp):
            def body(s):
                if l := s.at(2):
                    hold(sp, sp_turn, resid_done[l.b], l.i)
                    sp.dma_start(x_in[:, l.b, :, :], group_rows(g.x, l.n)).then_inc(x_here[l.b], 16)
                    hold(sp, sp_turn, m_turned[l.b], l.i)
                    sp.dma_start(m_in[:, l.b, :, :], group_rows(g.seg, l.n)).then_inc(m_here[l.b], 16)
                    hold(sp, sp_turn, h_turned[l.b], l.i)
                    sp.dma_start(h_in[:, l.b, :, :], group_rows(g.h1, l.n)).then_inc(h_here[l.b], 16)
                if r := s.at(-1):
                    hold(sp, sp_turn, x1_done[r.b], r.i + 1)
                    sp.dma_start(group_rows(g.x1, r.n), x1[:, r.b, :, :]).then_inc(x1_stored[r.b], 16)
                if r := s.at(-2):
                    hold(sp, sp_turn, th_done[r.b], r.i + 1)
                    sp.dma_start(group_rows(g.th, r.n), th[:, r.b, :, :]).then_inc(th_stored[r.b], 16)
                    hold(sp, sp_turn, ta_done[r.b], r.i + 1)
                    sp.dma_start(group_rows(g.ta, r.n, 2 * HEADS), ta[:, r.b, :, :]).then_inc(ta_stored[r.b], 16)
            run_steps(sp, of, 2, 2, body)
            for b in range(2):
                for stored in (x1_stored, th_stored, ta_stored):
                    sp.wait_ge(stored[b], 16 * (of // 2))

        @block.tensor
        def _(pe):
            def body(s):
                if r := s.at(-2):
                    pe.wait_ge(x1_done[r.b], r.i + 1)
                    q = r.at(-1)
                    if q:
                        pe.wait_ge(x1T_done[q.b], q.i + 1)
                    turn_group(pe, ps_1, x1, r, g.ident, x1_turned)
                if t := s.at(1):
                    q = t.at(-1)
                    pe.wait_ge(m_here[t.b], 16 * t.i + 16)
                    if q:
                        pe.wait_ge(mT_done[q.b], q.i + 1)
                    turn_group(pe, ps_m, m_in, t, g.ident, m_turned)
                    pe.wait_ge(h_here[t.b], 16 * t.i + 16)
                    if q:
                        pe.wait_ge(hT_done[q.b], q.i + 1)
                    turn_group(pe, ps_h, h_in, t, g.ident, h_turned)
                if s.at(0):
                    pe.wait_ge(mT_done[s.b], s.i + 1)
                    pe.wait_ge(hT_done[s.b], s.i + 1)
                    pe.wait_ge(value_done[s.b], s.i)
                    for j in range(QUAD):
                        c = slice(j * P, (j + 1) * P)
                        pe.matmul(ps_v[s.b][:, c], mT[:, s.b, c], g.w["W2lT"][:, :], start=True, stop=False)
                        last = pe.matmul(ps_v[s.b][:, c], hT[:, s.b, c], g.w["W2rT"][:, :], start=False, stop=True)
                    last.then_inc(v_summed[s.b], 1)
                if r := s.at(-2):
                    pe.wait_ge(x1T_done[r.b], r.i + 1)
                    pe.wait_ge(th_done[r.b], r.i)
                    q = r.at(-1)
                    if q:
                        pe.wait_ge(ta_done[q.b], q.i + 1)
                    for j in range(QUAD):
                        c = slice(j * P, (j + 1) * P)
                        pe.matmul(ps_ta[:, r.b, j, :], x1T[:, r.b, c], g.w["attT"][:, :], start=True, stop=True)
                        last = pe.matmul(ps_th[r.b][:, c], x1T[:, r.b, c], g.w["linT"][:, :], start=True, stop=True)
                    last.then_inc(th_summed[r.b], 1)
            run_steps(pe, of, 1, 2, body)

        @block.scalar
        def _(act):
            def body(s):
                if r := s.at(-2):
                    act.wait_ge(x1_turned[r.b], r.i + 1)
                    act.wait_ge(th_summed[r.b], r.i)
                    act.copy(x1T[:, r.b, :], ps_1[:, :]).then_inc(x1T_done[r.b], 1)
                if t := s.at(1):
                    act.wait_ge(h_turned[t.b], t.i + 1)
                    act.wait_ge(v_summed[t.b], t.i)
                    act.copy(hT[:, t.b, :], ps_h[:, :]).then_inc(hT_done[t.b], 1)
                if r := s.at(-1):
                    act.wait_ge(x1_stored[r.b], 16 * r.i)
                    act.wait_ge(x1_turned[r.b], r.i)
                    norm.apply(act, r, x1, value, x1_done)
                if r := s.at(-2):
                    act.wait_ge(th_summed[r.b], r.i + 1)
                    act.wait_ge(th_stored[r.b], 16 * r.i)
                    act.copy(flat(th, r.b), ps_th[r.b][:, :]).then_inc(th_done[r.b], 1)
                    act.wait_ge(ta_stored[r.b], 16 * r.i)
                    act.copy(ta[:, r.b, :, :], ps_ta[:, r.b, :, :]).then_inc(ta_done[r.b], 1)
            run_steps(act, of, 1, 2, body)

        @block.gpsimd
        def _(pool):
            power_constants(ph, pool, minus_half, consts)

            def body(s):
                if s.at(0):
                    pool.wait_ge(x_here[s.b], 16 * s.i + 16)
                    pool.wait_ge(value_done[s.b], s.i)
                    pool.tensor_tensor(flat(resid, s.b), flat(x_in, s.b), g.row["b2l"][:, :], ALU.add).then_inc(resid_done[s.b], 1)
                if r := s.at(-1):
                    norm.deviation(pool, r, minus_half)
            run_steps(pool, of, 0, 1, body)

        @block.vector
        def _(dve):
            def body(s):
                if r := s.at(-1):
                    norm.offset_of(dve, r)
                if s.at(0):
                    dve.wait_ge(v_summed[s.b], s.i + 1)
                    dve.wait_ge(resid_done[s.b], s.i + 1)
                    dve.wait_ge(x1_done[s.b], s.i)
                    dve.tensor_tensor(flat(value, s.b), ps_v[s.b][:, :], flat(resid, s.b), ALU.add).then_inc(value_done[s.b], 1)
                if t := s.at(1):
                    dve.wait_ge(m_turned[t.b], t.i + 1)
                    dve.wait_ge(v_summed[t.b], t.i)
                    dve.tensor_copy(mT[:, t.b, :], ps_m[:, :]).then_inc(mT_done[t.b], 1)
                if s.at(0):
                    dve.wait_ge(value_done[s.b], s.i + 1)
                    norm.stats_of(dve, s, value[:, s.b, :, :])
                    norm.moments_of(dve, s)
            run_steps(dve, of, 1, 1, body)


def edge_scores(nc, g):
    with Phase(nc, "score") as ph:
        src_ix, dst_ix = ph.sb("src_ix", [P, 2, QUAD], I32), ph.sb("dst_ix", [P, 2, QUAD], I32)
        at_src, at_dst = ph.sb("at_src", [P, 2, QUAD, 2 * HEADS]), ph.sb("at_dst", [P, 2, QUAD, 2 * HEADS])
        sums = ph.sb("sums", [P, 2, 2, QUAD, HEADS])
        leaky = ph.sb("leaky", [P, 2, 2, QUAD, HEADS])
        ix_here = ph.sems("ix_here")
        src_rows = [ph.sems(f"src_rows{b}_", QUAD) for b in range(2)]
        dst_rows = [ph.sems(f"dst_rows{b}_", QUAD) for b in range(2)]
        summed, leaky_done, score_done = ph.sems("summed"), ph.sems("leaky_done"), ph.sems("score_done")
        pool_turn, sp_turn = ph.sem("pool_turn"), ph.sem("sp_turn")
        block = ph.block()
        of = g.quads

        @block.sync
        def _(sp):
            def load(s):
                sp.dma_start(src_ix[:, s.b, :], g.srcw[:, ds(s.n * QUAD, QUAD)]).then_inc(ix_here[s.b], 16)
                sp.dma_start(dst_ix[:, s.b, :], g.dstw[:, ds(s.n * QUAD, QUAD)]).then_inc(ix_here[s.b], 16)

            def body(s):
                if l := s.at(2):
                    for u in range(QUAD):
                        hold(sp, sp_turn, src_rows[l.b][u], 16 * l.i)
                        hold(sp, sp_turn, dst_rows[l.b][u], 16 * l.i)
                    load(l)
            run_steps(sp, of, 2, 0, body)

        @block.gpsimd
        def _(pool):
            def body(s):
                hold(pool, pool_turn, ix_here[s.b], 32 * s.i + 32)
                hold(pool, pool_turn, summed[s.b], 2 * s.i)
                for u in range(QUAD):
                    for ix, rows, here in ((src_ix, at_src, src_rows), (dst_ix, at_dst, dst_rows)):
                        pool.indirect_dma_start(out=rows[:, s.b, u, :], out_offset=None, in_=g.ta,
                                                in_offset=bass.IndirectOffsetOnAxis(ap=ix[:, s.b, u:u + 1], axis=0)
                                                ).then_inc(here[s.b][u], 16)
            run_steps(pool, of, 0, 0, body)

        @block.vector
        def _(dve):
            def body(s):
                for u in range(QUAD):
                    dve.wait_ge(src_rows[s.b][u], 16 * s.i + 16)
                    dve.wait_ge(dst_rows[s.b][u], 16 * s.i + 16)
                dve.tensor_tensor(sums[:, s.b, 0, :, :], at_src[:, s.b, :, 0:HEADS], at_dst[:, s.b, :, HEADS:], ALU.add).then_inc(summed[s.b], 1)
                dve.tensor_tensor(sums[:, s.b, 1, :, :], at_dst[:, s.b, :, 0:HEADS], at_dst[:, s.b, :, HEADS:], ALU.add).then_inc(summed[s.b], 1)
                dve.wait_ge(summed[s.b], 2 * s.i + 2)
                both = sums[:, s.b, :, :, :].rearrange("p a t h -> p (a t h)")
                dve.scalar_tensor_tensor(leaky[:, s.b, :, :, :].rearrange("p a t h -> p (a t h)"), both, SLOPE, both,
                                         ALU.mult, ALU.max).then_inc(leaky_done[s.b], 1)
                dve.wait_ge(leaky_done[s.b], s.i + 1)
                dve.tensor_tensor(g.score[:, ds(s.n * QUAD * HEADS, QUAD * HEADS)],
                                  leaky[:, s.b, 0, :, :].rearrange("p t h -> p (t h)"),
                                  leaky[:, s.b, 1, :, :].rearrange("p t h -> p (t h)"), ALU.subtract).then_inc(score_done[s.b], 1)
            run_steps(dve, of, 0, 0, body)
            for b in range(2):
                dve.wait_ge(score_done[b], of // 2)
            dve.memset(g.score[0:1, :], LOW)


def edge_softmax(nc, g):
    runs = g.quads * QUAD // CHUNKS
    ch = CHUNKS * HEADS
    with Phase(nc, "soft") as ph:
        order = ph.sb("order", [ch, runs * P], I32)
        bar_up, bar_down = ph.sb("bar_up", [ch, runs * P]), ph.sb("bar_down", [ch, runs * P])
        line, up, down = (ph.sb(n, [ch, runs, P]) for n in ("line", "up", "down"))
        spare = ph.sb("spare", [ch, 2, runs])
        ends = ph.sb("ends", [ch, 4])
        row = ph.sb("row", [1, 4, CHUNKS, HEADS])
        carry = ph.sb("carry", [1, 2, CHUNKS, HEADS])
        init = ph.sb("init", [ch, 2])
        one = ph.sb("one", [1, 1])
        ps_in = [ph.ps(f"ps_in{k}") for k in range(2)]
        ps_out = [ph.ps(f"ps_out{k}") for k in range(2)]
        ps_row, ps_col = ph.ps("ps_row", [1, 512]), ph.ps("ps_col", [ch, 512])
        order_here, laid, line_read, line_done = ph.sem("order_here"), ph.sem("laid"), ph.sem("line_read"), ph.sem("line_done")
        step, scanned, back, back_read = ph.sem("step"), ph.sem("scanned"), ph.sem("back"), ph.sem("back_read")
        row_done, row_read, col_done, exp_done = ph.sem("row_done"), ph.sem("row_read"), ph.sem("col_done"), ph.sem("exp_done")
        block = ph.block()
        score = ph.sb("score", [P, runs, CHUNKS, HEADS])
        score_done = ph.sem("score_done")
        per = 512 // P
        trips = -(-runs // per)
        per_back = 512 // ch
        trips_back = 2 * -(-runs // per_back)

        @block.sync
        def _(sp):
            for c in range(CHUNKS):
                sp.dma_start(order[c * HEADS:(c + 1) * HEADS, :], g.order[c:c + 1, :].broadcast_to([HEADS, runs * P])).then_inc(order_here, 16)

        @block.tensor
        def _(pe):
            pe.wait_ge(score_done, 1)
            for k in range(trips):
                if k >= 2:
                    pe.wait_ge(line_read, k - 1)
                for r in range(k * per, min(runs, (k + 1) * per)):
                    last = pe.transpose(ps_in[k % 2][0:ch, (r % per) * P:(r % per + 1) * P],
                                        score[:, r, :, :].rearrange("p c h -> p (c h)"), g.ident[:, :])
                last.then_inc(laid, 1)
            pe.wait_ge(scanned, 1)
            for k in range(4):
                last = pe.transpose(ps_row[0:1, k * ch:(k + 1) * ch], ends[:, k:k + 1], g.ident[0:ch, 0:ch])
            last.then_inc(row_done, 1)
            pe.wait_ge(row_read, 1)
            for k in range(2):
                last = pe.matmul(ps_col[:, k:k + 1], carry[0:1, k, :, :].rearrange("p c h -> p (c h)"), one[0:1, 0:1], start=True, stop=True)
            last.then_inc(col_done, 1)
            pe.wait_ge(exp_done, 2)
            k = 0
            for source in (up, down):
                for a in range(0, runs, per_back):
                    if k >= 2:
                        pe.wait_ge(back_read, k - 1)
                    for r in range(a, min(runs, a + per_back)):
                        last = pe.transpose(ps_out[k % 2][:, (r - a) * ch:(r - a + 1) * ch], source[:, r, :], g.ident[0:ch, 0:ch])
                    last.then_inc(back, 1)
                    k += 1

        @block.scalar
        def _(act):
            for k in range(trips):
                act.wait_ge(laid, k + 1)
                a, z = k * per, min(runs, (k + 1) * per)
                act.copy(line[:, a:z, :].rearrange("p r e -> p (r e)"), ps_in[k % 2][0:ch, 0:(z - a) * P]).then_inc(line_read, 1)
            act.wait_ge(exp_done, 1)
            act.activation(up[:, :, :], up[:, :, :], ACT.Exp).then_inc(exp_done, 1)

        @block.vector
        def _(dve):
            done = [0]

            def chain(ins):
                done[0] += 1
                ins.then_inc(step, 1)
                dve.wait_ge(step, done[0])

            def exchange(tile):
                dve.tensor_copy(spare[:, 0, :], tile[:, :, LAST_SLOT])
                chain(dve.tensor_copy(spare[:, 1, :], tile[:, :, P - 1]))
                dve.tensor_copy(tile[:, :, LAST_SLOT], spare[:, 1, :])
                chain(dve.tensor_copy(tile[:, :, P - 1], spare[:, 0, :]))

            dve.tensor_copy(score[:, :, :, :].rearrange("p r c h -> p c r h"),
                            g.score[:, 0:CHUNKS * runs * HEADS].rearrange("p (c r h) -> p c r h", c=CHUNKS, r=runs)).then_inc(score_done, 1)
            dve.memset(one[:, :], 1.0)
            dve.memset(carry[0:1, 0, 0, :], LOW)
            dve.memset(carry[0:1, 1, CHUNKS - 1, :], LOW)
            dve.memset(bar_up[:, 0:1], 0.0)
            dve.memset(bar_down[:, runs * P - 1:], 0.0)
            dve.wait_ge(order_here, 16 * CHUNKS)
            dve.tensor_tensor(bar_up[:, 1:], order[:, 1:], order[:, 0:runs * P - 1], ALU.not_equal)
            chain(dve.tensor_tensor(bar_down[:, 0:runs * P - 1], order[:, 1:], order[:, 0:runs * P - 1], ALU.not_equal))
            dve.tensor_scalar(bar_up[:, :], bar_up[:, :], LOW, None, ALU.mult)
            chain(dve.tensor_scalar(bar_down[:, :], bar_down[:, :], LOW, None, ALU.mult))
            dve.tensor_reduce(ends[:, 2:3], bar_up[:, :], mybir.AxisListType.X, ALU.min)
            chain(dve.tensor_reduce(ends[:, 3:4], bar_down[:, :], mybir.AxisListType.X, ALU.min))
            dve.wait_ge(line_read, trips)
            exchange(line)
            scores = line[:, :, :].rearrange("p r e -> p (r e)")
            ups, downs = up[:, :, :].rearrange("p r e -> p (r e)"), down[:, :, :].rearrange("p r e -> p (r e)")

            def scan(first_up, first_down):
                dve.tensor_tensor_scan(ups, bar_up[:, :], scores, first_up, ALU.add, ALU.max)
                chain(dve.tensor_tensor_scan(downs[:, ::-1], bar_down[:, ::-1], scores[:, ::-1], first_down, ALU.add, ALU.max))

            scan(LOW, LOW)
            dve.tensor_copy(ends[:, 0:1], ups[:, runs * P - 1:])
            chain(dve.tensor_copy(ends[:, 1:2], downs[:, 0:1]))
            dve.sem_inc(scanned, 1)
            dve.wait_ge(row_done, 1)
            chain(dve.tensor_copy(row[0:1, :, :, :].rearrange("p k c h -> p (k c h)"), ps_row[0:1, 0:4 * ch]))
            for c in range(1, CHUNKS):
                z = CHUNKS - 1 - c
                dve.scalar_tensor_tensor(carry[0:1, 0, c, :], carry[0:1, 0, c - 1, :], row[0:1, 2, c - 1, 0:1], row[0:1, 0, c - 1, :],
                                         ALU.add, ALU.max)
                chain(dve.scalar_tensor_tensor(carry[0:1, 1, z, :], carry[0:1, 1, z + 1, :], row[0:1, 3, z + 1, 0:1],
                                               row[0:1, 1, z + 1, :], ALU.add, ALU.max))
            dve.sem_inc(row_read, 1)
            dve.wait_ge(col_done, 1)
            chain(dve.tensor_copy(init[:, :], ps_col[:, 0:2]))
            scan(init[:, 0:1], init[:, 1:2])
            chain(dve.scalar_tensor_tensor(downs, downs, 0.0, ups, ALU.max, ALU.max))
            chain(dve.tensor_tensor(ups, scores, downs, ALU.subtract))
            exchange(down)
            exchange(up)
            dve.sem_inc(exp_done, 1)
            k = 0
            for dst in (g.weight, g.peak):
                into = dst[:, 0:CHUNKS * runs * HEADS].rearrange("p (c r h) -> p c r h", c=CHUNKS, r=runs)
                for a in range(0, runs, per_back):
                    z = min(runs, a + per_back)
                    dve.wait_ge(back, k + 1)
                    for r in range(a, z):
                        last = dve.tensor_copy(into[:, :, r, :], ps_out[k % 2][:, (r - a) * ch:(r - a + 1) * ch].rearrange("p (c h) -> p c h", c=CHUNKS))
                    last.then_inc(back_read, 1)
                    k += 1


def apply_affine(dve, norm, s, between, out, tiles, gamma, extra, between_done, out_done):
    dve.wait_ge(norm.rstd_done[s.b], s.i + 1)
    for j in range(QUAD):
        dve.scalar_tensor_tensor(between[:, s.b, j, :], tiles[:, j, :], norm.moments[:, s.b, j, 0:1],
                                 gamma[:, 0:P], ALU.subtract, ALU.mult).then_inc(between_done[s.b], 1)
    dve.wait_ge(between_done[s.b], QUAD * s.i + QUAD)
    for j in range(QUAD):
        last = dve.scalar_tensor_tensor(out[:, s.b, j, :], between[:, s.b, j, :], norm.rstd[:, s.b, j:j + 1],
                                        extra[:, s.b, j, :], ALU.mult, ALU.add)
    last.then_inc(out_done[s.b], 1)


def in_tiles(bank):
    return bank[:, :].rearrange("p (j d) -> p j d", j=QUAD)


def gat_out(nc, g):
    with Phase(nc, "gatout") as ph:
        x_in, th_in, s_in = ph.sb("x_in", [P, 2, QUAD, P]), ph.sb("th_in", [P, 2, QUAD, P]), ph.sb("s_in", [P, 2, QUAD, AUG])
        loop_w, total_w, share = (ph.sb(n, [P, 2, QUAD, HEADS]) for n in ("loop_w", "total_w", "share"))
        own, total, mean = (ph.sb(n, [P, 2, QUAD, P]) for n in ("own", "total", "mean"))
        meanT = ph.sb("meanT", [P, 2, GROUP])
        between, value2, extra, x2 = (ph.sb(n, [P, 2, QUAD, P]) for n in ("between", "value2", "extra", "x2"))
        minus_half = ph.sb("minus_half", [P, 2 * QUAD])
        ps_m, ps_v = [ph.ps(f"ps_m{b}") for b in range(2)], [ph.ps(f"ps_v{b}") for b in range(2)]
        norm, norm2 = Norm(ph, "norm"), Norm(ph, "norm2")
        x_here, th_here, s_here, stored = (ph.sems(n) for n in ("x_here", "th_here", "s_here", "stored"))
        (loop_done, total_w_done, share_done, own_done, total_done, mean_done, turned, meanT_done, v_summed,
         between_done, value2_done, extra_done, x2_done) = (ph.sems(n) for n in (
             "loop_done", "total_w_done", "share_done", "own_done", "total_done", "mean_done", "turned", "meanT_done",
             "v_summed", "between_done", "value2_done", "extra_done", "x2_done"))
        sp_turn, consts = ph.sem("sp_turn"), ph.sem("consts")
        block = ph.block()
        of = g.groups

        def by_head(tile, b):
            return tile[:, b, :, :].rearrange("p j (h k) -> p (j h) k", k=HEAD_DIM)

        def spread(tile, b):
            return tile[:, b, :, :].rearrange("p j h -> p (j h)").unsqueeze(2).broadcast_to([P, QUAD * HEADS, HEAD_DIM])

        @block.sync
        def _(sp):
            def body(s):
                if l := s.at(2):
                    hold(sp, sp_turn, own_done[l.b], l.i)
                    sp.dma_start(th_in[:, l.b, :, :], group_rows(g.th, l.n)).then_inc(th_here[l.b], 16)
                    hold(sp, sp_turn, total_done[l.b], l.i)
                    sp.dma_start(s_in[:, l.b, :, :], group_rows(g.gat, l.n, AUG)).then_inc(s_here[l.b], 16)
                    hold(sp, sp_turn, extra_done[l.b], l.i)
                    sp.dma_start(x_in[:, l.b, :, :], group_rows(g.x1, l.n)).then_inc(x_here[l.b], 16)
                if r := s.at(-2):
                    hold(sp, sp_turn, x2_done[r.b], r.i + 1)
                    sp.dma_start(group_rows(g.x2, r.n), x2[:, r.b, :, :]).then_inc(stored[r.b], 16)
            run_steps(sp, of, 2, 2, body)
            for b in range(2):
                sp.wait_ge(stored[b], 16 * (of // 2))

        @block.scalar
        def _(act):
            def body(s):
                if n := s.at(1):
                    act.wait_ge(s_here[n.b], 16 * n.i + 16)
                    act.wait_ge(own_done[n.b], n.i)
                    act.wait_ge(total_w_done[n.b], n.i)
                    act.activation(loop_w[:, n.b, :, :], s_in[:, n.b, :, P + HEADS:], ACT.Exp, scale=-1.0).then_inc(loop_done[n.b], 1)
                if r := s.at(-2):
                    act.wait_ge(stored[r.b], 16 * r.i)
                    norm2.apply(act, r, x2, value2, x2_done)
                if s.at(0):
                    act.wait_ge(turned[s.b], s.i + 1)
                    act.wait_ge(v_summed[s.b], s.i)
                    act.activation(meanT[:, s.b, :], ps_m[s.b][:, :], ACT.Identity, bias=g.col[:, 0:1]).then_inc(meanT_done[s.b], 1)
            run_steps(act, of, 1, 2, body)

        @block.gpsimd
        def _(pool):
            power_constants(ph, pool, minus_half, consts)

            def body(s):
                if s.at(0):
                    pool.wait_ge(x_here[s.b], 16 * s.i + 16)
                    pool.wait_ge(value2_done[s.b], s.i)
                    pool.tensor_tensor(flat(extra, s.b), flat(x_in, s.b), g.row["ln1_beta"][:, :], ALU.add).then_inc(extra_done[s.b], 1)
                if r := s.at(-1):
                    norm.deviation(pool, r, minus_half)
                if n := s.at(1):
                    pool.wait_ge(th_here[n.b], 16 * n.i + 16)
                    pool.wait_ge(loop_done[n.b], n.i + 1)
                    pool.wait_ge(total_done[n.b], n.i)
                    pool.tensor_tensor(by_head(own, n.b), by_head(th_in, n.b), spread(loop_w, n.b), ALU.mult).then_inc(own_done[n.b], 1)
                if r := s.at(-1):
                    norm2.deviation(pool, r, minus_half)
            run_steps(pool, of, 1, 1, body)

        @block.tensor
        def _(pe):
            def body(s):
                pe.wait_ge(mean_done[s.b], s.i + 1)
                pe.wait_ge(meanT_done[s.b], s.i)
                turn_group(pe, ps_m[s.b], mean, s, g.ident, turned)
                pe.wait_ge(between_done[s.b], QUAD * s.i)
                pe.matmul(ps_v[s.b][:, :], g.ones[0:1, :], g.row["proj_b"][0:1, :], start=True, stop=False)
                pe.wait_ge(meanT_done[s.b], s.i + 1)
                for j in range(QUAD):
                    c = slice(j * P, (j + 1) * P)
                    last = pe.matmul(ps_v[s.b][:, c], meanT[:, s.b, c], g.w["projT"][:, :], start=False, stop=j == QUAD - 1)
                last.then_inc(v_summed[s.b], 1)
            run_steps(pe, of, 0, 0, body)

        @block.vector
        def _(dve):
            def body(s):
                here, r, q = s.at(0), s.at(-1), s.at(-2)
                if here:
                    dve.wait_ge(loop_done[s.b], s.i + 1)
                    dve.tensor_tensor(total_w[:, s.b, :, :], loop_w[:, s.b, :, :], s_in[:, s.b, :, P:P + HEADS], ALU.add).then_inc(total_w_done[s.b], 1)
                if q:
                    norm2.offset_of(dve, q)
                if r:
                    dve.wait_ge(v_summed[r.b], r.i + 1)
                    norm.stats_of(dve, r, in_tiles(ps_v[r.b]))
                if here:
                    dve.wait_ge(total_w_done[s.b], s.i + 1)
                    dve.reciprocal(share[:, s.b, :, :], total_w[:, s.b, :, :]).then_inc(share_done[s.b], 1)
                if r:
                    norm.moments_of(dve, r)
                if here:
                    dve.wait_ge(own_done[s.b], s.i + 1)
                    dve.tensor_tensor(total[:, s.b, :, :], own[:, s.b, :, :], s_in[:, s.b, :, 0:P], ALU.add).then_inc(total_done[s.b], 1)
                    dve.wait_ge(total_done[s.b], s.i + 1)
                    dve.wait_ge(share_done[s.b], s.i + 1)
                    dve.wait_ge(turned[s.b], s.i)
                    dve.tensor_tensor(by_head(mean, s.b), by_head(total, s.b), spread(share, s.b), ALU.mult).then_inc(mean_done[s.b], 1)
                if r:
                    dve.wait_ge(extra_done[r.b], r.i + 1)
                    dve.wait_ge(x2_done[r.b], r.i)
                    apply_affine(dve, norm, r, between, value2, in_tiles(ps_v[r.b]), g.row["ln1_gamma"], extra, between_done, value2_done)
                    dve.wait_ge(value2_done[r.b], r.i + 1)
                    norm2.stats_of(dve, r, value2[:, r.b, :, :])
                    norm2.moments_of(dve, r)
            run_steps(dve, of, 0, 2, body)


def edge_mlp(nc, g):
    with Phase(nc, "mlp") as ph:
        x_in, e_in = ph.sb("x_in", [P, 2, QUAD, P]), ph.sb("e_in", [P, 2, QUAD, P])
        xT, eT, hid1, hid2 = (ph.sb(n, [P, 2, GROUP]) for n in ("xT", "eT", "hid1", "hid2"))
        between, value2, extra, twice, x3 = (ph.sb(n, [P, 2, QUAD, P]) for n in ("between", "value2", "extra", "twice", "x3"))
        minus_half = ph.sb("minus_half", [P, 2 * QUAD])
        ps_x, ps_e, ps_1, ps_2 = ph.ps("ps_x"), ph.ps("ps_e"), ph.ps("ps_1"), ph.ps("ps_2")
        ps_v = [ph.ps(f"ps_v{b}") for b in range(2)]
        norm, norm2 = Norm(ph, "norm"), Norm(ph, "norm2")
        x_here, e_here, stored = (ph.sems(n) for n in ("x_here", "e_here", "stored"))
        (x_turned, e_turned, xT_done, eT_done, summed1, summed2, hid1_done, hid2_done, v_summed, twice_done,
         between_done, value2_done, extra_done, x3_done) = (ph.sems(n) for n in (
             "x_turned", "e_turned", "xT_done", "eT_done", "summed1", "summed2", "hid1_done", "hid2_done", "v_summed",
             "twice_done", "between_done", "value2_done", "extra_done", "x3_done"))
        sp_turn, consts = ph.sem("sp_turn"), ph.sem("consts")
        block = ph.block()
        of = g.groups

        @block.sync
        def _(sp):
            def body(s):
                if l := s.at(2):
                    hold(sp, sp_turn, x_turned[l.b], l.i)
                    hold(sp, sp_turn, twice_done[l.b], l.i)
                    sp.dma_start(x_in[:, l.b, :, :], group_rows(g.x2, l.n)).then_inc(x_here[l.b], 16)
                    hold(sp, sp_turn, e_turned[l.b], l.i)
                    sp.dma_start(e_in[:, l.b, :, :], group_rows(g.seg, l.n, P, P)).then_inc(e_here[l.b], 16)
                if r := s.at(-3):
                    hold(sp, sp_turn, x3_done[r.b], r.i + 1)
                    sp.dma_start(group_rows(g.x3, r.n), x3[:, r.b, :, :]).then_inc(stored[r.b], 16)
            run_steps(sp, of, 2, 3, body)
            for b in range(2):
                sp.wait_ge(stored[b], 16 * (of // 2))

        @block.tensor
        def _(pe):
            def body(s):
                if s.at(0):
                    pe.wait_ge(xT_done[s.b], s.i + 1)
                    pe.wait_ge(eT_done[s.b], s.i + 1)
                    if q := s.at(-1):
                        pe.wait_ge(hid1_done[q.b], q.i + 1)
                    pe.matmul(ps_1[:, :], g.w["W1"][:, 0, :], xT[:, s.b, :], start=True, stop=False)
                    pe.matmul(ps_1[:, :], g.w["W1"][:, 1, :], eT[:, s.b, :], start=False, stop=True).then_inc(summed1[s.b], 1)
                if t := s.at(1):
                    q = t.at(-1)
                    pe.wait_ge(x_here[t.b], 16 * t.i + 16)
                    if q:
                        pe.wait_ge(xT_done[q.b], q.i + 1)
                    turn_group(pe, ps_x, x_in, t, g.ident, x_turned)
                    pe.wait_ge(e_here[t.b], 16 * t.i + 16)
                    if q:
                        pe.wait_ge(eT_done[q.b], q.i + 1)
                    turn_group(pe, ps_e, e_in, t, g.ident, e_turned)
                if r := s.at(-1):
                    pe.wait_ge(between_done[r.b], QUAD * r.i)
                    pe.matmul(ps_v[r.b][:, :], g.ones[0:1, :], g.row["b3"][0:1, :], start=True, stop=False)
                    pe.wait_ge(hid2_done[r.b], r.i + 1)
                    for j in range(QUAD):
                        c = slice(j * P, (j + 1) * P)
                        last = pe.matmul(ps_v[r.b][:, c], hid2[:, r.b, c], g.w["W3"][:, :], start=False, stop=j == QUAD - 1)
                    last.then_inc(v_summed[r.b], 1)
                if s.at(0):
                    pe.wait_ge(hid1_done[s.b], s.i + 1)
                    if q := s.at(-1):
                        pe.wait_ge(hid2_done[q.b], q.i + 1)
                    pe.matmul(ps_2[:, :], g.w["W2"][:, :], hid1[:, s.b, :], start=True, stop=True).then_inc(summed2[s.b], 1)
            run_steps(pe, of, 1, 1, body)

        @block.scalar
        def _(act):
            def body(s):
                if s.at(0):
                    act.wait_ge(x_here[s.b], 16 * s.i + 16)
                    act.wait_ge(extra_done[s.b], s.i)
                    act.mul(flat(twice, s.b), flat(x_in, s.b), 2.0).then_inc(twice_done[s.b], 1)
                    act.wait_ge(summed1[s.b], s.i + 1)
                    act.wait_ge(summed2[s.b], s.i)
                    act.activation(hid1[:, s.b, :], ps_1[:, :], ACT.Relu, bias=g.col[:, 1:2]).then_inc(hid1_done[s.b], 1)
                if t := s.at(1):
                    act.wait_ge(x_turned[t.b], t.i + 1)
                    act.wait_ge(summed1[t.b], t.i)
                    act.copy(xT[:, t.b, :], ps_x[:, :]).then_inc(xT_done[t.b], 1)
                if r := s.at(-3):
                    act.wait_ge(stored[r.b], 16 * r.i)
                    norm2.apply(act, r, x3, value2, x3_done)
                if s.at(0):
                    act.wait_ge(summed2[s.b], s.i + 1)
                    act.wait_ge(v_summed[s.b], s.i)
                    act.activation(hid2[:, s.b, :], ps_2[:, :], ACT.Relu, bias=g.col[:, 2:3]).then_inc(hid2_done[s.b], 1)
            run_steps(act, of, 1, 3, body)

        @block.gpsimd
        def _(pool):
            power_constants(ph, pool, minus_half, consts)

            def body(s):
                if r := s.at(-2):
                    norm.deviation(pool, r, minus_half)
                if r := s.at(-1):
                    pool.wait_ge(twice_done[r.b], r.i + 1)
                    pool.wait_ge(value2_done[r.b], r.i)
                    pool.tensor_tensor(flat(extra, r.b), flat(twice, r.b), g.row["ln2_beta"][:, :], ALU.add).then_inc(extra_done[r.b], 1)
                if r := s.at(-2):
                    norm2.deviation(pool, r, minus_half)
            run_steps(pool, of, 0, 2, body)

        @block.vector
        def _(dve):
            def body(s):
                r, q = s.at(-2), s.at(-3)
                if r:
                    dve.wait_ge(v_summed[r.b], r.i + 1)
                    norm.stats_of(dve, r, in_tiles(ps_v[r.b]))
                if q:
                    norm2.offset_of(dve, q)
                if r:
                    norm.moments_of(dve, r)
                if t := s.at(1):
                    dve.wait_ge(e_turned[t.b], t.i + 1)
                    dve.wait_ge(summed1[t.b], t.i)
                    dve.tensor_copy(eT[:, t.b, :], ps_e[:, :]).then_inc(eT_done[t.b], 1)
                if r:
                    dve.wait_ge(extra_done[r.b], r.i + 1)
                    dve.wait_ge(x3_done[r.b], r.i)
                    apply_affine(dve, norm, r, between, value2, in_tiles(ps_v[r.b]), g.row["ln2_gamma"], extra, between_done, value2_done)
                    dve.wait_ge(value2_done[r.b], r.i + 1)
                    norm2.stats_of(dve, r, value2[:, r.b, :, :])
                    norm2.moments_of(dve, r)
            run_steps(dve, of, 1, 3, body)


def messages(nc, g, t, hv):
    wide = 2 * P
    edge_dim = g.edge_t.shape[0]
    with Phase(nc, f"msg{t}") as ph:
        src_ix, dst_ix, tgt_ix = (ph.sb(n, [P, 2, QUAD], I32) for n in ("src_ix", "dst_ix", "tgt_ix"))
        drow = ph.sb("drow", [P, 2, QUAD, P], I32)
        edge = ph.sb("edge", [edge_dim, 2, GROUP])
        at_dst, at_src = ph.sb("at_dst", [P, 2, QUAD, P]), ph.sb("at_src", [P, 2, QUAD, P])
        dstT, srcT = ph.sb("dstT", [P, 2, GROUP]), ph.sb("srcT", [P, 2, GROUP])
        hidT = ph.sb("hidT", [P, 2, 2, GROUP])
        msg, same, res = ph.sb("msg", [P, 2, QUAD, wide]), ph.sb("same", [P, 2, QUAD, P]), ph.sb("res", [P, 2, QUAD, wide])
        ps_d, ps_s = ph.ps("ps_d"), ph.ps("ps_s")
        ps_h = [ph.ps(f"ps_h{m}") for m in range(2)]
        ps_msg = ph.ps("ps_msg", [P, QUAD, wide])
        banks = ph.ps("sums", [P, 2, 2, wide])
        sums = [banks[:, u % 2, u // 2, :] for u in range(QUAD)]
        src_here, dst_here, tgt_here, drow_here, edge_here = (ph.sems(n) for n in ("src_here", "dst_here", "tgt_here", "drow_here", "edge_here"))
        dst_rows = [ph.sems(f"dst_rows{b}_", QUAD) for b in range(2)]
        src_rows = [ph.sems(f"src_rows{b}_", QUAD) for b in range(2)]
        scattered = [ph.sems(f"scattered{b}_", QUAD) for b in range(2)]
        (dst_turned, src_turned, dstT_done, srcT_done, hid_summed, hid_done, msg_summed, msg_done, same_done, carried, summed,
         read_out) = (ph.sems(n) for n in (
             "dst_turned", "src_turned", "dstT_done", "srcT_done", "hid_summed", "hid_done", "msg_summed", "msg_done",
             "same_done", "carried", "summed", "read_out"))
        start, pool_turn, sp_turn = ph.sem("start"), ph.sem("pool_turn"), ph.sem("sp_turn")
        block = ph.block()
        of = g.quads

        @block.sync
        def _(sp):
            def body(s):
                if l := s.at(4):
                    for u in range(QUAD):
                        hold(sp, sp_turn, src_rows[l.b][u], 16 * l.i)
                        hold(sp, sp_turn, dst_rows[l.b][u], 16 * l.i)
                    sp.dma_start(dst_ix[:, l.b, :], g.dstw[:, ds(l.n * QUAD, QUAD)]).then_inc(dst_here[l.b], 16)
                    sp.dma_start(src_ix[:, l.b, :], g.srcw[:, ds(l.n * QUAD, QUAD)]).then_inc(src_here[l.b], 16)
                if l := s.at(2):
                    hold(sp, sp_turn, same_done[l.b], QUAD * l.i)
                    sp.dma_start(drow[:, l.b, :, :].rearrange("p t e -> p (t e)"),
                                 g.drow[:, ds(l.n * GROUP, GROUP)].broadcast_to([P, GROUP])).then_inc(drow_here[l.b], 16)
                    hold(sp, sp_turn, hid_summed[l.b], 2 * l.i)
                    sp.dma_start(edge[:, l.b, :], g.edge_t[:, ds(l.n * GROUP, GROUP)]).then_inc(edge_here[l.b], 16)
                if l := s.at(1):
                    for u in range(QUAD):
                        hold(sp, sp_turn, scattered[l.b][u], 16 * l.i)
                    sp.dma_start(tgt_ix[:, l.b, :], g.at_node[:, ds(l.n * QUAD, QUAD)]).then_inc(tgt_here[l.b], 16)
            run_steps(sp, of, 4, 0, body)

        @block.gpsimd
        def _(pool):
            def body(s):
                if n := s.at(2):
                    hold(pool, pool_turn, dst_here[n.b], 16 * n.i + 16)
                    hold(pool, pool_turn, src_here[n.b], 16 * n.i + 16)
                    hold(pool, pool_turn, dst_turned[n.b], n.i)
                    hold(pool, pool_turn, src_turned[n.b], n.i)
                    for ix, rows, landed in ((dst_ix, at_dst, dst_rows), (src_ix, at_src, src_rows)):
                        for u in range(QUAD):
                            pool.indirect_dma_start(out=rows[:, n.b, u, :], out_offset=None, in_=hv,
                                                    in_offset=bass.IndirectOffsetOnAxis(ap=ix[:, n.b, u:u + 1], axis=0)
                                                    ).then_inc(landed[n.b][u], 16)
                if r := s.at(-1):
                    hold(pool, pool_turn, tgt_here[r.b], 16 * r.i + 16)
                    for u in range(QUAD):
                        hold(pool, pool_turn, read_out[r.b], QUAD * r.i + u + 1)
                        pool.indirect_dma_start(out=g.seg, out_offset=bass.IndirectOffsetOnAxis(ap=tgt_ix[:, r.b, u:u + 1], axis=0),
                                                in_=res[:, r.b, u, :], in_offset=None,
                                                bounds_check=g.nodes - 1, oob_is_err=False).then_inc(scattered[r.b][u], 16)
            run_steps(pool, of, 2, 1, body)
            for b in range(2):
                for u in range(QUAD):
                    pool.wait_ge(scattered[b][u], 16 * (of // 2))

        @block.tensor
        def _(pe):
            def hid_product(n, k):
                m, part = divmod(k, 3)
                c = slice(m * P, (m + 1) * P)
                lhs, rhs = ((g.w["mw1"][:, t, 0, c], dstT[:, n.b, :]), (g.w["mw1"][:, t, 1, c], srcT[:, n.b, :]),
                            (g.w["mw1e"][:, t, c], edge[:, n.b, :]))[part]
                if part == 0:
                    if q := n.at(-1):
                        pe.wait_ge(hid_done[q.b], 2 * q.i + m + 1)
                ins = pe.matmul(ps_h[m][:, :], lhs, rhs, start=part == 0, stop=part == 2)
                if part == 2:
                    ins.then_inc(hid_summed[n.b], 1)

            def body(s):
                nxt, here = s.at(1), s.at(0)
                if nxt:
                    for u in range(QUAD):
                        pe.wait_ge(dst_rows[nxt.b][u], 16 * nxt.i + 16)
                    if here:
                        pe.wait_ge(dstT_done[s.b], s.i + 1)
                    turn_group(pe, ps_d, at_dst, nxt, g.ident, dst_turned)
                    for u in range(QUAD):
                        pe.wait_ge(src_rows[nxt.b][u], 16 * nxt.i + 16)
                    if here:
                        pe.wait_ge(srcT_done[s.b], s.i + 1)
                    turn_group(pe, ps_s, at_src, nxt, g.ident, src_turned)
                if here:
                    pe.wait_ge(hid_done[s.b], 2 * s.i + 2)
                    if q := s.at(-1):
                        pe.wait_ge(msg_done[q.b], 2 * q.i + 2)
                    for u in range(QUAD):
                        c = slice(u * P, (u + 1) * P)
                        pe.matmul(ps_msg[:, u, :], hidT[:, s.b, 0, c], g.w["mw2"][:, t, 0, :], start=True, stop=False)
                        last = pe.matmul(ps_msg[:, u, :], hidT[:, s.b, 1, c], g.w["mw2"][:, t, 1, :], start=False, stop=True)
                        if u % 2:
                            last.then_inc(msg_summed[s.b], 1)
                if nxt:
                    pe.wait_ge(dstT_done[nxt.b], nxt.i + 1)
                    pe.wait_ge(srcT_done[nxt.b], nxt.i + 1)
                    pe.wait_ge(edge_here[nxt.b], 16 * nxt.i + 16)
                    hid_product(nxt, 0)
                for u in range(QUAD):
                    if nxt:
                        hid_product(nxt, u + 1)
                    if here:
                        if u == 0:
                            pe.wait_ge(read_out[1 - s.b], QUAD * (s.i + s.b) - (1 if s.at(-1) else 0))
                        pe.wait_ge(same_done[s.b], QUAD * s.i + u + 1)
                        pe.wait_ge(carried[s.b], QUAD * s.i + u + 1)
                        pe.matmul(sums[u], same[:, s.b, u, :], msg[:, s.b, u, :], start=True, stop=True).then_inc(summed[s.b], 1)
                if nxt:
                    hid_product(nxt, 5)
            run_steps(pe, of, 1, 0, body)

        @block.scalar
        def _(act):
            act.wait_ge(start, 1)

            def relu(n, m):
                act.wait_ge(hid_summed[n.b], 2 * n.i + m + 1)
                act.wait_ge(msg_summed[n.b], 2 * n.i)
                c = g.mlp_cols[t] + m
                act.activation(hidT[:, n.b, m, :], ps_h[m][:, :], ACT.Relu, bias=g.col[:, c:c + 1]).then_inc(hid_done[n.b], 1)

            def read(s, u):
                act.wait_ge(summed[s.b], QUAD * s.i + u + 1)
                act.wait_ge(scattered[s.b][u], 16 * s.i)
                act.copy(res[:, s.b, u, :], sums[u]).then_inc(read_out[s.b], 1)

            def body(s):
                nxt, here, before = s.at(1), s.at(0), s.at(-1)
                if nxt:
                    act.wait_ge(src_turned[nxt.b], nxt.i + 1)
                    act.wait_ge(hid_summed[nxt.b], 2 * nxt.i)
                    act.copy(srcT[:, nxt.b, :], ps_s[:, :]).then_inc(srcT_done[nxt.b], 1)
                for u in range(QUAD):
                    if here:
                        if u % 2 == 0:
                            act.wait_ge(msg_done[s.b], 2 * s.i + u // 2 + 1)
                        if u:
                            act.wait_ge(summed[s.b], QUAD * s.i + u)
                        elif before:
                            act.wait_ge(summed[before.b], QUAD * before.i + QUAD)
                        act.copy(msg[0:1, s.b, u, :], sums[(u - 1) % QUAD][LAST_SLOT:LAST_SLOT + 1, :]).then_inc(carried[s.b], 1)
                    if u and here:
                        read(s, u - 1)
                    elif u == 0 and before:
                        read(before, QUAD - 1)
                    if nxt and u == 1:
                        relu(nxt, 0)
                if nxt:
                    relu(nxt, 1)
            run_steps(act, of, 1, 1, body)

        @block.vector
        def _(dve):
            dve.memset(sums[QUAD - 1], 0.0).then_inc(start, 1)

            def body(s):
                nxt, here = s.at(1), s.at(0)
                if nxt:
                    dve.wait_ge(dst_turned[nxt.b], nxt.i + 1)
                    dve.wait_ge(hid_summed[nxt.b], 2 * nxt.i)
                    dve.tensor_copy(dstT[:, nxt.b, :], ps_d[:, :]).then_inc(dstT_done[nxt.b], 1)
                if here:
                    dve.wait_ge(summed[s.b], QUAD * s.i)
                    for pair in range(2):
                        u = slice(2 * pair, 2 * pair + 2)
                        dve.wait_ge(msg_summed[s.b], 2 * s.i + pair + 1)
                        dve.tensor_tensor(msg[:, s.b, u, :], ps_msg[:, u, :],
                                          g.w["mb2"][:, t, :].unsqueeze(1).broadcast_to([P, 2, wide]), ALU.add).then_inc(msg_done[s.b], 1)
                if nxt:
                    dve.wait_ge(drow_here[nxt.b], 16 * nxt.i + 16)
                    dve.wait_ge(summed[nxt.b], QUAD * nxt.i)
                    for u in range(QUAD):
                        dve.tensor_scalar(same[:, nxt.b, u, :], drow[:, nxt.b, u, :], g.dcol[:, ds(nxt.n * QUAD + u, 1)], None,
                                          ALU.is_equal).then_inc(same_done[nxt.b], 1)
            run_steps(dve, of, 1, 0, body)


def gated_update(nc, g, t, hv, into, last_round):
    with Phase(nc, f"gru{t}") as ph:
        v_in, a_in = ph.sb("v_in", [P, 2, QUAD, P]), ph.sb("a_in", [P, 2, QUAD, 2 * P])
        vT, aT = ph.sb("vT", [P, 2, GROUP]), ph.sb("aT", [P, 2, 2, GROUP])
        reset, update, cand_h, cand_s, cand, diff, part, newT = (ph.sb(n, [P, 2, GROUP]) for n in (
            "reset", "update", "cand_h", "cand_s", "cand", "diff", "part", "newT"))
        x_in, value, new = (ph.sb(n, [P, 2, QUAD, P]) for n in ("x_in", "value", "new"))
        minus_half = ph.sb("minus_half", [P, 2 * QUAD])
        ps_v, ps_a, ps_out = ph.ps("ps_v"), [ph.ps(f"ps_a{k}") for k in range(2)], ph.ps("ps_out")
        ps_r, ps_z, ps_h, ps_x = (ph.ps(n) for n in ("ps_r", "ps_z", "ps_h", "ps_x"))
        norm = Norm(ph, "norm")
        v_here, a_here, x_here, stored = (ph.sems(n) for n in ("v_here", "a_here", "x_here", "stored"))
        (v_turned, a_turned, vT_done, aT_done, r_summed, z_summed, h_summed, x_summed, reset_done, update_done, cand_h_done,
         cand_s_done, cand_done, diff_done, part_done, newT_done, new_turned, new_done, value_done) = (ph.sems(n) for n in (
             "v_turned", "a_turned", "vT_done", "aT_done", "r_summed", "z_summed", "h_summed", "x_summed", "reset_done",
             "update_done", "cand_h_done", "cand_s_done", "cand_done", "diff_done", "part_done", "newT_done", "new_turned",
             "new_done", "value_done"))
        sp_turn, consts = ph.sem("sp_turn"), ph.sem("consts")
        block = ph.block()
        of = g.groups
        lag = 2

        @block.sync
        def _(sp):
            def body(s):
                if l := s.at(2):
                    hold(sp, sp_turn, v_turned[l.b], l.i)
                    sp.dma_start(v_in[:, l.b, :, :], group_rows(hv, l.n)).then_inc(v_here[l.b], 16)
                    hold(sp, sp_turn, a_turned[l.b], 2 * l.i)
                    sp.dma_start(a_in[:, l.b, :, :], group_rows(g.seg, l.n, 2 * P)).then_inc(a_here[l.b], 16)
                if last_round and s.at(0):
                    hold(sp, sp_turn, value_done[s.b], s.i)
                    sp.dma_start(x_in[:, s.b, :, :], group_rows(g.x3, s.n)).then_inc(x_here[s.b], 16)
                if r := s.at(-lag):
                    hold(sp, sp_turn, new_done[r.b], r.i + 1)
                    sp.dma_start(group_rows(into, r.n), new[:, r.b, :, :]).then_inc(stored[r.b], 16)
            run_steps(sp, of, 2, lag, body)
            for b in range(2):
                sp.wait_ge(stored[b], 16 * (of // 2))

        @block.tensor
        def _(pe):
            wih, whh = g.w["wih"], g.w["whh"]

            def body(s):
                if n := s.at(1):
                    q = n.at(-1)
                    pe.wait_ge(v_here[n.b], 16 * n.i + 16)
                    if q:
                        pe.wait_ge(vT_done[q.b], q.i + 1)
                    turn_group(pe, ps_v, v_in, n, g.ident, v_turned)
                    pe.wait_ge(a_here[n.b], 16 * n.i + 16)
                    if q:
                        pe.wait_ge(aT_done[q.b], 2 * q.i + 2)
                    for k in range(2):
                        for j in range(QUAD):
                            turned = pe.transpose(ps_a[k][:, j * P:(j + 1) * P], a_in[:, n.b, j, k * P:(k + 1) * P], g.ident[:, :])
                        turned.then_inc(a_turned[n.b], 1)
                if s.at(0):
                    pe.wait_ge(vT_done[s.b], s.i + 1)
                    pe.wait_ge(aT_done[s.b], 2 * s.i + 2)
                    q = s.at(-1)
                    for bank, gate, free, done in ((ps_r, 0, reset_done, r_summed), (ps_z, 1, update_done, z_summed)):
                        c = slice(gate * P, (gate + 1) * P)
                        if q:
                            pe.wait_ge(free[q.b], q.i + 1)
                        pe.matmul(bank[:, :], whh[:, t, c], vT[:, s.b, :], start=True, stop=False)
                        pe.matmul(bank[:, :], wih[:, t, 0, c], aT[:, s.b, 0, :], start=False, stop=False)
                        pe.matmul(bank[:, :], wih[:, t, 1, c], aT[:, s.b, 1, :], start=False, stop=True).then_inc(done[s.b], 1)
                        if gate == 0:
                            if q:
                                pe.wait_ge(cand_h_done[q.b], q.i + 1)
                            pe.matmul(ps_h[:, :], whh[:, t, 2 * P:], vT[:, s.b, :], start=True, stop=True).then_inc(h_summed[s.b], 1)
                    if q:
                        pe.wait_ge(cand_s_done[q.b], q.i + 1)
                    pe.matmul(ps_x[:, :], wih[:, t, 0, 2 * P:], aT[:, s.b, 0, :], start=True, stop=False)
                    pe.matmul(ps_x[:, :], wih[:, t, 1, 2 * P:], aT[:, s.b, 1, :], start=False, stop=True).then_inc(x_summed[s.b], 1)
                if r := s.at(-1):
                    pe.wait_ge(newT_done[r.b], r.i + 1)
                    if q := r.at(-1):
                        pe.wait_ge((value_done if last_round else new_done)[q.b], q.i + 1)
                    for j in range(QUAD):
                        turned = pe.transpose(ps_out[:, j * P:(j + 1) * P], newT[:, r.b, j * P:(j + 1) * P], g.ident[:, :])
                    turned.then_inc(new_turned[r.b], 1)
            run_steps(pe, of, 1, 1, body)

        @block.scalar
        def _(act):
            bias = g.gate_bias

            def body(s):
                if n := s.at(1):
                    act.wait_ge(v_turned[n.b], n.i + 1)
                    act.wait_ge(diff_done[n.b], n.i)
                    act.copy(vT[:, n.b, :], ps_v[:, :]).then_inc(vT_done[n.b], 1)
                if s.at(0):
                    act.wait_ge(r_summed[s.b], s.i + 1)
                    act.wait_ge(cand_h_done[s.b], s.i)
                    act.activation(reset[:, s.b, :], ps_r[:, :], ACT.Sigmoid, bias=bias[:, t, 0:1]).then_inc(reset_done[s.b], 1)
                    act.wait_ge(z_summed[s.b], s.i + 1)
                    act.wait_ge(part_done[s.b], s.i)
                    act.activation(update[:, s.b, :], ps_z[:, :], ACT.Sigmoid, bias=bias[:, t, 1:2]).then_inc(update_done[s.b], 1)
                    act.wait_ge(cand_s_done[s.b], s.i + 1)
                    act.wait_ge(newT_done[s.b], s.i)
                    act.activation(cand[:, s.b, :], cand_s[:, s.b, :], ACT.Tanh, bias=bias[:, t, 2:3]).then_inc(cand_done[s.b], 1)
                if last_round:
                    if r := s.at(-2):
                        act.wait_ge(stored[r.b], 16 * r.i)
                        norm.apply(act, r, new, value, new_done)
                else:
                    if r := s.at(-1):
                        act.wait_ge(new_turned[r.b], r.i + 1)
                        act.wait_ge(stored[r.b], 16 * r.i)
                        act.copy(flat(new, r.b), ps_out[:, :]).then_inc(new_done[r.b], 1)
            run_steps(act, of, 1, 2, body)

        @block.gpsimd
        def _(pool):
            power_constants(ph, pool, minus_half, consts)

            def body(s):
                if s.at(0):
                    pool.wait_ge(cand_done[s.b], s.i + 1)
                    pool.wait_ge(part_done[s.b], s.i)
                    pool.tensor_tensor(diff[:, s.b, :], vT[:, s.b, :], cand[:, s.b, :], ALU.subtract).then_inc(diff_done[s.b], 1)
                    pool.wait_ge(diff_done[s.b], s.i + 1)
                    pool.wait_ge(newT_done[s.b], s.i)
                    pool.tensor_tensor(part[:, s.b, :], diff[:, s.b, :], update[:, s.b, :], ALU.mult).then_inc(part_done[s.b], 1)
                if last_round:
                    if r := s.at(-1):
                        norm.deviation(pool, r, minus_half)
            run_steps(pool, of, 0, 1, body)

        @block.vector
        def _(dve):
            bias = g.gate_bias

            def body(s):
                if n := s.at(1):
                    for k in range(2):
                        dve.wait_ge(a_turned[n.b], 2 * n.i + k + 1)
                        dve.wait_ge(x_summed[n.b], n.i)
                        dve.tensor_copy(aT[:, n.b, k, :], ps_a[k][:, :]).then_inc(aT_done[n.b], 1)
                if s.at(0):
                    dve.wait_ge(h_summed[s.b], s.i + 1)
                    dve.wait_ge(reset_done[s.b], s.i + 1)
                    dve.scalar_tensor_tensor(cand_h[:, s.b, :], ps_h[:, :], bias[:, t, 3:4], reset[:, s.b, :],
                                             ALU.add, ALU.mult).then_inc(cand_h_done[s.b], 1)
                    dve.wait_ge(x_summed[s.b], s.i + 1)
                    dve.wait_ge(cand_h_done[s.b], s.i + 1)
                    dve.wait_ge(cand_done[s.b], s.i)
                    dve.tensor_tensor(cand_s[:, s.b, :], ps_x[:, :], cand_h[:, s.b, :], ALU.add).then_inc(cand_s_done[s.b], 1)
                if last_round:
                    if r := s.at(-1):
                        dve.wait_ge(new_turned[r.b], r.i + 1)
                        dve.wait_ge(x_here[r.b], 16 * r.i + 16)
                        dve.wait_ge(new_done[r.b], r.i)
                        dve.tensor_tensor(flat(value, r.b), ps_out[:, :], flat(x_in, r.b), ALU.add).then_inc(value_done[r.b], 1)
                    if r := s.at(-2):
                        norm.offset_of(dve, r)
                    if r := s.at(-1):
                        dve.wait_ge(value_done[r.b], r.i + 1)
                        norm.stats_of(dve, r, value[:, r.b, :, :])
                        norm.moments_of(dve, r)
                if s.at(0):
                    dve.wait_ge(part_done[s.b], s.i + 1)
                    dve.wait_ge(new_turned[s.b], s.i)
                    dve.tensor_tensor(newT[:, s.b, :], part[:, s.b, :], cand[:, s.b, :], ALU.add).then_inc(newT_done[s.b], 1)
            run_steps(dve, of, 1, 2, body)


class Graph:
    pass


def build(nc, d, out, nodes, upto=99):
    g = Graph()
    g.nodes = nodes
    g.groups = d["x"].shape[0] // GROUP
    g.ntp = d["srcw"].shape[1]
    g.quads = g.ntp // QUAD - 2
    g.rounds = d["mlp_w1"].shape[0]
    np_ = d["x"].shape[0]
    g.x, g.drow, g.order, g.edge, g.edge_t, g.out = d["x"], d["drow"], d["order"], d["edge"], d["edge_t"], out
    with ExitStack() as stack:
        def sb(name, shape, dt=F32):
            return stack.enter_context(nc.sbuf_tensor(name, list(shape), dt))

        def table(name, width):
            return nc.dram_tensor(name, (np_, width), F32).ap()

        g.seg, g.gat = table("seg", 2 * P), table("gat", AUG)
        g.h1, g.x1, g.th, g.ta = table("h1", P), table("x1", P), table("th", P), table("ta", 2 * HEADS)
        g.x2, g.x3, g.x4 = table("x2", P), table("x3", P), table("x4", P)
        g.ident, g.ones = sb("ident", [P, P]), sb("ones", [1, P])
        g.srcw, g.dstw = sb("srcw_s", [P, g.ntp], I32), sb("dst_rows", [P, g.ntp], I32)
        g.at_node, g.at_left = sb("at_node", [P, g.ntp], I32), sb("at_left", [P, g.ntp], I32)
        g.dcol = sb("dcol", [P, g.ntp])
        g.w = {n: sb(f"w_{n}", [P, P]) for n in ("W1lT", "W1rT", "W2lT", "W2rT", "linT", "projT", "W2", "W3")}
        g.w["attT"] = sb("w_attT", [P, 2 * HEADS])
        g.w["W1"] = sb("w_W1", [P, 2, P])
        g.w["mw1"] = sb("w_mw1", [P, g.rounds, 2, 2 * P])
        g.w["mw1e"] = sb("w_mw1e", [d["mlp_w1"].shape[1] - 2 * P, g.rounds, 2 * P])
        g.w["mw2"] = sb("w_mw2", [P, g.rounds, 2, 2 * P])
        g.w["mb2"] = sb("w_mb2", [P, g.rounds, 2 * P])
        g.w["wih"] = sb("w_wih", [P, g.rounds, 2, 3 * P])
        g.w["whh"] = sb("w_whh", [P, g.rounds, 3 * P])
        g.rows = ("b1l", "b2l", "proj_b", "ln1_gamma", "ln1_beta", "b3", "ln2_gamma", "ln2_beta")
        g.row = {n: sb(f"row_{n}", [P, GROUP]) for n in g.rows}
        g.ncols = d["cols"].shape[1]
        g.col = sb("cols_s", [P, g.ncols])
        g.mlp_cols = [3 + 8 * r for r in range(g.rounds)]
        g.gate_cols = [5 + 8 * r for r in range(g.rounds)]
        g.gate_bias = sb("gate_bias", [P, g.rounds, 4])
        halves = g.seg.rearrange("n (c d) -> (n c) d", d=P)
        prepare(nc, g, d)
        if upto >= 1:
            edge_sums(nc, g, "sage1", g.at_node, g.seg, g.x, linear=g.edge, mean=True, clear=g.gat)
        if upto >= 2:
            sage_hidden(nc, g)
        if upto >= 3:
            edge_sums(nc, g, "sage2", g.at_left, halves, g.h1, mean=True)
        if upto >= 4:
            sage_out(nc, g)
        with ExitStack() as inner:
            slots = g.ntp * HEADS
            g.score, g.weight, g.peak = (inner.enter_context(nc.sbuf_tensor(n, [P, slots], F32)) for n in ("score", "weight", "peak"))
            if upto >= 5:
                edge_scores(nc, g)
                edge_softmax(nc, g)
            if upto >= 6:
                edge_sums(nc, g, "gat", g.at_node, g.gat, g.th, weights=(g.weight, g.peak))
        if upto >= 7:
            gat_out(nc, g)
        if upto >= 8:
            edge_mlp(nc, g)
        if upto >= 9:
            messages(nc, g, 0, g.x3)
        if upto >= 10:
            gated_update(nc, g, 0, g.x3, g.x4, False)
        if upto >= 11:
            messages(nc, g, 1, g.x4)
            gated_update(nc, g, 1, g.x4, out, True)


def arrange(inputs):
    import numpy as np
    a = {k: np.asarray(v) for k, v in inputs.items()}
    nodes, edges = a["x"].shape[0], a["src"].shape[0]
    tiles = -(-edges // EDGES_PER_TILE)
    quads = 2 * -(-tiles // (2 * QUAD))
    ntp = QUAD * (quads + 2)
    place = np.arange(P)
    place[[LAST_SLOT, P - 1]] = place[[P - 1, LAST_SLOT]]
    inorder = np.arange(ntp)[:, None] * EDGES_PER_TILE + np.arange(P)[None, :]
    slots = inorder[:, place]

    def padded(v, fill):
        p = np.full((inorder.max() + 2,) + v.shape[1:], fill, v.dtype)
        p[1:1 + edges] = v
        return p
    src, dst = padded(a["src"], 0), padded(a["dst"], -1)
    d = {}
    rows = -(-nodes // (2 * GROUP)) * 2 * GROUP
    d["x"] = np.zeros((rows, P), np.float32)
    d["x"][:nodes] = a["x"]
    d["srcw"], d["dstw"] = src[slots].T, dst[slots].T
    nxt = dst[slots + 1].T.copy()
    nxt[0] = d["dstw"][0]
    d["nxtw"] = nxt
    d["drow"] = dst[slots].reshape(1, -1)
    d["order"] = dst[inorder[:quads * QUAD]].reshape(CHUNKS, -1)
    d["edge"] = padded(a["edge_attr_128"], 0)[slots].reshape(-1, P)
    d["edge_t"] = padded(a["edge_attr_26"], 0)[slots].reshape(ntp * P, -1).T
    for k, n in (("W1lT", "L0_gnn_W1l"), ("W1rT", "L0_gnn_W1r"), ("W2lT", "L0_gnn_W2l"), ("W2rT", "L0_gnn_W2r"),
                 ("linT", "L1_gnn_lin_w"), ("projT", "L1_gnn_proj_w")):
        d[k] = a[n].T
    d["lin_w"] = a["L1_gnn_lin_w"]
    d["W1"], d["W2"], d["W3"] = a["L2_gnn_W1"], a["L2_gnn_W2"], a["L2_gnn_W3"]
    d["att_src"], d["att_dst"] = a["L1_gnn_att_src"].reshape(P, 1), a["L1_gnn_att_dst"].reshape(P, 1)
    d["head_of"] = np.repeat(np.eye(HEADS, dtype=np.float32), HEAD_DIM, axis=0)
    d["ident"] = np.eye(P, dtype=np.float32)
    for k, n in (("b1l", "L0_gnn_b1l"), ("b2l", "L0_gnn_b2l"), ("proj_b", "L1_gnn_proj_b"),
                 ("ln1_gamma", "L1_gnn_ln_gamma"), ("ln1_beta", "L1_gnn_ln_beta"), ("b3", "L2_gnn_b3"),
                 ("ln2_gamma", "L2_gnn_gamma"), ("ln2_beta", "L2_gnn_beta")):
        d[k] = a[n].reshape(1, P)
    cols = [a["L1_gnn_gat_bias"], a["L2_gnn_b1"], a["L2_gnn_b2"]]
    for r in range(a["L3_gnn_mlp_w1"].shape[0]):
        cols += [*a["L3_gnn_mlp_b1"][r].reshape(2, P), *a["L3_gnn_gru_bih"][r].reshape(3, P),
                 *a["L3_gnn_gru_bhh"][r].reshape(3, P)]
    d["cols"] = np.stack(cols, axis=1)
    d["mlp_w1"], d["mlp_w2"], d["mlp_b2"] = a["L3_gnn_mlp_w1"], a["L3_gnn_mlp_w2"], a["L3_gnn_mlp_b2"]
    d["wihT"], d["whhT"] = a["L3_gnn_gru_wih"].transpose(0, 2, 1), a["L3_gnn_gru_whh"].transpose(0, 2, 1)
    return {k: np.ascontiguousarray(v) for k, v in d.items()}, nodes


def kernel(**inputs):
    import concourse.bacc as bacc
    from concourse.bass_utils import run_bass_kernel_spmd

    arrays, nodes = arrange(inputs)
    nc = bacc.Bacc("TRN2", target_bir_lowering=False, num_devices=1)
    d = {k: nc.dram_tensor(f"in_{k}", v.shape, mybir.dt.from_np(v.dtype), kind="ExternalInput").ap()
         for k, v in arrays.items()}
    out = nc.dram_tensor("out", arrays["x"].shape, F32, kind="ExternalOutput").ap()
    build(nc, d, out, nodes)
    r = run_bass_kernel_spmd(nc, [{f"in_{k}": v for k, v in arrays.items()}], core_ids=[0])
    return r.results[0]["out"][:nodes]
```

```python
from contextlib import ExitStack

import concourse.bass as bass
from concourse import mybir
from concourse.bass import ds

F32 = mybir.dt.float32
I32 = mybir.dt.int32
ALU = mybir.AluOpType
ACT = mybir.ActivationFunctionType

P = 128
EDGES_PER_TILE = P - 1
LAST_SLOT = 32
QUAD = 4
GROUP = QUAD * P
HEADS, HEAD_DIM = 8, 16
CHUNKS = 8
EPS = 1e-5
SLOPE = 0.2
SKIP = 1.0e6
LOW = -1.0e30
AUG = 144


class Step:

    def __init__(self, i, b, of):
        self.i, self.b, self.of = i, b, of

    def at(self, k):
        i, b = self.i + (self.b + k) // 2, (self.b + k) % 2
        if isinstance(i, int) and not 0 <= 2 * i + b < self.of:
            return None
        return Step(i, b, self.of)

    @property
    def n(self):
        return 2 * self.i + self.b


def run_steps(eng, of, before, after, body):
    lo = (after + 1) // 2 + 1
    hi = (of - before) // 2
    for n in range(-before, 2 * lo):
        body(Step(n // 2, n % 2, of))
    with eng.Fori(lo, hi) as i:
        body(Step(i, 0, of))
        body(Step(i, 1, of))
    for n in range(2 * hi, of + after):
        body(Step(n // 2, n % 2, of))


class Phase:

    def __init__(self, nc, name):
        self.nc, self.name, self.stack, self.held = nc, name, ExitStack(), []

    def __enter__(self):
        return self

    def __exit__(self, *e):
        self.stack.__exit__(*e)
        self.nc.clear_and_free_semaphores(self.held)
        self.nc.all_engine_barrier()

    def sb(self, name, shape, dt=F32):
        return self.stack.enter_context(self.nc.sbuf_tensor(f"{self.name}_{name}", list(shape), dt))

    def ps(self, name, shape=(P, 512)):
        return self.stack.enter_context(self.nc.psum_tensor(f"{self.name}_{name}", list(shape), F32))

    def sem(self, name):
        self.held.append(self.nc.alloc_semaphore(f"{self.name}_{name}"))
        return self.held[-1]

    def sems(self, name, n=2):
        return [self.sem(f"{name}{k}") for k in range(n)]

    def block(self):
        return self.stack.enter_context(self.nc.Block())


def group_rows(table, n, width=P, at=0):
    rows = table[ds(n * GROUP, GROUP), :].rearrange("(p j) d -> p j d", j=QUAD)
    return rows if width is None else rows[:, :, at:at + width]


def hold(eng, turn, sem, value):
    eng.wait_ge(sem, value)
    eng.sem_inc(turn, 1)


def clear_table(eng, table, zeros, cleared):
    rows, width = table.shape
    per = rows // P
    flat = table.rearrange("(p a) d -> p (a d)", p=P)
    starts = range(0, per * width, zeros.shape[1])
    for a in starts:
        z = min(a + zeros.shape[1], per * width)
        eng.dma_start(flat[:, a:z], zeros[:, 0:z - a]).then_inc(cleared, 16)
    return len(starts)


def prepare(nc, g, d):
    with Phase(nc, "prep") as ph:
        loaded = ph.sem("loaded")
        zeros = ph.sb("zeros", [P, 4096])
        zeroed, cleared = ph.sem("zeroed"), ph.sem("cleared")
        dstw, nxtw = ph.sb("dstw", [P, g.ntp], I32), ph.sb("nxtw", [P, g.ntp], I32)
        skip = ph.sb("skip", [P, g.ntp])
        target = ph.sb("target", [P, g.ntp])
        att = ph.sb("att", [P, 2])
        head_of = ph.sb("head_of", [P, HEADS])
        att_mat = ph.sb("att_mat", [P, 2 * HEADS])
        lin = ph.sb("lin", [P, P])
        psum = ph.ps("psum")
        index_step = ph.sem("index_step")
        att_done, prod_done = ph.sem("att_done"), ph.sem("prod_done")
        block = ph.block()

        loads = [(dstw[:, :], d["dstw"]), (nxtw[:, :], d["nxtw"]), (g.srcw[:, :], d["srcw"]),
                 (att[:, 0:1], d["att_src"]), (att[:, 1:2], d["att_dst"]),
                 (head_of[:, :], d["head_of"]), (lin[:, :], d["lin_w"]), (g.ident[:, :], d["ident"])]
        for name in ("W1lT", "W1rT", "W2lT", "W2rT", "projT", "W2", "W3"):
            loads.append((g.w[name][:, :], d[name]))
        loads.append((g.w["linT"][:, :], d["linT"]))
        loads.append((g.w["W1"][:, :, :], d["W1"].rearrange("(c p) n -> p c n", p=P)))
        for r in range(g.rounds):
            loads.append((g.w["mw1"][:, r, :, :], d["mlp_w1"][r, 0:2 * P, :].rearrange("(c p) n -> p c n", p=P)))
            loads.append((g.w["mw1e"][:, r, :], d["mlp_w1"][r, 2 * P:, :]))
            loads.append((g.w["mw2"][:, r, :, :], d["mlp_w2"][r].rearrange("(c p) n -> p c n", p=P)))
            loads.append((g.w["wih"][:, r, :, :], d["wihT"][r].rearrange("(c p) n -> p c n", p=P)))
            loads.append((g.w["whh"][:, r, :], d["whhT"][r]))
            loads.append((g.w["mb2"][:, r, :], d["mlp_b2"][r:r + 1, :].broadcast_to([P, 2 * P])))
        for name in g.rows:
            for j in range(QUAD):
                loads.append((g.row[name][:, j * P:(j + 1) * P], d[name].broadcast_to([P, P])))
        loads.append((g.col[:, 0:g.ncols], d["cols"]))

        @block.sync
        def _(sp):
            for dst, src in loads:
                sp.dma_start(dst, src).then_inc(loaded, 16)
            sp.wait_ge(loaded, 16 * len(loads))

        @block.scalar
        def _(act):
            act.wait_ge(zeroed, 1)
            transfers = clear_table(act, g.seg, zeros, cleared)
            act.wait_ge(cleared, 16 * transfers)

        @block.vector
        def _(dve):
            dve.memset(zeros[:, :], 0.0).then_inc(zeroed, 1)
            dve.memset(g.ones[:, :], 1.0)
            dve.wait_ge(loaded, 16 * len(loads))
            dve.tensor_copy(g.dcol[:, :], dstw[:, :]).then_inc(index_step, 1)
            dve.tensor_tensor(skip[:, :], dstw[:, :], nxtw[:, :], ALU.is_equal).then_inc(index_step, 1)
            dve.wait_ge(index_step, 2)
            dve.scalar_tensor_tensor(target[:, :], skip[:, :], SKIP, g.dcol[:, :], ALU.mult, ALU.add).then_inc(index_step, 1)
            dve.wait_ge(index_step, 3)
            dve.tensor_copy(g.at_node[:, :], target[:, :])
            dve.tensor_scalar(g.at_left[:, :], target[:, :], 2.0, None, ALU.mult)
            dve.tensor_scalar(g.dstw[:, :], g.dcol[:, :], 0.0, None, ALU.max)
            dve.tensor_scalar(att_mat[:, 0:HEADS], head_of[:, :], att[:, 0:1], None, ALU.mult)
            dve.tensor_scalar(att_mat[:, HEADS:], head_of[:, :], att[:, 1:2], None, ALU.mult).then_inc(att_done, 1)
            for r in range(g.rounds):
                c = g.gate_cols[r]
                dve.tensor_tensor(g.gate_bias[:, r, 0:2], g.col[:, c:c + 2], g.col[:, c + 3:c + 5], ALU.add)
                dve.tensor_copy(g.gate_bias[:, r, 2:3], g.col[:, c + 2:c + 3])
                dve.tensor_copy(g.gate_bias[:, r, 3:4], g.col[:, c + 5:c + 6])
            dve.wait_ge(prod_done, 1)
            dve.tensor_copy(g.w["attT"][:, :], psum[:, 0:2 * HEADS])

        @block.tensor
        def _(pe):
            pe.wait_ge(att_done, 1)
            pe.matmul(psum[:, 0:2 * HEADS], lin[:, :], att_mat[:, :], start=True, stop=True).then_inc(prod_done, 1)


def store_quad(sp, kept, s, rows, stored):
    sp.dma_start(kept[ds(s.n * GROUP, GROUP), :].rearrange("(u p) d -> p u d", p=P), rows[:, s.b, :, 0:P]).then_inc(stored[s.b], 16)


def edge_sums(nc, g, name, target_index, target, gather=None, kept=None, linear=None, mean=False, weights=None, side=None):
    width = 2 * P if linear is not None else P
    cols = width + (1 if mean else 0) + (HEADS if weights else 0)
    out_cols = AUG if weights else width
    bound = g.nodes * (target.shape[0] // g.x.shape[0])
    with Phase(nc, name) as ph:
        src_ix, tgt_ix = ph.sb("src_ix", [P, 2, QUAD], I32), ph.sb("tgt_ix", [P, 2, QUAD], I32)
        drow = ph.sb("drow", [P, 2, QUAD, P], I32)
        msg = ph.sb("msg", [P, 2, QUAD, cols])
        raw = ph.sb("raw", [P, 2, QUAD, P]) if weights else msg
        same = ph.sb("same", [P, 2, QUAD, P])
        res = ph.sb("res", [P, 2, QUAD, out_cols])
        share = ph.sb("share", [P, 2, QUAD])
        count = ph.sb("count", [P, 2, QUAD])
        plain = ph.sb("plain", [P, 2, QUAD, cols if mean else 1])
        sums = ph.ps("sums", [P, QUAD, 512])
        if side is not None:
            source, weight, bias_row, residual, into = side
            side_in, side_res, side_out = (ph.sb(n, [P, 2, 2, QUAD, P]) for n in ("side_in", "side_res", "side_out"))
            side_sum, side_T = ph.sb("side_sum", [P, 2, GROUP]), ph.sb("side_T", [P, 2, GROUP])
            ps_turn, ps_prod = [ph.ps(f"ps_turn{k}") for k in range(2)], [ph.ps(f"ps_prod{k}") for k in range(2)]
        in_here, res_here, side_stored = ph.sems("in_here"), ph.sems("res_here"), ph.sems("side_stored")
        turned, side_T_done, produced = ph.sems("turned"), ph.sems("side_T_done"), ph.sems("produced")
        biased_done, side_done = ph.sems("biased_done"), ph.sems("side_done")
        src_here, tgt_here, drow_here = ph.sems("src_here"), ph.sems("tgt_here"), ph.sems("drow_here")
        edge_here = ph.sems("edge_here")
        rows_here = [ph.sems(f"rows_here{b}_", QUAD) for b in range(2)]
        scattered = [ph.sems(f"scattered{b}_", QUAD) for b in range(2)]
        same_done, msg_done, carried = ph.sems("same_done"), ph.sems("msg_done"), ph.sems("carried")
        summed, share_done, res_done = ph.sems("summed"), ph.sems("share_done"), ph.sems("res_done")
        read_out, maxima_done = ph.sems("read_out"), ph.sems("maxima_done")
        start = ph.sem("start")
        pool_turn, sp_turn = ph.sem("pool_turn"), ph.sem("sp_turn")
        block = ph.block()
        of = g.quads
        assert side is None or 2 * ((of - 1) // 2) <= g.groups // 2 <= of

        def job(s):
            return s if side is not None and s and (not isinstance(s.i, int) or s.n < g.groups // 2) else None

        def wait_rows(eng, s, u):
            eng.wait_ge(rows_here[s.b][u if gather is not None else 0], 16 * s.i + 16)

        def load_quad(sp, s, which):
            if which == "src" and gather is not None:
                sp.dma_start(src_ix[:, s.b, :], g.srcw[:, ds(s.n * QUAD, QUAD)]).then_inc(src_here[s.b], 16)
            if which == "tgt":
                sp.dma_start(tgt_ix[:, s.b, :], target_index[:, ds(s.n * QUAD, QUAD)]).then_inc(tgt_here[s.b], 16)
            if which == "drow":
                sp.dma_start(drow[:, s.b, :, :].rearrange("p t e -> p (t e)"),
                             g.drow[:, ds(s.n * GROUP, GROUP)].broadcast_to([P, GROUP])).then_inc(drow_here[s.b], 16)
            if which == "kept" and kept is not None:
                sp.dma_start(raw[:, s.b, :, 0:P], kept[ds(s.n * GROUP, GROUP), :].rearrange("(u p) d -> p u d", p=P)
                             ).then_inc(rows_here[s.b][0], 16)
            if which == "edge" and linear is not None:
                sp.dma_start(msg[:, s.b, :, P:2 * P], linear[ds(s.n * GROUP, GROUP), :].rearrange("(u p) d -> p u d", p=P)
                             ).then_inc(edge_here[s.b], 16)

        @block.sync
        def _(sp):
            def body(s):
                if gather is not None and (n := s.at(3)):
                    for u in range(QUAD):
                        hold(sp, sp_turn, rows_here[n.b][u], 16 * n.i)
                    load_quad(sp, n, "src")
                if n := s.at(2):
                    hold(sp, sp_turn, same_done[n.b], QUAD * n.i)
                    load_quad(sp, n, "drow")
                    if linear is not None or kept is not None:
                        hold(sp, sp_turn, summed[n.b], QUAD * n.i)
                        load_quad(sp, n, "kept")
                        load_quad(sp, n, "edge")
                if n := s.at(1):
                    for u in range(QUAD):
                        hold(sp, sp_turn, scattered[n.b][u], 16 * n.i)
                    load_quad(sp, n, "tgt")
                if n := job(s.at(2)):
                    hold(sp, sp_turn, turned[n.b], 2 * n.i)
                    for k in range(2):
                        sp.dma_start(side_in[:, n.b, k, :, :], group_rows(source, 2 * n.n + k)).then_inc(in_here[n.b], 16)
                    if residual is not None:
                        hold(sp, sp_turn, side_done[n.b], 2 * n.i)
                        for k in range(2):
                            sp.dma_start(side_res[:, n.b, k, :, :], group_rows(residual, 2 * n.n + k)).then_inc(res_here[n.b], 16)
                if r := job(s.at(-1)):
                    hold(sp, sp_turn, side_done[r.b], 2 * r.i + 2)
                    for k in range(2):
                        sp.dma_start(group_rows(into, 2 * r.n + k), side_out[:, r.b, k, :, :]).then_inc(side_stored[r.b], 16)
            run_steps(sp, of, 3, 1, body)
            if side is not None:
                for b in range(2):
                    sp.wait_ge(side_stored[b], 32 * ((g.groups // 2 + 1 - b) // 2))

        @block.gpsimd
        def _(pool):
            def fetch(s):
                hold(pool, pool_turn, src_here[s.b], 16 * s.i + 16)

            def fetch_tile(s, u):
                pool.indirect_dma_start(out=raw[:, s.b, u, 0:P], out_offset=None, in_=gather,
                                        in_offset=bass.IndirectOffsetOnAxis(ap=src_ix[:, s.b, u:u + 1], axis=0)
                                        ).then_inc(rows_here[s.b][u], 16)

            def body(s):
                if gather is not None and (n := s.at(1)):
                    fetch(n)
                    hold(pool, pool_turn, summed[n.b], QUAD * n.i)
                    for u in range(QUAD):
                        fetch_tile(n, u)
                if r := s.at(-1):
                    hold(pool, pool_turn, tgt_here[r.b], 16 * r.i + 16)
                    for u in range(QUAD):
                        hold(pool, pool_turn, (res_done if mean else read_out)[r.b], QUAD * r.i + u + 1)
                        if weights:
                            hold(pool, pool_turn, maxima_done[r.b], QUAD * r.i + u + 1)
                        pool.indirect_dma_start(out=target, out_offset=bass.IndirectOffsetOnAxis(ap=tgt_ix[:, r.b, u:u + 1], axis=0),
                                                in_=res[:, r.b, u, :], in_offset=None,
                                                bounds_check=bound - 1, oob_is_err=False).then_inc(scattered[r.b][u], 16)
            run_steps(pool, of, 1, 1, body)
            for b in range(2):
                for u in range(QUAD):
                    pool.wait_ge(scattered[b][u], 16 * (of // 2))

        @block.scalar
        def _(act):
            act.wait_ge(start, 1)

            def read(s, u):
                act.wait_ge(summed[s.b], QUAD * s.i + u + 1)
                if mean:
                    act.wait_ge(res_done[s.b], QUAD * s.i)
                    act.copy(plain[:, s.b, u, :], sums[:, u, 0:cols]).then_inc(read_out[s.b], 1)
                else:
                    act.wait_ge(scattered[s.b][u], 16 * s.i)
                    act.copy(res[:, s.b, u, 0:cols], sums[:, u, 0:cols]).then_inc(read_out[s.b], 1)

            def body(s):
                before, here = s.at(-1), s.at(0)
                for u in range(QUAD):
                    if here:
                        if linear is not None and u == 0:
                            act.wait_ge(edge_here[s.b], 16 * s.i + 16)
                        if weights:
                            act.wait_ge(msg_done[s.b], QUAD * s.i + u + 1)
                        else:
                            wait_rows(act, s, u)
                        if u:
                            act.wait_ge(summed[s.b], QUAD * s.i + u)
                        elif before:
                            act.wait_ge(summed[before.b], QUAD * before.i + QUAD)
                        act.copy(msg[0:1, s.b, u, :], sums[LAST_SLOT:LAST_SLOT + 1, (u - 1) % QUAD, 0:cols]).then_inc(carried[s.b], 1)
                    if u and here:
                        read(s, u - 1)
                    elif u == 0 and before:
                        read(before, QUAD - 1)
                if n := job(s.at(1)):
                    for k in range(2):
                        act.wait_ge(turned[n.b], 2 * n.i + k + 1)
                        if here:
                            act.wait_ge(produced[s.b], 2 * s.i + k + 1)
                        act.copy(side_T[:, k, :], ps_turn[k][:, :]).then_inc(side_T_done[n.b], 1)
            run_steps(act, of, 1, 1, body)

        @block.vector
        def _(dve):
            if mean:
                dve.memset(msg[:, :, :, width:width + 1], 1.0)
            dve.memset(sums[:, QUAD - 1, :], 0.0).then_inc(start, 1)

            def compare(s):
                dve.wait_ge(drow_here[s.b], 16 * s.i + 16)
                dve.wait_ge(summed[s.b], QUAD * s.i)
                for u in range(QUAD):
                    dve.tensor_scalar(same[:, s.b, u, :], drow[:, s.b, u, :], g.dcol[:, ds(s.n * QUAD + u, 1)], None,
                                      ALU.is_equal).then_inc(same_done[s.b], 1)

            def weigh(s):
                dve.wait_ge(summed[s.b], QUAD * s.i)
                for u in range(QUAD):
                    wait_rows(dve, s, u)
                    wts = weights[0][:, ds((s.n * QUAD + u) * HEADS, HEADS)]
                    dve.tensor_copy(msg[:, s.b, u, P:P + HEADS], wts)
                    dve.tensor_tensor(msg[:, s.b, u, 0:P].rearrange("p (h k) -> p h k", k=HEAD_DIM),
                                      raw[:, s.b, u, :].rearrange("p (h k) -> p h k", k=HEAD_DIM),
                                      wts.unsqueeze(2).broadcast_to([P, HEADS, HEAD_DIM]), ALU.mult).then_inc(msg_done[s.b], 1)

            def add_maxima(s):
                for u in range(QUAD):
                    dve.wait_ge(scattered[s.b][u], 16 * s.i)
                    dve.tensor_copy(res[:, s.b, u, cols:], weights[1][:, ds((s.n * QUAD + u) * HEADS, HEADS)]).then_inc(maxima_done[s.b], 1)

            def body(s):
                if n := s.at(1):
                    compare(n)
                    if weights:
                        weigh(n)
                if weights and s.at(0):
                    add_maxima(s)
                if c := job(s.at(0)):
                    dve.wait_ge(side_stored[c.b], 32 * c.i)
                    for k in range(2):
                        dve.wait_ge(produced[c.b], 2 * c.i + k + 1)
                        out = side_out[:, c.b, k, :, :].rearrange("p j d -> p (j d)")
                        if residual is None:
                            dve.tensor_tensor(out, ps_prod[k][:, :], bias_row[:, :], ALU.add).then_inc(side_done[c.b], 1)
                        else:
                            dve.tensor_tensor(side_sum[:, k, :], ps_prod[k][:, :], bias_row[:, :], ALU.add).then_inc(biased_done[c.b], 1)
                    if residual is not None:
                        dve.wait_ge(res_here[c.b], 32 * c.i + 32)
                        for k in range(2):
                            dve.wait_ge(biased_done[c.b], 2 * c.i + k + 1)
                            dve.tensor_tensor(side_out[:, c.b, k, :, :].rearrange("p j d -> p (j d)"), side_sum[:, k, :],
                                              side_res[:, c.b, k, :, :].rearrange("p j d -> p (j d)"), ALU.add).then_inc(side_done[c.b], 1)
                if mean and s.at(0):
                    dve.wait_ge(read_out[s.b], QUAD * s.i + QUAD)
                    dve.tensor_scalar(count[:, s.b, :], plain[:, s.b, :, width], 1.0, None, ALU.max).then_inc(share_done[s.b], 1)
                    dve.wait_ge(share_done[s.b], 2 * s.i + 1)
                    dve.reciprocal(share[:, s.b, :], count[:, s.b, :]).then_inc(share_done[s.b], 1)
                    dve.wait_ge(share_done[s.b], 2 * s.i + 2)
                    for u in range(QUAD):
                        dve.wait_ge(scattered[s.b][u], 16 * s.i)
                        if linear is not None:
                            dve.tensor_copy(res[:, s.b, u, P:], plain[:, s.b, u, P:2 * P])
                        dve.tensor_scalar(res[:, s.b, u, 0:P], plain[:, s.b, u, 0:P], share[:, s.b, u:u + 1], None,
                                          ALU.mult).then_inc(res_done[s.b], 1)
            run_steps(dve, of, 1, 0, body)

        @block.tensor
        def _(pe):
            def product(c, q, k):
                pe.wait_ge(side_T_done[c.b], 2 * c.i + k + 1)
                if q:
                    pe.wait_ge(side_done[q.b], 2 * q.i + k + 1)
                for j in range(QUAD):
                    columns = slice(j * P, (j + 1) * P)
                    last = pe.matmul(ps_prod[k][:, columns], side_T[:, k, columns], weight[:, :], start=True, stop=True)
                last.then_inc(produced[c.b], 1)

            def turn(n, k):
                pe.wait_ge(in_here[n.b], 32 * n.i + 32)
                for j in range(QUAD):
                    last = pe.transpose(ps_turn[k][:, j * P:(j + 1) * P], side_in[:, n.b, k, j, :], g.ident[:, :])
                last.then_inc(turned[n.b], 1)

            def body(s):
                here, before, nxt, cur = s.at(0), s.at(-1), job(s.at(1)), job(s.at(0))
                for u in range(QUAD):
                    if here:
                        if before:
                            pe.wait_ge(read_out[before.b], QUAD * before.i + u + 1)
                        pe.wait_ge(same_done[s.b], QUAD * s.i + u + 1)
                        pe.wait_ge(carried[s.b], QUAD * s.i + u + 1)
                        pe.matmul(sums[:, u, 0:cols], same[:, s.b, u, :], msg[:, s.b, u, :], start=True, stop=True
                                  ).then_inc(summed[s.b], 1)
                    if cur and u < 2:
                        product(cur, job(before), u)
                    if nxt and u >= 2:
                        turn(nxt, u - 2)
            run_steps(pe, of, 1, 0, body)


def sage_hidden(nc, g):
    with Phase(nc, "hid") as ph:
        p_in, m_in, h = (ph.sb(n, [P, 2, 2, QUAD, P]) for n in ("p_in", "m_in", "h"))
        mT, added = ph.sb("mT", [P, 2, 2, GROUP]), ph.sb("added", [P, 2, 2, GROUP])
        ps_m, ps_h = ([[ph.ps(f"{n}{b}_{k}") for k in range(2)] for b in range(2)] for n in ("ps_m", "ps_h"))
        p_here, m_here, stored = ph.sems("p_here"), ph.sems("m_here"), ph.sems("stored")
        m_turned, mT_done, sp_turn = ph.sems("m_turned"), ph.sems("mT_done"), ph.sem("sp_turn")
        h_summed, added_done, h_done = ph.sems("h_summed"), ph.sems("added_done"), ph.sems("h_done")
        block = ph.block()
        of = g.groups // 2

        @block.sync
        def _(sp):
            def body(s):
                if l := s.at(2):
                    hold(sp, sp_turn, m_turned[l.b], 2 * l.i)
                    for k in range(2):
                        sp.dma_start(m_in[:, l.b, k, :, :], group_rows(g.seg, 2 * l.n + k)).then_inc(m_here[l.b], 16)
                if l := s.at(1):
                    hold(sp, sp_turn, added_done[l.b], 2 * l.i)
                    for k in range(2):
                        sp.dma_start(p_in[:, l.b, k, :, :], group_rows(g.pre, 2 * l.n + k)).then_inc(p_here[l.b], 16)
                if r := s.at(-1):
                    hold(sp, sp_turn, h_done[r.b], 2 * r.i + 2)
                    for k in range(2):
                        sp.dma_start(group_rows(g.h1, 2 * r.n + k), h[:, r.b, k, :, :]).then_inc(stored[r.b], 16)
            run_steps(sp, of, 2, 1, body)
            for b in range(2):
                sp.wait_ge(stored[b], 32 * ((of + 1 - b) // 2))

        @block.tensor
        def _(pe):
            def body(s):
                for k in range(2):
                    if t := s.at(1):
                        pe.wait_ge(m_here[t.b], 32 * t.i + 32)
                        pe.wait_ge(mT_done[t.b], 2 * t.i)
                        for j in range(QUAD):
                            turned = pe.transpose(ps_m[t.b][k][:, j * P:(j + 1) * P], m_in[:, t.b, k, j, :], g.ident[:, :])
                        turned.then_inc(m_turned[t.b], 1)
                    if s.at(0):
                        pe.wait_ge(mT_done[s.b], 2 * s.i + k + 1)
                        pe.wait_ge(added_done[s.b], 2 * s.i)
                        for j in range(QUAD):
                            c = slice(j * P, (j + 1) * P)
                            last = pe.matmul(ps_h[s.b][k][:, c], mT[:, s.b, k, c], g.w["W1lT"][:, :], start=True, stop=True)
                        last.then_inc(h_summed[s.b], 1)
            run_steps(pe, of, 1, 0, body)

        @block.scalar
        def _(act):
            def body(s):
                for k in range(2):
                    if n := s.at(1):
                        act.wait_ge(m_turned[n.b], 2 * n.i + k + 1)
                        act.wait_ge(h_summed[n.b], 2 * n.i)
                        act.copy(mT[:, n.b, k, :], ps_m[n.b][k][:, :]).then_inc(mT_done[n.b], 1)
                    if r := s.at(-1):
                        act.wait_ge(added_done[r.b], 2 * r.i + k + 1)
                        act.wait_ge(stored[r.b], 32 * r.i)
                        act.activation(h[:, r.b, k, :, :].rearrange("p j d -> p (j d)"), added[:, r.b, k, :], ACT.Relu).then_inc(h_done[r.b], 1)
            run_steps(act, of, 1, 1, body)

        @block.vector
        def _(dve):
            def body(s):
                for k in range(2):
                    dve.wait_ge(h_summed[s.b], 2 * s.i + k + 1)
                    dve.wait_ge(p_here[s.b], 32 * s.i + 32)
                    dve.wait_ge(h_done[s.b], 2 * s.i)
                    dve.tensor_tensor(added[:, s.b, k, :], ps_h[s.b][k][:, :], p_in[:, s.b, k, :, :].rearrange("p j d -> p (j d)"),
                                      ALU.add).then_inc(added_done[s.b], 1)
            run_steps(dve, of, 0, 0, body)


class Norm:

    def __init__(self, ph, name):
        self.stats = ph.sb(f"{name}_stats", [P, 2, QUAD, 6])
        self.moments = ph.sb(f"{name}_moments", [P, 2, QUAD, 2])
        self.shifted = ph.sb(f"{name}_shifted", [P, 2, QUAD])
        self.rstd = ph.sb(f"{name}_rstd", [P, 2, QUAD])
        self.offset = ph.sb(f"{name}_offset", [P, 2, QUAD])
        self.dve_turn = ph.sem(f"{name}_dve_turn")
        self.offset_done = ph.sems(f"{name}_offset_done")
        self.stats_done = ph.sems(f"{name}_stats_done")
        self.moments_done = ph.sems(f"{name}_moments_done")
        self.shifted_done = ph.sems(f"{name}_shifted_done")
        self.rstd_done = ph.sems(f"{name}_rstd_done")

    def stats_of(self, dve, s, tiles):
        for j in range(QUAD):
            dve.bn_stats(self.stats[:, s.b, j, :], tiles[:, j, :]).then_inc(self.stats_done[s.b], 1)

    def moments_of(self, dve, s):
        dve.wait_ge(self.rstd_done[s.b], s.i)
        hold(dve, self.dve_turn, self.stats_done[s.b], QUAD * s.i + QUAD)
        for j in range(QUAD):
            dve.bn_aggr(self.moments[:, s.b, j, :], self.stats[:, s.b, j, :]).then_inc(self.moments_done[s.b], 1)

    def deviation(self, pool, s, minus_half):
        pool.wait_ge(self.moments_done[s.b], QUAD * s.i + QUAD)
        pool.tensor_tensor(self.shifted[:, s.b, :], self.moments[:, s.b, :, 1], minus_half[:, QUAD:], ALU.add).then_inc(self.shifted_done[s.b], 1)
        pool.wait_ge(self.shifted_done[s.b], s.i + 1)
        pool.tensor_tensor(self.rstd[:, s.b, :], self.shifted[:, s.b, :], minus_half[:, 0:QUAD], ALU.pow).then_inc(self.rstd_done[s.b], 1)

    def offset_of(self, dve, s):
        dve.wait_ge(self.rstd_done[s.b], s.i + 1)
        dve.scalar_tensor_tensor(self.offset[:, s.b, :], self.moments[:, s.b, :, 0], -1.0, self.rstd[:, s.b, :],
                                 ALU.mult, ALU.mult).then_inc(self.offset_done[s.b], 1)

    def apply(self, act, s, out, tiles, done):
        act.wait_ge(self.offset_done[s.b], s.i + 1)
        for j in range(QUAD):
            last = act.activation(out[:, s.b, j, :], tiles[:, j, :], ACT.Identity,
                                  bias=self.offset[:, s.b, j:j + 1], scale=self.rstd[:, s.b, j:j + 1])
        last.then_inc(done[s.b], 1)


def power_constants(ph, pool, tile, done):
    pool.memset(tile[:, 0:QUAD], -0.5).then_inc(done, 1)
    pool.memset(tile[:, QUAD:], EPS).then_inc(done, 1)
    pool.wait_ge(done, 2)


def turn_group(pe, psum, tile, s, ident, done):
    for j in range(QUAD):
        last = pe.transpose(psum[:, j * P:(j + 1) * P], tile[:, s.b, j, :], ident[:, :])
    last.then_inc(done[s.b], 1)


def flat(tile, b):
    return tile[:, b, :, :].rearrange("p j d -> p (j d)")


def sage_out(nc, g):
    with Phase(nc, "sageout") as ph:
        p_in, m_in = (ph.sb(n, [P, 2, QUAD, P]) for n in ("p_in", "m_in"))
        mT, x1T = (ph.sb(n, [P, 2, GROUP]) for n in ("mT", "x1T"))
        value, x1 = (ph.sb(n, [P, 2, QUAD, P]) for n in ("value", "x1"))
        th, ta = ph.sb("th", [P, 2, QUAD, AUG]), ph.sb("ta", [P, 2, QUAD, 2 * HEADS])
        minus_half = ph.sb("minus_half", [P, 2 * QUAD])
        ps_m, ps_1 = ph.ps("ps_m"), ph.ps("ps_1")
        ps_v, ps_th = [ph.ps(f"ps_v{b}") for b in range(2)], [ph.ps(f"ps_th{b}") for b in range(2)]
        ps_ta = ph.ps("ps_ta", [P, 2, QUAD, 2 * HEADS])
        norm = Norm(ph, "norm")
        p_here, m_here, x1_stored, th_stored, ta_stored = (ph.sems(n) for n in (
            "p_here", "m_here", "x1_stored", "th_stored", "ta_stored"))
        m_turned, x1_turned, mT_done, x1T_done = (ph.sems(n) for n in ("m_turned", "x1_turned", "mT_done", "x1T_done"))
        v_summed, th_summed, value_done, x1_done, th_done, ta_done = (ph.sems(n) for n in (
            "v_summed", "th_summed", "value_done", "x1_done", "th_done", "ta_done"))
        sp_turn, consts = ph.sem("sp_turn"), ph.sem("consts")
        block = ph.block()
        of = g.groups

        @block.sync
        def _(sp):
            def body(s):
                if l := s.at(2):
                    hold(sp, sp_turn, m_turned[l.b], l.i)
                    sp.dma_start(m_in[:, l.b, :, :], group_rows(g.seg, l.n)).then_inc(m_here[l.b], 16)
                if l := s.at(1):
                    hold(sp, sp_turn, value_done[l.b], l.i)
                    sp.dma_start(p_in[:, l.b, :, :], group_rows(g.pre2, l.n)).then_inc(p_here[l.b], 16)
                if r := s.at(-2):
                    hold(sp, sp_turn, x1_done[r.b], r.i + 1)
                    sp.dma_start(group_rows(g.x1, r.n), x1[:, r.b, :, :]).then_inc(x1_stored[r.b], 16)
                if r := s.at(-4):
                    hold(sp, sp_turn, th_done[r.b], r.i + 1)
                    sp.dma_start(group_rows(g.th, r.n, AUG), th[:, r.b, :, :]).then_inc(th_stored[r.b], 16)
                    hold(sp, sp_turn, ta_done[r.b], r.i + 1)
                    sp.dma_start(group_rows(g.ta, r.n, 2 * HEADS), ta[:, r.b, :, :]).then_inc(ta_stored[r.b], 16)
            run_steps(sp, of, 2, 4, body)
            for b in range(2):
                for stored in (x1_stored, th_stored, ta_stored):
                    sp.wait_ge(stored[b], 16 * (of // 2))

        @block.tensor
        def _(pe):
            def body(s):
                if r := s.at(-3):
                    pe.wait_ge(x1_done[r.b], r.i + 1)
                    q = r.at(-1)
                    if q:
                        pe.wait_ge(x1T_done[q.b], q.i + 1)
                    turn_group(pe, ps_1, x1, r, g.ident, x1_turned)
                if t := s.at(1):
                    q = t.at(-1)
                    pe.wait_ge(m_here[t.b], 16 * t.i + 16)
                    if q:
                        pe.wait_ge(mT_done[q.b], q.i + 1)
                    turn_group(pe, ps_m, m_in, t, g.ident, m_turned)
                if s.at(0):
                    pe.wait_ge(mT_done[s.b], s.i + 1)
                    pe.wait_ge(value_done[s.b], s.i)
                    for j in range(QUAD):
                        c = slice(j * P, (j + 1) * P)
                        last = pe.matmul(ps_v[s.b][:, c], mT[:, s.b, c], g.w["W2lT"][:, :], start=True, stop=True)
                    last.then_inc(v_summed[s.b], 1)
                if r := s.at(-3):
                    pe.wait_ge(x1T_done[r.b], r.i + 1)
                    pe.wait_ge(th_done[r.b], r.i)
                    q = r.at(-1)
                    if q:
                        pe.wait_ge(ta_done[q.b], q.i + 1)
                    for j in range(QUAD):
                        c = slice(j * P, (j + 1) * P)
                        pe.matmul(ps_ta[:, r.b, j, :], x1T[:, r.b, c], g.w["attT"][:, :], start=True, stop=True)
                        last = pe.matmul(ps_th[r.b][:, c], x1T[:, r.b, c], g.w["linT"][:, :], start=True, stop=True)
                    last.then_inc(th_summed[r.b], 1)
            run_steps(pe, of, 1, 3, body)

        @block.scalar
        def _(act):
            def body(s):
                if r := s.at(-3):
                    act.wait_ge(x1_turned[r.b], r.i + 1)
                    act.wait_ge(th_summed[r.b], r.i)
                    act.copy(x1T[:, r.b, :], ps_1[:, :]).then_inc(x1T_done[r.b], 1)
                if r := s.at(-4):
                    act.wait_ge(th_summed[r.b], r.i + 1)
                    act.wait_ge(th_stored[r.b], 16 * r.i)
                    act.wait_ge(ta_stored[r.b], 16 * r.i)
                    act.copy(th[:, r.b, :, 0:P], ps_th[r.b][:, :].rearrange("p (j d) -> p j d", j=QUAD))
                    act.copy(th[:, r.b, :, P:], ps_ta[:, r.b, :, :]).then_inc(th_done[r.b], 1)
                    act.copy(ta[:, r.b, :, :], ps_ta[:, r.b, :, :]).then_inc(ta_done[r.b], 1)
                if r := s.at(-2):
                    act.wait_ge(x1_stored[r.b], 16 * r.i)
                    act.wait_ge(x1_turned[r.b], r.i)
                    norm.apply(act, r, x1, value[:, r.b, :, :], x1_done)
            run_steps(act, of, 0, 4, body)

        @block.gpsimd
        def _(pool):
            power_constants(ph, pool, minus_half, consts)

            def body(s):
                if r := s.at(-1):
                    norm.deviation(pool, r, minus_half)
            run_steps(pool, of, 0, 1, body)

        @block.vector
        def _(dve):
            def body(s):
                if t := s.at(1):
                    dve.wait_ge(m_turned[t.b], t.i + 1)
                    dve.wait_ge(v_summed[t.b], t.i)
                    dve.tensor_copy(mT[:, t.b, :], ps_m[:, :]).then_inc(mT_done[t.b], 1)
                if s.at(0):
                    dve.wait_ge(v_summed[s.b], s.i + 1)
                    dve.wait_ge(p_here[s.b], 16 * s.i + 16)
                    dve.wait_ge(x1_done[s.b], s.i)
                    dve.tensor_tensor(flat(value, s.b), ps_v[s.b][:, :], flat(p_in, s.b), ALU.add).then_inc(value_done[s.b], 1)
                if s.at(0):
                    dve.wait_ge(value_done[s.b], s.i + 1)
                    norm.stats_of(dve, s, value[:, s.b, :, :])
                if r := s.at(-1):
                    norm.offset_of(dve, r)
                if s.at(0):
                    norm.moments_of(dve, s)
            run_steps(dve, of, 1, 1, body)


def edge_scores(nc, g):
    with Phase(nc, "score") as ph:
        src_ix, dst_ix = ph.sb("src_ix", [P, 2, QUAD], I32), ph.sb("dst_ix", [P, 2, QUAD], I32)
        at_src, at_dst = ph.sb("at_src", [P, 2, QUAD, AUG]), ph.sb("at_dst", [P, 2, QUAD, 2 * HEADS])
        sums = ph.sb("sums", [P, 2, 2, QUAD, HEADS])
        leaky = ph.sb("leaky", [P, 2, 2, QUAD, HEADS])
        ix_here, kept_stored = ph.sems("ix_here"), ph.sems("kept_stored")
        src_rows = [ph.sems(f"src_rows{b}_", QUAD) for b in range(2)]
        dst_rows = [ph.sems(f"dst_rows{b}_", QUAD) for b in range(2)]
        summed, leaky_done, score_done = ph.sems("summed"), ph.sems("leaky_done"), ph.sems("score_done")
        pool_turn, sp_turn = ph.sem("pool_turn"), ph.sem("sp_turn")
        block = ph.block()
        of = g.quads

        @block.sync
        def _(sp):
            def load(s):
                sp.dma_start(src_ix[:, s.b, :], g.srcw[:, ds(s.n * QUAD, QUAD)]).then_inc(ix_here[s.b], 16)
                sp.dma_start(dst_ix[:, s.b, :], g.dstw[:, ds(s.n * QUAD, QUAD)]).then_inc(ix_here[s.b], 16)

            def body(s):
                if s.at(0):
                    for u in range(QUAD):
                        hold(sp, sp_turn, src_rows[s.b][u], 16 * s.i + 16)
                    store_quad(sp, g.kept, s, at_src, kept_stored)
                if l := s.at(2):
                    for u in range(QUAD):
                        hold(sp, sp_turn, src_rows[l.b][u], 16 * l.i)
                        hold(sp, sp_turn, dst_rows[l.b][u], 16 * l.i)
                    load(l)
            run_steps(sp, of, 2, 0, body)
            for b in range(2):
                sp.wait_ge(kept_stored[b], 16 * (of // 2))

        @block.gpsimd
        def _(pool):
            def body(s):
                hold(pool, pool_turn, ix_here[s.b], 32 * s.i + 32)
                hold(pool, pool_turn, summed[s.b], 2 * s.i)
                hold(pool, pool_turn, kept_stored[s.b], 16 * s.i)
                for u in range(QUAD):
                    for ix, rows, here, table in ((src_ix, at_src, src_rows, g.th), (dst_ix, at_dst, dst_rows, g.ta)):
                        pool.indirect_dma_start(out=rows[:, s.b, u, :], out_offset=None, in_=table,
                                                in_offset=bass.IndirectOffsetOnAxis(ap=ix[:, s.b, u:u + 1], axis=0)
                                                ).then_inc(here[s.b][u], 16)
            run_steps(pool, of, 0, 0, body)

        @block.vector
        def _(dve):
            def body(s):
                for u in range(QUAD):
                    dve.wait_ge(src_rows[s.b][u], 16 * s.i + 16)
                    dve.wait_ge(dst_rows[s.b][u], 16 * s.i + 16)
                dve.tensor_tensor(sums[:, s.b, 0, :, :], at_src[:, s.b, :, P:P + HEADS], at_dst[:, s.b, :, HEADS:], ALU.add).then_inc(summed[s.b], 1)
                dve.tensor_tensor(sums[:, s.b, 1, :, :], at_dst[:, s.b, :, 0:HEADS], at_dst[:, s.b, :, HEADS:], ALU.add).then_inc(summed[s.b], 1)
                dve.wait_ge(summed[s.b], 2 * s.i + 2)
                both = sums[:, s.b, :, :, :].rearrange("p a t h -> p (a t h)")
                dve.scalar_tensor_tensor(leaky[:, s.b, :, :, :].rearrange("p a t h -> p (a t h)"), both, SLOPE, both,
                                         ALU.mult, ALU.max).then_inc(leaky_done[s.b], 1)
                dve.wait_ge(leaky_done[s.b], s.i + 1)
                dve.tensor_tensor(g.score[:, ds(s.n * QUAD * HEADS, QUAD * HEADS)],
                                  leaky[:, s.b, 0, :, :].rearrange("p t h -> p (t h)"),
                                  leaky[:, s.b, 1, :, :].rearrange("p t h -> p (t h)"), ALU.subtract).then_inc(score_done[s.b], 1)
            run_steps(dve, of, 0, 0, body)
            for b in range(2):
                dve.wait_ge(score_done[b], of // 2)
            dve.memset(g.score[0:1, :], LOW)


def edge_softmax(nc, g):
    runs = g.quads * QUAD // CHUNKS
    ch = CHUNKS * HEADS
    with Phase(nc, "soft") as ph:
        order = ph.sb("order", [ch, runs * P], I32)
        bar_up, bar_down = ph.sb("bar_up", [ch, runs * P]), ph.sb("bar_down", [ch, runs * P])
        line, up, down = (ph.sb(n, [ch, runs, P]) for n in ("line", "up", "down"))
        spare = ph.sb("spare", [ch, 2, runs])
        ends = ph.sb("ends", [ch, 4])
        row = ph.sb("row", [1, 4, CHUNKS, HEADS])
        carry = ph.sb("carry", [1, 2, CHUNKS, HEADS])
        init = ph.sb("init", [ch, 2])
        one = ph.sb("one", [1, 1])
        ps_in = [ph.ps(f"ps_in{k}") for k in range(2)]
        ps_out = [ph.ps(f"ps_out{k}") for k in range(2)]
        ps_row, ps_col = ph.ps("ps_row", [1, 512]), ph.ps("ps_col", [ch, 512])
        order_here, laid, line_read, line_done = ph.sem("order_here"), ph.sem("laid"), ph.sem("line_read"), ph.sem("line_done")
        step, scanned, back, back_read = ph.sem("step"), ph.sem("scanned"), ph.sem("back"), ph.sem("back_read")
        row_done, row_read, col_done, exp_done = ph.sem("row_done"), ph.sem("row_read"), ph.sem("col_done"), ph.sem("exp_done")
        zeros = ph.sb("zeros", [P, 4096])
        zeroed, cleared = ph.sem("zeroed"), ph.sem("cleared")
        block = ph.block()
        score = ph.sb("score", [P, runs, CHUNKS, HEADS])
        score_done = ph.sem("score_done")
        per = 512 // P
        trips = -(-runs // per)
        per_back = 512 // ch
        trips_back = 2 * -(-runs // per_back)

        @block.sync
        def _(sp):
            for c in range(CHUNKS):
                sp.dma_start(order[c * HEADS:(c + 1) * HEADS, :], g.order[c:c + 1, :].broadcast_to([HEADS, runs * P])).then_inc(order_here, 16)
            sp.wait_ge(zeroed, 1)
            transfers = clear_table(sp, g.gat, zeros, cleared)
            sp.wait_ge(cleared, 16 * transfers)

        @block.gpsimd
        def _(pool):
            pool.memset(zeros[:, :], 0.0).then_inc(zeroed, 1)

        @block.tensor
        def _(pe):
            pe.wait_ge(score_done, 1)
            for k in range(trips):
                if k >= 2:
                    pe.wait_ge(line_read, k - 1)
                for r in range(k * per, min(runs, (k + 1) * per)):
                    last = pe.transpose(ps_in[k % 2][0:ch, (r % per) * P:(r % per + 1) * P],
                                        score[:, r, :, :].rearrange("p c h -> p (c h)"), g.ident[:, :])
                last.then_inc(laid, 1)
            pe.wait_ge(scanned, 1)
            for k in range(4):
                last = pe.transpose(ps_row[0:1, k * ch:(k + 1) * ch], ends[:, k:k + 1], g.ident[0:ch, 0:ch])
            last.then_inc(row_done, 1)
            pe.wait_ge(row_read, 1)
            for k in range(2):
                last = pe.matmul(ps_col[:, k:k + 1], carry[0:1, k, :, :].rearrange("p c h -> p (c h)"), one[0:1, 0:1], start=True, stop=True)
            last.then_inc(col_done, 1)
            pe.wait_ge(exp_done, 2)
            k = 0
            for source in (up, down):
                for a in range(0, runs, per_back):
                    if k >= 2:
                        pe.wait_ge(back_read, k - 1)
                    for r in range(a, min(runs, a + per_back)):
                        last = pe.transpose(ps_out[k % 2][:, (r - a) * ch:(r - a + 1) * ch], source[:, r, :], g.ident[0:ch, 0:ch])
                    last.then_inc(back, 1)
                    k += 1

        @block.scalar
        def _(act):
            for k in range(trips):
                act.wait_ge(laid, k + 1)
                a, z = k * per, min(runs, (k + 1) * per)
                act.copy(line[:, a:z, :].rearrange("p r e -> p (r e)"), ps_in[k % 2][0:ch, 0:(z - a) * P]).then_inc(line_read, 1)
            act.wait_ge(exp_done, 1)
            act.activation(up[:, :, :], up[:, :, :], ACT.Exp).then_inc(exp_done, 1)

        @block.vector
        def _(dve):
            done = [0]

            def chain(ins):
                done[0] += 1
                ins.then_inc(step, 1)
                dve.wait_ge(step, done[0])

            def exchange(tile):
                dve.tensor_copy(spare[:, 0, :], tile[:, :, LAST_SLOT])
                chain(dve.tensor_copy(spare[:, 1, :], tile[:, :, P - 1]))
                dve.tensor_copy(tile[:, :, LAST_SLOT], spare[:, 1, :])
                chain(dve.tensor_copy(tile[:, :, P - 1], spare[:, 0, :]))

            dve.tensor_copy(score[:, :, :, :].rearrange("p r c h -> p c r h"),
                            g.score[:, 0:CHUNKS * runs * HEADS].rearrange("p (c r h) -> p c r h", c=CHUNKS, r=runs)).then_inc(score_done, 1)
            dve.memset(one[:, :], 1.0)
            dve.memset(carry[0:1, 0, 0, :], LOW)
            dve.memset(carry[0:1, 1, CHUNKS - 1, :], LOW)
            dve.memset(bar_up[:, 0:1], 0.0)
            dve.memset(bar_down[:, runs * P - 1:], 0.0)
            dve.wait_ge(order_here, 16 * CHUNKS)
            dve.tensor_tensor(bar_up[:, 1:], order[:, 1:], order[:, 0:runs * P - 1], ALU.not_equal)
            chain(dve.tensor_tensor(bar_down[:, 0:runs * P - 1], order[:, 1:], order[:, 0:runs * P - 1], ALU.not_equal))
            dve.tensor_scalar(bar_up[:, :], bar_up[:, :], LOW, None, ALU.mult)
            chain(dve.tensor_scalar(bar_down[:, :], bar_down[:, :], LOW, None, ALU.mult))
            dve.tensor_reduce(ends[:, 2:3], bar_up[:, :], mybir.AxisListType.X, ALU.min)
            chain(dve.tensor_reduce(ends[:, 3:4], bar_down[:, :], mybir.AxisListType.X, ALU.min))
            dve.wait_ge(line_read, trips)
            exchange(line)
            scores = line[:, :, :].rearrange("p r e -> p (r e)")
            ups, downs = up[:, :, :].rearrange("p r e -> p (r e)"), down[:, :, :].rearrange("p r e -> p (r e)")

            def scan(first_up, first_down):
                dve.tensor_tensor_scan(ups, bar_up[:, :], scores, first_up, ALU.add, ALU.max)
                chain(dve.tensor_tensor_scan(downs[:, ::-1], bar_down[:, ::-1], scores[:, ::-1], first_down, ALU.add, ALU.max))

            scan(LOW, LOW)
            dve.tensor_copy(ends[:, 0:1], ups[:, runs * P - 1:])
            chain(dve.tensor_copy(ends[:, 1:2], downs[:, 0:1]))
            dve.sem_inc(scanned, 1)
            dve.wait_ge(row_done, 1)
            chain(dve.tensor_copy(row[0:1, :, :, :].rearrange("p k c h -> p (k c h)"), ps_row[0:1, 0:4 * ch]))
            for c in range(1, CHUNKS):
                z = CHUNKS - 1 - c
                dve.scalar_tensor_tensor(carry[0:1, 0, c, :], carry[0:1, 0, c - 1, :], row[0:1, 2, c - 1, 0:1], row[0:1, 0, c - 1, :],
                                         ALU.add, ALU.max)
                chain(dve.scalar_tensor_tensor(carry[0:1, 1, z, :], carry[0:1, 1, z + 1, :], row[0:1, 3, z + 1, 0:1],
                                               row[0:1, 1, z + 1, :], ALU.add, ALU.max))
            dve.sem_inc(row_read, 1)
            dve.wait_ge(col_done, 1)
            chain(dve.tensor_copy(init[:, :], ps_col[:, 0:2]))
            scan(init[:, 0:1], init[:, 1:2])
            chain(dve.scalar_tensor_tensor(downs, downs, 0.0, ups, ALU.max, ALU.max))
            chain(dve.tensor_tensor(ups, scores, downs, ALU.subtract))
            exchange(down)
            exchange(up)
            dve.sem_inc(exp_done, 1)
            k = 0
            for dst in (g.weight, g.peak):
                into = dst[:, 0:CHUNKS * runs * HEADS].rearrange("p (c r h) -> p c r h", c=CHUNKS, r=runs)
                for a in range(0, runs, per_back):
                    z = min(runs, a + per_back)
                    dve.wait_ge(back, k + 1)
                    for r in range(a, z):
                        last = dve.tensor_copy(into[:, :, r, :], ps_out[k % 2][:, (r - a) * ch:(r - a + 1) * ch].rearrange("p (c h) -> p c h", c=CHUNKS))
                    last.then_inc(back_read, 1)
                    k += 1


def centre(dve, norm, s, between, tiles, gamma, between_done):
    for j in range(QUAD):
        dve.scalar_tensor_tensor(between[:, s.b, j, :], tiles[:, j, :], norm.moments[:, s.b, j, 0:1],
                                 gamma[:, 0:P], ALU.subtract, ALU.mult).then_inc(between_done[s.b], 1)


def scale_and_add(dve, norm, s, out, between, extra, between_done, out_done):
    dve.wait_ge(norm.rstd_done[s.b], s.i + 1)
    dve.wait_ge(between_done[s.b], QUAD * s.i + QUAD)
    for j in range(QUAD):
        last = dve.scalar_tensor_tensor(out[:, s.b, j, :], between[:, s.b, j, :], norm.rstd[:, s.b, j:j + 1],
                                        extra[:, s.b, j, :], ALU.mult, ALU.add)
    last.then_inc(out_done[s.b], 1)


def in_tiles(bank):
    return bank[:, :].rearrange("p (j d) -> p j d", j=QUAD)


def gat_out(nc, g):
    with Phase(nc, "gatout") as ph:
        x_in, th_in, s_in = ph.sb("x_in", [P, 2, QUAD, P]), ph.sb("th_in", [P, 2, QUAD, P]), ph.sb("s_in", [P, 2, QUAD, AUG])
        loop_w, total_w, share = (ph.sb(n, [P, 2, QUAD, HEADS]) for n in ("loop_w", "total_w", "share"))
        own, total, mean = (ph.sb(n, [P, 2, QUAD, P]) for n in ("own", "total", "mean"))
        meanT = ph.sb("meanT", [P, 2, GROUP])
        normed, scaled, value2, extra, x2 = (ph.sb(n, [P, 2, QUAD, P]) for n in ("normed", "scaled", "value2", "extra", "x2"))
        minus_half = ph.sb("minus_half", [P, 2 * QUAD])
        ps_m, ps_v = [ph.ps(f"ps_m{b}") for b in range(2)], [ph.ps(f"ps_v{b}") for b in range(2)]
        norm, norm2 = Norm(ph, "norm"), Norm(ph, "norm2")
        x_here, th_here, s_here, stored = (ph.sems(n) for n in ("x_here", "th_here", "s_here", "stored"))
        (loop_done, total_w_done, share_done, own_done, total_done, mean_done, turned, meanT_done, v_summed,
         normed_done, scaled_done, value2_done, extra_done, x2_done) = (ph.sems(n) for n in (
             "loop_done", "total_w_done", "share_done", "own_done", "total_done", "mean_done", "turned", "meanT_done",
             "v_summed", "normed_done", "scaled_done", "value2_done", "extra_done", "x2_done"))
        sp_turn, consts = ph.sem("sp_turn"), ph.sem("consts")
        block = ph.block()
        of = g.groups

        def by_head(tile, b):
            return tile[:, b, :, :].rearrange("p j (h k) -> p (j h) k", k=HEAD_DIM)

        def spread(tile, b):
            return tile[:, b, :, :].rearrange("p j h -> p (j h)").unsqueeze(2).broadcast_to([P, QUAD * HEADS, HEAD_DIM])

        @block.sync
        def _(sp):
            def body(s):
                if l := s.at(2):
                    hold(sp, sp_turn, own_done[l.b], l.i)
                    sp.dma_start(th_in[:, l.b, :, :], group_rows(g.th, l.n, P, 0)).then_inc(th_here[l.b], 16)
                    hold(sp, sp_turn, total_done[l.b], l.i)
                    sp.dma_start(s_in[:, l.b, :, :], group_rows(g.gat, l.n, AUG)).then_inc(s_here[l.b], 16)
                if l := s.at(1):
                    hold(sp, sp_turn, extra_done[l.b], l.i)
                    sp.dma_start(x_in[:, l.b, :, :], group_rows(g.x1, l.n)).then_inc(x_here[l.b], 16)
                if r := s.at(-3):
                    hold(sp, sp_turn, x2_done[r.b], r.i + 1)
                    sp.dma_start(group_rows(g.x2, r.n), x2[:, r.b, :, :]).then_inc(stored[r.b], 16)
            run_steps(sp, of, 2, 3, body)
            for b in range(2):
                sp.wait_ge(stored[b], 16 * (of // 2))

        @block.scalar
        def _(act):
            def body(s):
                if n := s.at(1):
                    act.wait_ge(s_here[n.b], 16 * n.i + 16)
                    act.wait_ge(own_done[n.b], n.i)
                    act.wait_ge(total_w_done[n.b], n.i)
                    act.activation(loop_w[:, n.b, :, :], s_in[:, n.b, :, P + HEADS:], ACT.Exp, scale=-1.0).then_inc(loop_done[n.b], 1)
                if s.at(0):
                    act.wait_ge(turned[s.b], s.i + 1)
                    act.wait_ge(v_summed[s.b], s.i)
                    act.activation(meanT[:, s.b, :], ps_m[s.b][:, :], ACT.Identity, bias=g.col[:, 0:1]).then_inc(meanT_done[s.b], 1)
                if r := s.at(-1):
                    act.wait_ge(scaled_done[r.b], r.i)
                    norm.apply(act, r, normed, in_tiles(ps_v[r.b]), normed_done)
                if r := s.at(-3):
                    act.wait_ge(stored[r.b], 16 * r.i)
                    norm2.apply(act, r, x2, value2[:, r.b, :, :], x2_done)
            run_steps(act, of, 1, 3, body)

        @block.gpsimd
        def _(pool):
            power_constants(ph, pool, minus_half, consts)

            def body(s):
                if r := s.at(-3):
                    norm2.deviation(pool, r, minus_half)
                if r := s.at(-1):
                    norm.deviation(pool, r, minus_half)
                if n := s.at(1):
                    pool.wait_ge(th_here[n.b], 16 * n.i + 16)
                    pool.wait_ge(loop_done[n.b], n.i + 1)
                    pool.wait_ge(total_done[n.b], n.i)
                    pool.tensor_tensor(by_head(own, n.b), by_head(th_in, n.b), spread(loop_w, n.b), ALU.mult).then_inc(own_done[n.b], 1)
                if r := s.at(-1):
                    pool.wait_ge(x_here[r.b], 16 * r.i + 16)
                    pool.wait_ge(value2_done[r.b], r.i)
                    pool.tensor_tensor(flat(extra, r.b), flat(x_in, r.b), g.row["ln1_beta"][:, :], ALU.add).then_inc(extra_done[r.b], 1)
            run_steps(pool, of, 1, 3, body)

        @block.tensor
        def _(pe):
            def body(s):
                pe.wait_ge(normed_done[s.b], s.i)
                pe.matmul(ps_v[s.b][:, :], g.ones[0:1, :], g.row["proj_b"][0:1, :], start=True, stop=False)
                pe.wait_ge(mean_done[s.b], s.i + 1)
                pe.wait_ge(meanT_done[s.b], s.i)
                turn_group(pe, ps_m[s.b], mean, s, g.ident, turned)
                pe.wait_ge(meanT_done[s.b], s.i + 1)
                for j in range(QUAD):
                    c = slice(j * P, (j + 1) * P)
                    last = pe.matmul(ps_v[s.b][:, c], meanT[:, s.b, c], g.w["projT"][:, :], start=False, stop=j == QUAD - 1)
                last.then_inc(v_summed[s.b], 1)
            run_steps(pe, of, 0, 0, body)

        @block.vector
        def _(dve):
            def body(s):
                here, r, q = s.at(0), s.at(-1), s.at(-2)
                if here:
                    dve.wait_ge(loop_done[s.b], s.i + 1)
                    dve.tensor_tensor(total_w[:, s.b, :, :], loop_w[:, s.b, :, :], s_in[:, s.b, :, P:P + HEADS], ALU.add).then_inc(total_w_done[s.b], 1)
                    dve.wait_ge(own_done[s.b], s.i + 1)
                    dve.tensor_tensor(total[:, s.b, :, :], own[:, s.b, :, :], s_in[:, s.b, :, 0:P], ALU.add).then_inc(total_done[s.b], 1)
                    dve.wait_ge(total_w_done[s.b], s.i + 1)
                    dve.reciprocal(share[:, s.b, :, :], total_w[:, s.b, :, :]).then_inc(share_done[s.b], 1)
                    dve.wait_ge(total_done[s.b], s.i + 1)
                    dve.wait_ge(share_done[s.b], s.i + 1)
                    dve.wait_ge(turned[s.b], s.i)
                    dve.tensor_tensor(by_head(mean, s.b), by_head(total, s.b), spread(share, s.b), ALU.mult).then_inc(mean_done[s.b], 1)
                if r:
                    dve.wait_ge(v_summed[r.b], r.i + 1)
                    norm.stats_of(dve, r, in_tiles(ps_v[r.b]))
                if d := s.at(-3):
                    norm2.offset_of(dve, d)
                if r:
                    norm.moments_of(dve, r)
                if q:
                    dve.wait_ge(normed_done[q.b], q.i + 1)
                    dve.tensor_tensor(flat(scaled, q.b), flat(normed, q.b), g.row["ln1_gamma"][:, :], ALU.mult).then_inc(scaled_done[q.b], 1)
                    dve.wait_ge(scaled_done[q.b], q.i + 1)
                    dve.wait_ge(extra_done[q.b], q.i + 1)
                    dve.wait_ge(x2_done[q.b], q.i)
                    dve.tensor_tensor(flat(value2, q.b), flat(scaled, q.b), flat(extra, q.b), ALU.add).then_inc(value2_done[q.b], 1)
                if r:
                    norm.offset_of(dve, r)
                if q:
                    dve.wait_ge(value2_done[q.b], q.i + 1)
                    norm2.stats_of(dve, q, value2[:, q.b, :, :])
                    norm2.moments_of(dve, q)
            run_steps(dve, of, 0, 3, body)


def edge_mlp(nc, g):
    with Phase(nc, "mlp") as ph:
        x_in, e_in = ph.sb("x_in", [P, 2, QUAD, P]), ph.sb("e_in", [P, 2, QUAD, P])
        xT, eT, hid1, hid2 = (ph.sb(n, [P, 2, GROUP]) for n in ("xT", "eT", "hid1", "hid2"))
        between, value2, extra, twice, x3 = (ph.sb(n, [P, 2, QUAD, P]) for n in ("between", "value2", "extra", "twice", "x3"))
        minus_half = ph.sb("minus_half", [P, 2 * QUAD])
        ps_x, ps_e, ps_1, ps_2 = ph.ps("ps_x"), ph.ps("ps_e"), ph.ps("ps_1"), ph.ps("ps_2")
        ps_v = [ph.ps(f"ps_v{b}") for b in range(2)]
        norm, norm2 = Norm(ph, "norm"), Norm(ph, "norm2")
        x_here, e_here, stored = (ph.sems(n) for n in ("x_here", "e_here", "stored"))
        (x_turned, e_turned, xT_done, eT_done, summed1, summed2, hid1_done, hid2_done, v_summed, twice_done,
         between_done, value2_done, extra_done, x3_done) = (ph.sems(n) for n in (
             "x_turned", "e_turned", "xT_done", "eT_done", "summed1", "summed2", "hid1_done", "hid2_done", "v_summed",
             "twice_done", "between_done", "value2_done", "extra_done", "x3_done"))
        sp_turn, consts = ph.sem("sp_turn"), ph.sem("consts")
        block = ph.block()
        of = g.groups

        @block.sync
        def _(sp):
            def body(s):
                if l := s.at(2):
                    hold(sp, sp_turn, e_turned[l.b], l.i)
                    sp.dma_start(e_in[:, l.b, :, :], group_rows(g.seg, l.n, P, P)).then_inc(e_here[l.b], 16)
                    hold(sp, sp_turn, x_turned[l.b], l.i)
                    hold(sp, sp_turn, twice_done[l.b], l.i)
                    sp.dma_start(x_in[:, l.b, :, :], group_rows(g.x2, l.n)).then_inc(x_here[l.b], 16)
                if r := s.at(-4):
                    hold(sp, sp_turn, x3_done[r.b], r.i + 1)
                    sp.dma_start(group_rows(g.x3, r.n), x3[:, r.b, :, :]).then_inc(stored[r.b], 16)
            run_steps(sp, of, 2, 4, body)
            for b in range(2):
                sp.wait_ge(stored[b], 16 * (of // 2))

        @block.tensor
        def _(pe):
            def body(s):
                if s.at(0):
                    pe.wait_ge(xT_done[s.b], s.i + 1)
                    pe.wait_ge(eT_done[s.b], s.i + 1)
                    if q := s.at(-1):
                        pe.wait_ge(hid1_done[q.b], q.i + 1)
                    pe.matmul(ps_1[:, :], g.w["W1"][:, 0, :], xT[:, s.b, :], start=True, stop=False)
                    pe.matmul(ps_1[:, :], g.w["W1"][:, 1, :], eT[:, s.b, :], start=False, stop=True).then_inc(summed1[s.b], 1)
                if t := s.at(1):
                    q = t.at(-1)
                    pe.wait_ge(x_here[t.b], 16 * t.i + 16)
                    if q:
                        pe.wait_ge(xT_done[q.b], q.i + 1)
                    turn_group(pe, ps_x, x_in, t, g.ident, x_turned)
                    pe.wait_ge(e_here[t.b], 16 * t.i + 16)
                    if q:
                        pe.wait_ge(eT_done[q.b], q.i + 1)
                    turn_group(pe, ps_e, e_in, t, g.ident, e_turned)
                if r := s.at(-1):
                    pe.wait_ge(between_done[r.b], QUAD * r.i)
                    pe.matmul(ps_v[r.b][:, :], g.ones[0:1, :], g.row["b3"][0:1, :], start=True, stop=False)
                    pe.wait_ge(hid2_done[r.b], r.i + 1)
                    for j in range(QUAD):
                        c = slice(j * P, (j + 1) * P)
                        last = pe.matmul(ps_v[r.b][:, c], hid2[:, r.b, c], g.w["W3"][:, :], start=False, stop=j == QUAD - 1)
                    last.then_inc(v_summed[r.b], 1)
                if s.at(0):
                    pe.wait_ge(hid1_done[s.b], s.i + 1)
                    if q := s.at(-1):
                        pe.wait_ge(hid2_done[q.b], q.i + 1)
                    pe.matmul(ps_2[:, :], g.w["W2"][:, :], hid1[:, s.b, :], start=True, stop=True).then_inc(summed2[s.b], 1)
            run_steps(pe, of, 1, 1, body)

        @block.scalar
        def _(act):
            def body(s):
                if s.at(0):
                    act.wait_ge(summed1[s.b], s.i + 1)
                    act.wait_ge(summed2[s.b], s.i)
                    act.activation(hid1[:, s.b, :], ps_1[:, :], ACT.Relu, bias=g.col[:, 1:2]).then_inc(hid1_done[s.b], 1)
                if t := s.at(1):
                    act.wait_ge(x_turned[t.b], t.i + 1)
                    act.wait_ge(summed1[t.b], t.i)
                    act.copy(xT[:, t.b, :], ps_x[:, :]).then_inc(xT_done[t.b], 1)
                    act.wait_ge(e_turned[t.b], t.i + 1)
                    act.copy(eT[:, t.b, :], ps_e[:, :]).then_inc(eT_done[t.b], 1)
                if s.at(0):
                    act.wait_ge(x_here[s.b], 16 * s.i + 16)
                    act.wait_ge(extra_done[s.b], s.i)
                    act.mul(flat(twice, s.b), flat(x_in, s.b), 2.0).then_inc(twice_done[s.b], 1)
                if r := s.at(-4):
                    act.wait_ge(stored[r.b], 16 * r.i)
                    norm2.apply(act, r, x3, value2[:, r.b, :, :], x3_done)
                if s.at(0):
                    act.wait_ge(summed2[s.b], s.i + 1)
                    act.wait_ge(v_summed[s.b], s.i)
                    act.activation(hid2[:, s.b, :], ps_2[:, :], ACT.Relu, bias=g.col[:, 2:3]).then_inc(hid2_done[s.b], 1)
            run_steps(act, of, 1, 4, body)

        @block.gpsimd
        def _(pool):
            power_constants(ph, pool, minus_half, consts)

            def body(s):
                if r := s.at(-2):
                    norm.deviation(pool, r, minus_half)
                if r := s.at(-3):
                    norm2.deviation(pool, r, minus_half)
                if r := s.at(-1):
                    pool.wait_ge(twice_done[r.b], r.i + 1)
                    pool.wait_ge(value2_done[r.b], r.i)
                    pool.tensor_tensor(flat(extra, r.b), flat(twice, r.b), g.row["ln2_beta"][:, :], ALU.add).then_inc(extra_done[r.b], 1)
            run_steps(pool, of, 0, 3, body)

        @block.vector
        def _(dve):
            def body(s):
                r, q = s.at(-2), s.at(-3)
                if r:
                    dve.wait_ge(v_summed[r.b], r.i + 1)
                    norm.stats_of(dve, r, in_tiles(ps_v[r.b]))
                if q:
                    dve.wait_ge(value2_done[q.b], q.i + 1)
                    norm2.stats_of(dve, q, value2[:, q.b, :, :])
                if r:
                    norm.moments_of(dve, r)
                if q:
                    norm2.moments_of(dve, q)
                if r:
                    dve.wait_ge(norm.moments_done[r.b], QUAD * r.i + QUAD)
                    centre(dve, norm, r, between, in_tiles(ps_v[r.b]), g.row["ln2_gamma"], between_done)
                    dve.wait_ge(extra_done[r.b], r.i + 1)
                    dve.wait_ge(x3_done[r.b], r.i)
                    scale_and_add(dve, norm, r, value2, between, extra, between_done, value2_done)
                if q:
                    norm2.offset_of(dve, q)
            run_steps(dve, of, 1, 3, body)


def messages(nc, g, t, hv):
    wide = 2 * P
    edge_dim = g.edge_t.shape[0]
    with Phase(nc, f"msg{t}") as ph:
        src_ix, dst_ix, tgt_ix = (ph.sb(n, [P, 2, QUAD], I32) for n in ("src_ix", "dst_ix", "tgt_ix"))
        drow = ph.sb("drow", [P, 2, QUAD, P], I32)
        edge = ph.sb("edge", [edge_dim, 2, GROUP])
        at_dst, at_src = ph.sb("at_dst", [P, 2, QUAD, P]), ph.sb("at_src", [P, 2, QUAD, P])
        dstT, srcT = ph.sb("dstT", [P, 2, GROUP]), ph.sb("srcT", [P, 2, GROUP])
        hidT = ph.sb("hidT", [P, 2, 2, GROUP])
        msg, same, res = ph.sb("msg", [P, 2, QUAD, wide]), ph.sb("same", [P, 2, QUAD, P]), ph.sb("res", [P, 2, QUAD, wide])
        ps_d, ps_s = ph.ps("ps_d"), ph.ps("ps_s")
        ps_h = [ph.ps(f"ps_h{m}") for m in range(2)]
        ps_msg = ph.ps("ps_msg", [P, QUAD, wide])
        banks = ph.ps("sums", [P, 2, 2, wide])
        sums = [banks[:, u % 2, u // 2, :] for u in range(QUAD)]
        src_here, dst_here, tgt_here, drow_here, edge_here = (ph.sems(n) for n in ("src_here", "dst_here", "tgt_here", "drow_here", "edge_here"))
        dst_rows = [ph.sems(f"dst_rows{b}_", QUAD) for b in range(2)]
        src_rows = [ph.sems(f"src_rows{b}_", QUAD) for b in range(2)]
        scattered = [ph.sems(f"scattered{b}_", QUAD) for b in range(2)]
        (dst_turned, src_turned, dstT_done, srcT_done, hid_summed, hid_done, msg_summed, msg_done, same_done, carried, summed,
         read_out) = (ph.sems(n) for n in (
             "dst_turned", "src_turned", "dstT_done", "srcT_done", "hid_summed", "hid_done", "msg_summed", "msg_done",
             "same_done", "carried", "summed", "read_out"))
        start, pool_turn, sp_turn = ph.sem("start"), ph.sem("pool_turn"), ph.sem("sp_turn")
        block = ph.block()
        of = g.quads

        @block.sync
        def _(sp):
            def body(s):
                if l := s.at(4):
                    for u in range(QUAD):
                        hold(sp, sp_turn, src_rows[l.b][u], 16 * l.i)
                        hold(sp, sp_turn, dst_rows[l.b][u], 16 * l.i)
                    sp.dma_start(dst_ix[:, l.b, :], g.dstw[:, ds(l.n * QUAD, QUAD)]).then_inc(dst_here[l.b], 16)
                    sp.dma_start(src_ix[:, l.b, :], g.srcw[:, ds(l.n * QUAD, QUAD)]).then_inc(src_here[l.b], 16)
                if l := s.at(2):
                    hold(sp, sp_turn, same_done[l.b], QUAD * l.i)
                    sp.dma_start(drow[:, l.b, :, :].rearrange("p t e -> p (t e)"),
                                 g.drow[:, ds(l.n * GROUP, GROUP)].broadcast_to([P, GROUP])).then_inc(drow_here[l.b], 16)
                    hold(sp, sp_turn, hid_summed[l.b], 2 * l.i)
                    sp.dma_start(edge[:, l.b, :], g.edge_t[:, ds(l.n * GROUP, GROUP)]).then_inc(edge_here[l.b], 16)
                if l := s.at(1):
                    for u in range(QUAD):
                        hold(sp, sp_turn, scattered[l.b][u], 16 * l.i)
                    sp.dma_start(tgt_ix[:, l.b, :], g.at_node[:, ds(l.n * QUAD, QUAD)]).then_inc(tgt_here[l.b], 16)
            run_steps(sp, of, 4, 0, body)

        @block.gpsimd
        def _(pool):
            def body(s):
                if n := s.at(2):
                    hold(pool, pool_turn, dst_here[n.b], 16 * n.i + 16)
                    hold(pool, pool_turn, src_here[n.b], 16 * n.i + 16)
                    hold(pool, pool_turn, dst_turned[n.b], n.i)
                    hold(pool, pool_turn, src_turned[n.b], n.i)
                    for ix, rows, landed in ((dst_ix, at_dst, dst_rows), (src_ix, at_src, src_rows)):
                        for u in range(QUAD):
                            pool.indirect_dma_start(out=rows[:, n.b, u, :], out_offset=None, in_=hv,
                                                    in_offset=bass.IndirectOffsetOnAxis(ap=ix[:, n.b, u:u + 1], axis=0)
                                                    ).then_inc(landed[n.b][u], 16)
                if r := s.at(-1):
                    hold(pool, pool_turn, tgt_here[r.b], 16 * r.i + 16)
                    for u in range(QUAD):
                        hold(pool, pool_turn, read_out[r.b], QUAD * r.i + u + 1)
                        pool.indirect_dma_start(out=g.seg, out_offset=bass.IndirectOffsetOnAxis(ap=tgt_ix[:, r.b, u:u + 1], axis=0),
                                                in_=res[:, r.b, u, :], in_offset=None,
                                                bounds_check=g.nodes - 1, oob_is_err=False).then_inc(scattered[r.b][u], 16)
            run_steps(pool, of, 2, 1, body)
            for b in range(2):
                for u in range(QUAD):
                    pool.wait_ge(scattered[b][u], 16 * (of // 2))

        @block.tensor
        def _(pe):
            def hid_product(n, k):
                m, part = divmod(k, 3)
                c = slice(m * P, (m + 1) * P)
                lhs, rhs = ((g.w["mw1"][:, t, 0, c], dstT[:, n.b, :]), (g.w["mw1"][:, t, 1, c], srcT[:, n.b, :]),
                            (g.w["mw1e"][:, t, c], edge[:, n.b, :]))[part]
                if part == 0:
                    if q := n.at(-1):
                        pe.wait_ge(hid_done[q.b], 2 * q.i + m + 1)
                ins = pe.matmul(ps_h[m][:, :], lhs, rhs, start=part == 0, stop=part == 2)
                if part == 2:
                    ins.then_inc(hid_summed[n.b], 1)

            def body(s):
                nxt, here = s.at(1), s.at(0)
                if nxt:
                    for u in range(QUAD):
                        pe.wait_ge(dst_rows[nxt.b][u], 16 * nxt.i + 16)
                    if here:
                        pe.wait_ge(dstT_done[s.b], s.i + 1)
                    turn_group(pe, ps_d, at_dst, nxt, g.ident, dst_turned)
                    for u in range(QUAD):
                        pe.wait_ge(src_rows[nxt.b][u], 16 * nxt.i + 16)
                    if here:
                        pe.wait_ge(srcT_done[s.b], s.i + 1)
                    turn_group(pe, ps_s, at_src, nxt, g.ident, src_turned)
                if here:
                    pe.wait_ge(hid_done[s.b], 2 * s.i + 2)
                    if q := s.at(-1):
                        pe.wait_ge(msg_done[q.b], 2 * q.i + 2)
                    for u in range(QUAD):
                        c = slice(u * P, (u + 1) * P)
                        pe.matmul(ps_msg[:, u, :], hidT[:, s.b, 0, c], g.w["mw2"][:, t, 0, :], start=True, stop=False)
                        last = pe.matmul(ps_msg[:, u, :], hidT[:, s.b, 1, c], g.w["mw2"][:, t, 1, :], start=False, stop=True)
                        if u % 2:
                            last.then_inc(msg_summed[s.b], 1)
                if nxt:
                    pe.wait_ge(dstT_done[nxt.b], nxt.i + 1)
                    pe.wait_ge(srcT_done[nxt.b], nxt.i + 1)
                    pe.wait_ge(edge_here[nxt.b], 16 * nxt.i + 16)
                    hid_product(nxt, 0)
                for u in range(QUAD):
                    if nxt:
                        hid_product(nxt, u + 1)
                    if here:
                        if u == 0:
                            pe.wait_ge(read_out[1 - s.b], QUAD * (s.i + s.b) - (1 if s.at(-1) else 0))
                        pe.wait_ge(same_done[s.b], QUAD * s.i + u + 1)
                        pe.wait_ge(carried[s.b], QUAD * s.i + u + 1)
                        pe.matmul(sums[u], same[:, s.b, u, :], msg[:, s.b, u, :], start=True, stop=True).then_inc(summed[s.b], 1)
                if nxt:
                    hid_product(nxt, 5)
            run_steps(pe, of, 1, 0, body)

        @block.scalar
        def _(act):
            act.wait_ge(start, 1)

            def relu(n, m):
                act.wait_ge(hid_summed[n.b], 2 * n.i + m + 1)
                act.wait_ge(msg_summed[n.b], 2 * n.i)
                c = g.mlp_cols[t] + m
                act.activation(hidT[:, n.b, m, :], ps_h[m][:, :], ACT.Relu, bias=g.col[:, c:c + 1]).then_inc(hid_done[n.b], 1)

            def read(s, u):
                act.wait_ge(summed[s.b], QUAD * s.i + u + 1)
                act.wait_ge(scattered[s.b][u], 16 * s.i)
                act.copy(res[:, s.b, u, :], sums[u]).then_inc(read_out[s.b], 1)

            def body(s):
                nxt, here, before = s.at(1), s.at(0), s.at(-1)
                if nxt:
                    act.wait_ge(src_turned[nxt.b], nxt.i + 1)
                    act.wait_ge(hid_summed[nxt.b], 2 * nxt.i)
                    act.copy(srcT[:, nxt.b, :], ps_s[:, :]).then_inc(srcT_done[nxt.b], 1)
                for u in range(QUAD):
                    if here:
                        if u % 2 == 0:
                            act.wait_ge(msg_done[s.b], 2 * s.i + u // 2 + 1)
                        if u:
                            act.wait_ge(summed[s.b], QUAD * s.i + u)
                        elif before:
                            act.wait_ge(summed[before.b], QUAD * before.i + QUAD)
                        act.copy(msg[0:1, s.b, u, :], sums[(u - 1) % QUAD][LAST_SLOT:LAST_SLOT + 1, :]).then_inc(carried[s.b], 1)
                    if u and here:
                        read(s, u - 1)
                    elif u == 0 and before:
                        read(before, QUAD - 1)
                    if nxt and u == 1:
                        relu(nxt, 0)
                if nxt:
                    relu(nxt, 1)
            run_steps(act, of, 1, 1, body)

        @block.vector
        def _(dve):
            dve.memset(sums[QUAD - 1], 0.0).then_inc(start, 1)

            def body(s):
                nxt, here = s.at(1), s.at(0)
                if nxt:
                    dve.wait_ge(dst_turned[nxt.b], nxt.i + 1)
                    dve.wait_ge(hid_summed[nxt.b], 2 * nxt.i)
                    dve.tensor_copy(dstT[:, nxt.b, :], ps_d[:, :]).then_inc(dstT_done[nxt.b], 1)
                if here:
                    dve.wait_ge(summed[s.b], QUAD * s.i)
                    for pair in range(2):
                        u = slice(2 * pair, 2 * pair + 2)
                        dve.wait_ge(msg_summed[s.b], 2 * s.i + pair + 1)
                        dve.tensor_tensor(msg[:, s.b, u, :], ps_msg[:, u, :],
                                          g.w["mb2"][:, t, :].unsqueeze(1).broadcast_to([P, 2, wide]), ALU.add).then_inc(msg_done[s.b], 1)
                if nxt:
                    dve.wait_ge(drow_here[nxt.b], 16 * nxt.i + 16)
                    dve.wait_ge(summed[nxt.b], QUAD * nxt.i)
                    for u in range(QUAD):
                        dve.tensor_scalar(same[:, nxt.b, u, :], drow[:, nxt.b, u, :], g.dcol[:, ds(nxt.n * QUAD + u, 1)], None,
                                          ALU.is_equal).then_inc(same_done[nxt.b], 1)
            run_steps(dve, of, 1, 0, body)


def gated_update(nc, g, t, hv, into, last_round):
    with Phase(nc, f"gru{t}") as ph:
        v_in, a_in = ph.sb("v_in", [P, 2, QUAD, P]), ph.sb("a_in", [P, 2, QUAD, 2 * P])
        vT, aT = ph.sb("vT", [P, 2, GROUP]), ph.sb("aT", [P, 2, 2, GROUP])
        reset, update, cand_h, cand_s, cand, diff, part, newT = (ph.sb(n, [P, 2, GROUP]) for n in (
            "reset", "update", "cand_h", "cand_s", "cand", "diff", "part", "newT"))
        x_in, value, new = (ph.sb(n, [P, 2, QUAD, P]) for n in ("x_in", "value", "new"))
        minus_half = ph.sb("minus_half", [P, 2 * QUAD])
        ps_v, ps_a, ps_out = ph.ps("ps_v"), [ph.ps(f"ps_a{k}") for k in range(2)], ph.ps("ps_out")
        ps_r, ps_z, ps_h, ps_x = (ph.ps(n) for n in ("ps_r", "ps_z", "ps_h", "ps_x"))
        norm = Norm(ph, "norm")
        v_here, a_here, x_here, stored = (ph.sems(n) for n in ("v_here", "a_here", "x_here", "stored"))
        (v_turned, a_turned, vT_done, aT_done, r_summed, z_summed, h_summed, x_summed, reset_done, update_done, cand_h_done,
         cand_s_done, cand_done, diff_done, part_done, newT_done, new_turned, new_done, value_done) = (ph.sems(n) for n in (
             "v_turned", "a_turned", "vT_done", "aT_done", "r_summed", "z_summed", "h_summed", "x_summed", "reset_done",
             "update_done", "cand_h_done", "cand_s_done", "cand_done", "diff_done", "part_done", "newT_done", "new_turned",
             "new_done", "value_done"))
        sp_turn, consts = ph.sem("sp_turn"), ph.sem("consts")
        block = ph.block()
        of = g.groups
        lag = 2

        @block.sync
        def _(sp):
            def body(s):
                if l := s.at(2):
                    hold(sp, sp_turn, v_turned[l.b], l.i)
                    sp.dma_start(v_in[:, l.b, :, :], group_rows(hv, l.n)).then_inc(v_here[l.b], 16)
                    hold(sp, sp_turn, a_turned[l.b], 2 * l.i)
                    sp.dma_start(a_in[:, l.b, :, :], group_rows(g.seg, l.n, 2 * P)).then_inc(a_here[l.b], 16)
                if last_round and s.at(0):
                    hold(sp, sp_turn, value_done[s.b], s.i)
                    sp.dma_start(x_in[:, s.b, :, :], group_rows(g.x3, s.n)).then_inc(x_here[s.b], 16)
                if r := s.at(-lag):
                    hold(sp, sp_turn, new_done[r.b], r.i + 1)
                    sp.dma_start(group_rows(into, r.n), new[:, r.b, :, :]).then_inc(stored[r.b], 16)
            run_steps(sp, of, 2, lag, body)
            for b in range(2):
                sp.wait_ge(stored[b], 16 * (of // 2))

        @block.tensor
        def _(pe):
            wih, whh = g.w["wih"], g.w["whh"]

            def body(s):
                if n := s.at(1):
                    q = n.at(-1)
                    pe.wait_ge(v_here[n.b], 16 * n.i + 16)
                    if q:
                        pe.wait_ge(vT_done[q.b], q.i + 1)
                    turn_group(pe, ps_v, v_in, n, g.ident, v_turned)
                    pe.wait_ge(a_here[n.b], 16 * n.i + 16)
                    if q:
                        pe.wait_ge(aT_done[q.b], 2 * q.i + 2)
                    for k in range(2):
                        for j in range(QUAD):
                            turned = pe.transpose(ps_a[k][:, j * P:(j + 1) * P], a_in[:, n.b, j, k * P:(k + 1) * P], g.ident[:, :])
                        turned.then_inc(a_turned[n.b], 1)
                if s.at(0):
                    pe.wait_ge(vT_done[s.b], s.i + 1)
                    pe.wait_ge(aT_done[s.b], 2 * s.i + 2)
                    q = s.at(-1)
                    for bank, gate, free, done in ((ps_r, 0, reset_done, r_summed), (ps_z, 1, update_done, z_summed)):
                        c = slice(gate * P, (gate + 1) * P)
                        if q:
                            pe.wait_ge(free[q.b], q.i + 1)
                        pe.matmul(bank[:, :], whh[:, t, c], vT[:, s.b, :], start=True, stop=False)
                        pe.matmul(bank[:, :], wih[:, t, 0, c], aT[:, s.b, 0, :], start=False, stop=False)
                        pe.matmul(bank[:, :], wih[:, t, 1, c], aT[:, s.b, 1, :], start=False, stop=True).then_inc(done[s.b], 1)
                        if gate == 0:
                            if q:
                                pe.wait_ge(cand_h_done[q.b], q.i + 1)
                            pe.matmul(ps_h[:, :], whh[:, t, 2 * P:], vT[:, s.b, :], start=True, stop=True).then_inc(h_summed[s.b], 1)
                    if q:
                        pe.wait_ge(cand_s_done[q.b], q.i + 1)
                    pe.matmul(ps_x[:, :], wih[:, t, 0, 2 * P:], aT[:, s.b, 0, :], start=True, stop=False)
                    pe.matmul(ps_x[:, :], wih[:, t, 1, 2 * P:], aT[:, s.b, 1, :], start=False, stop=True).then_inc(x_summed[s.b], 1)
                if r := s.at(-1):
                    pe.wait_ge(newT_done[r.b], r.i + 1)
                    if q := r.at(-1):
                        pe.wait_ge((value_done if last_round else new_done)[q.b], q.i + 1)
                    for j in range(QUAD):
                        turned = pe.transpose(ps_out[:, j * P:(j + 1) * P], newT[:, r.b, j * P:(j + 1) * P], g.ident[:, :])
                    turned.then_inc(new_turned[r.b], 1)
            run_steps(pe, of, 1, 1, body)

        @block.scalar
        def _(act):
            bias = g.gate_bias

            def body(s):
                if n := s.at(1):
                    act.wait_ge(v_turned[n.b], n.i + 1)
                    act.wait_ge(diff_done[n.b], n.i)
                    act.copy(vT[:, n.b, :], ps_v[:, :]).then_inc(vT_done[n.b], 1)
                if s.at(0):
                    act.wait_ge(r_summed[s.b], s.i + 1)
                    act.wait_ge(cand_h_done[s.b], s.i)
                    act.activation(reset[:, s.b, :], ps_r[:, :], ACT.Sigmoid, bias=bias[:, t, 0:1]).then_inc(reset_done[s.b], 1)
                    act.wait_ge(z_summed[s.b], s.i + 1)
                    act.wait_ge(part_done[s.b], s.i)
                    act.activation(update[:, s.b, :], ps_z[:, :], ACT.Sigmoid, bias=bias[:, t, 1:2]).then_inc(update_done[s.b], 1)
                    act.wait_ge(cand_s_done[s.b], s.i + 1)
                    act.wait_ge(newT_done[s.b], s.i)
                    act.activation(cand[:, s.b, :], cand_s[:, s.b, :], ACT.Tanh, bias=bias[:, t, 2:3]).then_inc(cand_done[s.b], 1)
                if last_round:
                    if r := s.at(-2):
                        act.wait_ge(stored[r.b], 16 * r.i)
                        norm.apply(act, r, new, value[:, r.b, :, :], new_done)
                else:
                    if r := s.at(-1):
                        act.wait_ge(new_turned[r.b], r.i + 1)
                        act.wait_ge(stored[r.b], 16 * r.i)
                        act.copy(flat(new, r.b), ps_out[:, :]).then_inc(new_done[r.b], 1)
            run_steps(act, of, 1, 2, body)

        @block.gpsimd
        def _(pool):
            power_constants(ph, pool, minus_half, consts)

            def body(s):
                if s.at(0):
                    pool.wait_ge(cand_done[s.b], s.i + 1)
                    pool.wait_ge(part_done[s.b], s.i)
                    pool.tensor_tensor(diff[:, s.b, :], vT[:, s.b, :], cand[:, s.b, :], ALU.subtract).then_inc(diff_done[s.b], 1)
                    pool.wait_ge(diff_done[s.b], s.i + 1)
                    pool.wait_ge(newT_done[s.b], s.i)
                    pool.tensor_tensor(part[:, s.b, :], diff[:, s.b, :], update[:, s.b, :], ALU.mult).then_inc(part_done[s.b], 1)
                if last_round:
                    if r := s.at(-1):
                        norm.deviation(pool, r, minus_half)
            run_steps(pool, of, 0, 1, body)

        @block.vector
        def _(dve):
            bias = g.gate_bias

            def body(s):
                if n := s.at(1):
                    for k in range(2):
                        dve.wait_ge(a_turned[n.b], 2 * n.i + k + 1)
                        dve.wait_ge(x_summed[n.b], n.i)
                        dve.tensor_copy(aT[:, n.b, k, :], ps_a[k][:, :]).then_inc(aT_done[n.b], 1)
                if s.at(0):
                    dve.wait_ge(h_summed[s.b], s.i + 1)
                    dve.wait_ge(reset_done[s.b], s.i + 1)
                    dve.scalar_tensor_tensor(cand_h[:, s.b, :], ps_h[:, :], bias[:, t, 3:4], reset[:, s.b, :],
                                             ALU.add, ALU.mult).then_inc(cand_h_done[s.b], 1)
                    dve.wait_ge(x_summed[s.b], s.i + 1)
                    dve.wait_ge(cand_h_done[s.b], s.i + 1)
                    dve.wait_ge(cand_done[s.b], s.i)
                    dve.tensor_tensor(cand_s[:, s.b, :], ps_x[:, :], cand_h[:, s.b, :], ALU.add).then_inc(cand_s_done[s.b], 1)
                if last_round:
                    if r := s.at(-1):
                        dve.wait_ge(new_turned[r.b], r.i + 1)
                        dve.wait_ge(x_here[r.b], 16 * r.i + 16)
                        dve.wait_ge(new_done[r.b], r.i)
                        dve.tensor_tensor(flat(value, r.b), ps_out[:, :], flat(x_in, r.b), ALU.add).then_inc(value_done[r.b], 1)
                    if r := s.at(-2):
                        norm.offset_of(dve, r)
                    if r := s.at(-1):
                        dve.wait_ge(value_done[r.b], r.i + 1)
                        norm.stats_of(dve, r, value[:, r.b, :, :])
                        norm.moments_of(dve, r)
                if s.at(0):
                    dve.wait_ge(part_done[s.b], s.i + 1)
                    dve.wait_ge(new_turned[s.b], s.i)
                    dve.tensor_tensor(newT[:, s.b, :], part[:, s.b, :], cand[:, s.b, :], ALU.add).then_inc(newT_done[s.b], 1)
            run_steps(dve, of, 1, 2, body)


class Graph:
    pass


def build(nc, d, out, nodes):
    g = Graph()
    g.nodes = nodes
    g.groups = d["x"].shape[0] // GROUP
    g.ntp = d["srcw"].shape[1]
    g.quads = g.ntp // QUAD - 2
    g.rounds = d["mlp_w1"].shape[0]
    np_ = d["x"].shape[0]
    g.x, g.drow, g.order, g.edge, g.edge_t, g.out = d["x"], d["drow"], d["order"], d["edge"], d["edge_t"], out
    with ExitStack() as stack:
        def sb(name, shape, dt=F32):
            return stack.enter_context(nc.sbuf_tensor(name, list(shape), dt))

        def table(name, width):
            return nc.dram_tensor(name, (np_, width), F32).ap()

        g.seg, g.gat = table("seg", 2 * P), table("gat", AUG)
        g.h1, g.x1, g.th, g.ta = table("h1", P), table("x1", P), table("th", AUG), table("ta", 2 * HEADS)
        g.kept = nc.dram_tensor("kept", (g.quads * GROUP, P), F32).ap()
        g.pre, g.pre2 = table("pre", P), table("pre2", P)
        g.x2, g.x3, g.x4 = table("x2", P), table("x3", P), table("x4", P)
        g.ident, g.ones = sb("ident", [P, P]), sb("ones", [1, P])
        g.srcw, g.dstw = sb("srcw_s", [P, g.ntp], I32), sb("dst_rows", [P, g.ntp], I32)
        g.at_node, g.at_left = sb("at_node", [P, g.ntp], I32), sb("at_left", [P, g.ntp], I32)
        g.dcol = sb("dcol", [P, g.ntp])
        g.w = {n: sb(f"w_{n}", [P, P]) for n in ("W1lT", "W1rT", "W2lT", "W2rT", "linT", "projT", "W2", "W3")}
        g.w["attT"] = sb("w_attT", [P, 2 * HEADS])
        g.w["W1"] = sb("w_W1", [P, 2, P])
        g.w["mw1"] = sb("w_mw1", [P, g.rounds, 2, 2 * P])
        g.w["mw1e"] = sb("w_mw1e", [d["mlp_w1"].shape[1] - 2 * P, g.rounds, 2 * P])
        g.w["mw2"] = sb("w_mw2", [P, g.rounds, 2, 2 * P])
        g.w["mb2"] = sb("w_mb2", [P, g.rounds, 2 * P])
        g.w["wih"] = sb("w_wih", [P, g.rounds, 2, 3 * P])
        g.w["whh"] = sb("w_whh", [P, g.rounds, 3 * P])
        g.rows = ("b1l", "b2l", "proj_b", "ln1_gamma", "ln1_beta", "b3", "ln2_gamma", "ln2_beta")
        g.row = {n: sb(f"row_{n}", [P, GROUP]) for n in g.rows}
        g.ncols = d["cols"].shape[1]
        g.col = sb("cols_s", [P, g.ncols])
        g.mlp_cols = [3 + 8 * r for r in range(g.rounds)]
        g.gate_cols = [5 + 8 * r for r in range(g.rounds)]
        g.gate_bias = sb("gate_bias", [P, g.rounds, 4])
        halves = g.seg.rearrange("n (c d) -> (n c) d", d=P)
        prepare(nc, g, d)
        edge_sums(nc, g, "sage1", g.at_node, g.seg, gather=g.x, linear=g.edge, mean=True,
                  side=(g.x, g.w["W1rT"], g.row["b1l"], None, g.pre))
        sage_hidden(nc, g)
        edge_sums(nc, g, "sage2", g.at_left, halves, gather=g.h1, mean=True,
                  side=(g.h1, g.w["W2rT"], g.row["b2l"], g.x, g.pre2))
        sage_out(nc, g)
        with ExitStack() as inner:
            slots = g.ntp * HEADS
            g.score, g.weight, g.peak = (inner.enter_context(nc.sbuf_tensor(n, [P, slots], F32)) for n in ("score", "weight", "peak"))
            edge_scores(nc, g)
            edge_softmax(nc, g)
            edge_sums(nc, g, "gat", g.at_node, g.gat, kept=g.kept, weights=(g.weight, g.peak))
        gat_out(nc, g)
        edge_mlp(nc, g)
        messages(nc, g, 0, g.x3)
        gated_update(nc, g, 0, g.x3, g.x4, False)
        messages(nc, g, 1, g.x4)
        gated_update(nc, g, 1, g.x4, out, True)


def arrange(inputs):
    import numpy as np
    a = {k: np.asarray(v) for k, v in inputs.items()}
    nodes, edges = a["x"].shape[0], a["src"].shape[0]
    tiles = -(-edges // EDGES_PER_TILE)
    quads = 2 * -(-tiles // (2 * QUAD))
    ntp = QUAD * (quads + 2)
    place = np.arange(P)
    place[[LAST_SLOT, P - 1]] = place[[P - 1, LAST_SLOT]]
    inorder = np.arange(ntp)[:, None] * EDGES_PER_TILE + np.arange(P)[None, :]
    slots = inorder[:, place]

    def padded(v, fill):
        p = np.full((inorder.max() + 2,) + v.shape[1:], fill, v.dtype)
        p[1:1 + edges] = v
        return p
    src, dst = padded(a["src"], 0), padded(a["dst"], -1)
    d = {}
    rows = -(-nodes // (2 * GROUP)) * 2 * GROUP
    d["x"] = np.zeros((rows, P), np.float32)
    d["x"][:nodes] = a["x"]
    d["srcw"], d["dstw"] = src[slots].T, dst[slots].T
    nxt = dst[slots + 1].T.copy()
    nxt[0] = d["dstw"][0]
    d["nxtw"] = nxt
    d["drow"] = dst[slots].reshape(1, -1)
    d["order"] = dst[inorder[:quads * QUAD]].reshape(CHUNKS, -1)
    d["edge"] = padded(a["edge_attr_128"], 0)[slots].reshape(-1, P)
    d["edge_t"] = padded(a["edge_attr_26"], 0)[slots].reshape(ntp * P, -1).T
    for k, n in (("W1lT", "L0_gnn_W1l"), ("W1rT", "L0_gnn_W1r"), ("W2lT", "L0_gnn_W2l"), ("W2rT", "L0_gnn_W2r"),
                 ("linT", "L1_gnn_lin_w"), ("projT", "L1_gnn_proj_w")):
        d[k] = a[n].T
    d["lin_w"] = a["L1_gnn_lin_w"]
    d["W1"], d["W2"], d["W3"] = a["L2_gnn_W1"], a["L2_gnn_W2"], a["L2_gnn_W3"]
    d["att_src"], d["att_dst"] = a["L1_gnn_att_src"].reshape(P, 1), a["L1_gnn_att_dst"].reshape(P, 1)
    d["head_of"] = np.repeat(np.eye(HEADS, dtype=np.float32), HEAD_DIM, axis=0)
    d["ident"] = np.eye(P, dtype=np.float32)
    for k, n in (("b1l", "L0_gnn_b1l"), ("b2l", "L0_gnn_b2l"), ("proj_b", "L1_gnn_proj_b"),
                 ("ln1_gamma", "L1_gnn_ln_gamma"), ("ln1_beta", "L1_gnn_ln_beta"), ("b3", "L2_gnn_b3"),
                 ("ln2_gamma", "L2_gnn_gamma"), ("ln2_beta", "L2_gnn_beta")):
        d[k] = a[n].reshape(1, P)
    cols = [a["L1_gnn_gat_bias"], a["L2_gnn_b1"], a["L2_gnn_b2"]]
    for r in range(a["L3_gnn_mlp_w1"].shape[0]):
        cols += [*a["L3_gnn_mlp_b1"][r].reshape(2, P), *a["L3_gnn_gru_bih"][r].reshape(3, P),
                 *a["L3_gnn_gru_bhh"][r].reshape(3, P)]
    d["cols"] = np.stack(cols, axis=1)
    d["mlp_w1"], d["mlp_w2"], d["mlp_b2"] = a["L3_gnn_mlp_w1"], a["L3_gnn_mlp_w2"], a["L3_gnn_mlp_b2"]
    d["wihT"], d["whhT"] = a["L3_gnn_gru_wih"].transpose(0, 2, 1), a["L3_gnn_gru_whh"].transpose(0, 2, 1)
    return {k: np.ascontiguousarray(v) for k, v in d.items()}, nodes


def kernel(**inputs):
    import concourse.bacc as bacc
    from concourse.bass_utils import run_bass_kernel_spmd

    arrays, nodes = arrange(inputs)
    nc = bacc.Bacc("TRN2", target_bir_lowering=False, num_devices=1)
    d = {k: nc.dram_tensor(f"in_{k}", v.shape, mybir.dt.from_np(v.dtype), kind="ExternalInput").ap()
         for k, v in arrays.items()}
    out = nc.dram_tensor("out", arrays["x"].shape, F32, kind="ExternalOutput").ap()
    build(nc, d, out, nodes)
    r = run_bass_kernel_spmd(nc, [{f"in_{k}": v for k, v in arrays.items()}], core_ids=[0])
    return r.results[0]["out"][:nodes]
```
